# Optimizing a Trainium2 kernel written in Bass

```python
import numpy as np
import jax
import jax.numpy as jnp

def _softmax(x, axis=-1):
    return jax.nn.softmax(x, axis=axis)

def _gelu(x):
    return jax.nn.gelu(x, approximate=True)

def _silu(x):
    return jax.nn.silu(x)

def _sigmoid(x):
    return jax.nn.sigmoid(x)

def _layernorm(x, axis=-1, eps=1e-05):
    m = jnp.mean(x, axis=axis, keepdims=True)
    v = jnp.var(x, axis=axis, keepdims=True)
    return (x - m) / jnp.sqrt(v + eps)

def _scatter_add(tgt, idx, src, axis=0):
    return tgt.at[idx].add(src)

def _segment_sum(src, seg, n):
    return jax.ops.segment_sum(src, seg, n)
kernel_name = 'mk_sandwich_d2_jaxref_r8_a91350'

def setup_inputs(seed: int=0):
    np.random.seed(seed)
    _w = jnp.asarray

    def _L0_attn_setup():
        import math
        import jax, jax.numpy as jnp
        import numpy as np
        B, L, D_MODEL, N_HEADS = (4, 512, 128, 16)
        HEAD_DIM = D_MODEL // N_HEADS
        NUM_LANDMARKS = 128

        def _split_heads(t):
            b, l, _ = t.shape
            return t.reshape(b, l, N_HEADS, HEAD_DIM).transpose(0, 2, 1, 3)

        def _iterative_inv(mat, n_iter=6):
            I = jnp.eye(mat.shape[-1], dtype=mat.dtype)
            K = mat
            V = K.swapaxes(-1, -2) / jnp.max(jnp.sum(K, axis=-2))
            for _ in range(n_iter):
                KV = jnp.matmul(K, V)
                V = jnp.matmul(0.25 * V, 13.0 * I - jnp.matmul(KV, 15.0 * I - jnp.matmul(KV, 7.0 * I - KV)))
            return V
        key = jax.random.key(seed)
        ks = jax.random.split(key, 7)
        s = 1.0 / math.sqrt(D_MODEL)
        return {'x': jax.random.normal(ks[0], (B, L, D_MODEL), dtype=jnp.float32), 'Wq': jax.random.uniform(ks[1], (D_MODEL, D_MODEL), jnp.float32, -s, s), 'bq': jax.random.uniform(ks[2], (D_MODEL,), jnp.float32, -s, s), 'Wk': jax.random.uniform(ks[3], (D_MODEL, D_MODEL), jnp.float32, -s, s), 'bk': jax.random.uniform(ks[4], (D_MODEL,), jnp.float32, -s, s), 'Wv': jax.random.uniform(ks[5], (D_MODEL, D_MODEL), jnp.float32, -s, s), 'bv': jax.random.uniform(ks[6], (D_MODEL,), jnp.float32, -s, s)}
    _L0_attn_in = _L0_attn_setup()

    def _L0_ffn_setup():
        import jax, jax.numpy as jnp
        import numpy as np
        DIM = 128
        DEPTH = 2
        HEADS = 8
        DIM_HEAD = 64
        WINDOW = 64
        INNER = HEADS * DIM_HEAD
        HID = int(DIM * 4 * 2 / 3)
        B, N = (2, 1024)
        QK_SCALE = 8.0

        def shift_token(t):
            t1, t2 = jnp.split(t, 2, axis=-1)
            t2 = jnp.pad(t2, ((0, 0), (1, 0), (0, 0)))[:, :-1]
            return jnp.concatenate([t1, t2], axis=-1)

        def l2norm(t):
            return t / jnp.clip(jnp.linalg.norm(t, axis=-1, keepdims=True), 1e-12)

        def rotate_half(x):
            x1, x2 = jnp.split(x, 2, axis=-1)
            return jnp.concatenate([-x2, x1], axis=-1)

        def rotary_xpos(q, k):
            n = q.shape[-2]
            half_idx = jnp.arange(0, DIM_HEAD, 2, dtype=jnp.float32)
            inv_freq = 1.0 / 10000.0 ** (half_idx / DIM_HEAD)
            t = jnp.arange(n, dtype=jnp.float32)
            freqs = t[:, None] * inv_freq[None, :]
            freqs = jnp.concatenate([freqs, freqs], axis=-1)
            base = (half_idx + 0.4 * DIM_HEAD) / (1.4 * DIM_HEAD)
            power = (t - n // 2) / float(WINDOW // 2)
            scale = base[None, :] ** power[:, None]
            scale = jnp.concatenate([scale, scale], axis=-1)
            cos, sin = (jnp.cos(freqs), jnp.sin(freqs))
            q = q * cos * scale + rotate_half(q) * sin * scale
            k = k * cos / scale + rotate_half(k) * sin / scale
            return (q, k)

        def local_attention(q, k, v):
            b, h, n, d = q.shape
            w = n // WINDOW
            bq = q.reshape(b, h, w, WINDOW, d) * QK_SCALE
            bk = k.reshape(b, h, w, WINDOW, d)
            bv = v.reshape(b, h, w, WINDOW, d)

            def look_around(t):
                p = jnp.pad(t, ((0, 0), (0, 0), (1, 0), (0, 0), (0, 0)))
                return jnp.concatenate([p[:, :, :w], p[:, :, 1:]], axis=3)
            bk, bv = (look_around(bk), look_around(bv))
            bt = jnp.arange(n).reshape(w, WINDOW)
            btp = jnp.pad(bt, ((1, 0), (0, 0)), constant_values=-1)
            btk = jnp.concatenate([btp[:w], btp[1:]], axis=1)
            sim = jnp.einsum('bhwid,bhwjd->bhwij', bq, bk)
            i = bt[:, :, None]
            j = btk[:, None, :]
            mask = (i < j) | (i > j + WINDOW) | (j == -1)
            sim = jnp.where(mask, -jnp.finfo(sim.dtype).max, sim)
            attn = jax.nn.softmax(sim, axis=-1)
            out = jnp.einsum('bhwij,bhwjd->bhwid', attn, bv)
            return out.reshape(b, h, n, d)

        def _layer(x, wqkv, qs, ksc, wo, lg, lb, w1, b1, w2, b2):
            b, n, _ = x.shape
            h = shift_token(x)
            qkv = h @ wqkv
            q, k, v = jnp.split(qkv, 3, axis=-1)
            to_heads = lambda t: t.reshape(b, n, HEADS, DIM_HEAD).transpose(0, 2, 1, 3)
            q, k, v = (to_heads(q), to_heads(k), to_heads(v))
            q = l2norm(q) * qs
            k = l2norm(k) * ksc
            q, k = rotary_xpos(q, k)
            o = local_attention(q, k, v)
            o = o.transpose(0, 2, 1, 3).reshape(b, n, INNER)
            x = x + o @ wo
            h = shift_token(x)
            mu = h.mean(-1, keepdims=True)
            var = h.var(-1, keepdims=True)
            h = (h - mu) / jnp.sqrt(var + 1e-05) * lg + lb
            h = h @ w1 + b1
            a, g = jnp.split(h, 2, axis=-1)
            h = a * jax.nn.gelu(g, approximate=False)
            x = x + h @ w2 + b2
            return x
        key = jax.random.key(seed)
        ks = jax.random.split(key, 6)
        return {'x': jax.random.normal(ks[0], (B, N, DIM), jnp.float32), 'wqkv': jax.random.normal(ks[1], (DEPTH, DIM, 3 * INNER), jnp.float32) * 0.02, 'q_scale': jnp.ones((DEPTH, DIM_HEAD), jnp.float32), 'k_scale': jnp.ones((DEPTH, DIM_HEAD), jnp.float32), 'wo': jax.random.normal(ks[2], (DEPTH, INNER, DIM), jnp.float32) * 0.02, 'ln_g': jnp.ones((DEPTH, DIM), jnp.float32), 'ln_b': jnp.zeros((DEPTH, DIM), jnp.float32), 'w1': jax.random.normal(ks[3], (DEPTH, DIM, 2 * HID), jnp.float32) * 0.02, 'b1': jnp.zeros((DEPTH, 2 * HID), jnp.float32), 'w2': jax.random.normal(ks[4], (DEPTH, HID, DIM), jnp.float32) * 0.02, 'b2': jnp.zeros((DEPTH, DIM), jnp.float32)}
    _L0_ffn_in = _L0_ffn_setup()

    def _L1_attn_setup():
        import jax, jax.numpy as jnp
        import numpy as np
        import math
        D_MODEL = 128
        NUM_HEADS = 16
        key = jax.random.key(seed)
        k1, k2, k3 = jax.random.split(key, 3)
        B, S = (2, 256)
        x = jax.random.normal(k1, (B, S, D_MODEL), dtype=jnp.float32)
        W_kqv = jax.random.normal(k2, (D_MODEL, 3 * D_MODEL), dtype=jnp.float32) * (1.0 / math.sqrt(D_MODEL))
        m = jax.random.normal(k3, (NUM_HEADS, 1, 1), dtype=jnp.float32)
        return {'x': x, 'W_kqv': W_kqv, 'm': m}
    _L1_attn_in = _L1_attn_setup()

    def _L1_ffn_setup():
        import jax, jax.numpy as jnp
        import numpy as np
        E = 8
        K = 2
        R = 64
        ALPHA = 128.0
        SCALING = ALPHA / R
        key = jax.random.key(seed)
        k0, k1, k2, k3 = jax.random.split(key, 4)
        B, S, D = (4, 512, 128)
        x = jax.random.normal(k0, (B, S, D), jnp.float32)
        Wg = jax.random.normal(k1, (E, D), jnp.float32) * 0.02
        bg = jnp.zeros((E,), jnp.float32)
        W1 = jax.random.normal(k2, (E, R, D), jnp.float32) * (1.0 / np.sqrt(D))
        W2 = jax.random.normal(k3, (E, D, R), jnp.float32) * 0.02
        return {'x': x, 'Wg': Wg, 'bg': bg, 'W1': W1, 'W2': W2}
    _L1_ffn_in = _L1_ffn_setup()
    _d = {'L0_attn_x': _L0_attn_in['x'], 'L0_attn_Wq': _L0_attn_in['Wq'], 'L0_attn_bq': _L0_attn_in['bq'], 'L0_attn_Wk': _L0_attn_in['Wk'], 'L0_attn_bk': _L0_attn_in['bk'], 'L0_attn_Wv': _L0_attn_in['Wv'], 'L0_attn_bv': _L0_attn_in['bv'], 'L0_ffn_wqkv': _L0_ffn_in['wqkv'], 'L0_ffn_q_scale': _L0_ffn_in['q_scale'], 'L0_ffn_k_scale': _L0_ffn_in['k_scale'], 'L0_ffn_wo': _L0_ffn_in['wo'], 'L0_ffn_ln_g': _L0_ffn_in['ln_g'], 'L0_ffn_ln_b': _L0_ffn_in['ln_b'], 'L0_ffn_w1': _L0_ffn_in['w1'], 'L0_ffn_b1': _L0_ffn_in['b1'], 'L0_ffn_w2': _L0_ffn_in['w2'], 'L0_ffn_b2': _L0_ffn_in['b2'], 'L1_attn_W_kqv': _L1_attn_in['W_kqv'], 'L1_attn_m': _L1_attn_in['m'], 'L1_ffn_Wg': _L1_ffn_in['Wg'], 'L1_ffn_bg': _L1_ffn_in['bg'], 'L1_ffn_W1': _L1_ffn_in['W1'], 'L1_ffn_W2': _L1_ffn_in['W2']}
    _x0 = _d['L0_attn_x']
    _d['L0_attn_x'] = jax.random.normal(jax.random.fold_in(jax.random.key(seed), 1), (16, 256, 128), dtype=_x0.dtype)
    del _x0
    return _d

def reference(L0_attn_x, L0_attn_Wq, L0_attn_bq, L0_attn_Wk, L0_attn_bk, L0_attn_Wv, L0_attn_bv, L0_ffn_wqkv, L0_ffn_q_scale, L0_ffn_k_scale, L0_ffn_wo, L0_ffn_ln_g, L0_ffn_ln_b, L0_ffn_w1, L0_ffn_b1, L0_ffn_w2, L0_ffn_b2, L1_attn_W_kqv, L1_attn_m, L1_ffn_Wg, L1_ffn_bg, L1_ffn_W1, L1_ffn_W2):

    def _L0_attn_ref(x, Wq, bq, Wk, bk, Wv, bv):
        import math
        import jax, jax.numpy as jnp
        import numpy as np
        B, L, D_MODEL, N_HEADS = (4, 512, 128, 16)
        HEAD_DIM = D_MODEL // N_HEADS
        NUM_LANDMARKS = 128

        def _split_heads(t):
            b, l, _ = t.shape
            return t.reshape(b, l, N_HEADS, HEAD_DIM).transpose(0, 2, 1, 3)

        def _iterative_inv(mat, n_iter=6):
            I = jnp.eye(mat.shape[-1], dtype=mat.dtype)
            K = mat
            V = K.swapaxes(-1, -2) / jnp.max(jnp.sum(K, axis=-2))
            for _ in range(n_iter):
                KV = jnp.matmul(K, V)
                V = jnp.matmul(0.25 * V, 13.0 * I - jnp.matmul(KV, 15.0 * I - jnp.matmul(KV, 7.0 * I - KV)))
            return V
        Q = _split_heads(x @ Wq.T + bq)
        K = _split_heads(x @ Wk.T + bk)
        V = _split_heads(x @ Wv.T + bv)
        b, h, l, d = Q.shape
        scale = 1.0 / math.sqrt(math.sqrt(HEAD_DIM))
        Q = Q * scale
        K = K * scale
        seg = l // NUM_LANDMARKS
        Q_lm = Q.reshape(b, h, NUM_LANDMARKS, seg, d).mean(axis=-2)
        K_lm = K.reshape(b, h, NUM_LANDMARKS, seg, d).mean(axis=-2)
        kernel_1 = jax.nn.softmax(jnp.einsum('bhld,bhmd->bhlm', Q, K_lm), axis=-1)
        kernel_2 = jax.nn.softmax(jnp.einsum('bhmd,bhnd->bhmn', Q_lm, K_lm), axis=-1)
        kernel_3 = jax.nn.softmax(jnp.einsum('bhmd,bhld->bhml', Q_lm, K), axis=-1)
        X = jnp.matmul(jnp.matmul(kernel_1, _iterative_inv(kernel_2)), jnp.matmul(kernel_3, V))
        out = X.transpose(0, 2, 1, 3).reshape(b, l, h * d)
        return out

    def _L0_ffn_ref(x, wqkv, q_scale, k_scale, wo, ln_g, ln_b, w1, b1, w2, b2):
        import jax, jax.numpy as jnp
        import numpy as np
        DIM = 128
        DEPTH = 2
        HEADS = 8
        DIM_HEAD = 64
        WINDOW = 64
        INNER = HEADS * DIM_HEAD
        HID = int(DIM * 4 * 2 / 3)
        B, N = (2, 1024)
        QK_SCALE = 8.0

        def shift_token(t):
            t1, t2 = jnp.split(t, 2, axis=-1)
            t2 = jnp.pad(t2, ((0, 0), (1, 0), (0, 0)))[:, :-1]
            return jnp.concatenate([t1, t2], axis=-1)

        def l2norm(t):
            return t / jnp.clip(jnp.linalg.norm(t, axis=-1, keepdims=True), 1e-12)

        def rotate_half(x):
            x1, x2 = jnp.split(x, 2, axis=-1)
            return jnp.concatenate([-x2, x1], axis=-1)

        def rotary_xpos(q, k):
            n = q.shape[-2]
            half_idx = jnp.arange(0, DIM_HEAD, 2, dtype=jnp.float32)
            inv_freq = 1.0 / 10000.0 ** (half_idx / DIM_HEAD)
            t = jnp.arange(n, dtype=jnp.float32)
            freqs = t[:, None] * inv_freq[None, :]
            freqs = jnp.concatenate([freqs, freqs], axis=-1)
            base = (half_idx + 0.4 * DIM_HEAD) / (1.4 * DIM_HEAD)
            power = (t - n // 2) / float(WINDOW // 2)
            scale = base[None, :] ** power[:, None]
            scale = jnp.concatenate([scale, scale], axis=-1)
            cos, sin = (jnp.cos(freqs), jnp.sin(freqs))
            q = q * cos * scale + rotate_half(q) * sin * scale
            k = k * cos / scale + rotate_half(k) * sin / scale
            return (q, k)

        def local_attention(q, k, v):
            b, h, n, d = q.shape
            w = n // WINDOW
            bq = q.reshape(b, h, w, WINDOW, d) * QK_SCALE
            bk = k.reshape(b, h, w, WINDOW, d)
            bv = v.reshape(b, h, w, WINDOW, d)

            def look_around(t):
                p = jnp.pad(t, ((0, 0), (0, 0), (1, 0), (0, 0), (0, 0)))
                return jnp.concatenate([p[:, :, :w], p[:, :, 1:]], axis=3)
            bk, bv = (look_around(bk), look_around(bv))
            bt = jnp.arange(n).reshape(w, WINDOW)
            btp = jnp.pad(bt, ((1, 0), (0, 0)), constant_values=-1)
            btk = jnp.concatenate([btp[:w], btp[1:]], axis=1)
            sim = jnp.einsum('bhwid,bhwjd->bhwij', bq, bk)
            i = bt[:, :, None]
            j = btk[:, None, :]
            mask = (i < j) | (i > j + WINDOW) | (j == -1)
            sim = jnp.where(mask, -jnp.finfo(sim.dtype).max, sim)
            attn = jax.nn.softmax(sim, axis=-1)
            out = jnp.einsum('bhwij,bhwjd->bhwid', attn, bv)
            return out.reshape(b, h, n, d)

        def _layer(x, wqkv, qs, ksc, wo, lg, lb, w1, b1, w2, b2):
            b, n, _ = x.shape
            h = shift_token(x)
            qkv = h @ wqkv
            q, k, v = jnp.split(qkv, 3, axis=-1)
            to_heads = lambda t: t.reshape(b, n, HEADS, DIM_HEAD).transpose(0, 2, 1, 3)
            q, k, v = (to_heads(q), to_heads(k), to_heads(v))
            q = l2norm(q) * qs
            k = l2norm(k) * ksc
            q, k = rotary_xpos(q, k)
            o = local_attention(q, k, v)
            o = o.transpose(0, 2, 1, 3).reshape(b, n, INNER)
            x = x + o @ wo
            h = shift_token(x)
            mu = h.mean(-1, keepdims=True)
            var = h.var(-1, keepdims=True)
            h = (h - mu) / jnp.sqrt(var + 1e-05) * lg + lb
            h = h @ w1 + b1
            a, g = jnp.split(h, 2, axis=-1)
            h = a * jax.nn.gelu(g, approximate=False)
            x = x + h @ w2 + b2
            return x
        for l in range(DEPTH):
            x = _layer(x, wqkv[l], q_scale[l], k_scale[l], wo[l], ln_g[l], ln_b[l], w1[l], b1[l], w2[l], b2[l])
        return x

    def _L1_attn_ref(x, W_kqv, m):
        import jax, jax.numpy as jnp
        import numpy as np
        import math
        D_MODEL = 128
        NUM_HEADS = 16
        B, S, D = x.shape
        H = NUM_HEADS
        hd = D // H
        scale = math.sqrt(D)
        kqv = x @ W_kqv
        k, q, v = jnp.split(kqv, 3, axis=-1)
        q = q.reshape(B, S, H, hd)
        k = k.reshape(B, S, H, hd)
        v = v.reshape(B, S, H, hd)
        rel = (jnp.arange(S)[None, :] - jnp.arange(S)[:, None]).astype(x.dtype)
        bias = m[None, :, :, :] * rel[None, None, :, :]
        score = jnp.einsum('bqhd,bkhd->bhqk', q, k) / scale + bias
        causal = jnp.tril(jnp.ones((S, S), dtype=bool))
        score = jnp.where(causal[None, None, :, :], score, -jnp.inf)
        attn = jax.nn.softmax(score, axis=-1)
        out = jnp.einsum('bhqk,bkhd->bqhd', attn, v).reshape(B, S, D)
        return out

    def _L1_ffn_ref(x, Wg, bg, W1, W2):
        import jax, jax.numpy as jnp
        import numpy as np
        E = 8
        K = 2
        R = 64
        ALPHA = 128.0
        SCALING = ALPHA / R
        orig_shape = x.shape
        D = orig_shape[-1]
        xf = x.reshape(-1, D)
        logits = xf @ Wg.T + bg
        top_gates, top_idx = jax.lax.top_k(logits, K)
        top_gates = jax.nn.softmax(top_gates, axis=-1)
        h = jax.nn.gelu(jnp.einsum('nd,erd->enr', xf, W1), approximate=False)
        eout = SCALING * jnp.einsum('enr,edr->ned', h, W2)
        sel = jnp.take_along_axis(eout, top_idx[:, :, None], axis=1)
        out = jnp.sum(top_gates[:, :, None] * sel, axis=1)
        return out.reshape(orig_shape)
    x = L0_attn_x
    x = x + _layernorm(_L0_attn_ref(_layernorm(x, axis=-1), L0_attn_Wq, L0_attn_bq, L0_attn_Wk, L0_attn_bk, L0_attn_Wv, L0_attn_bv), axis=-1)
    x = x + _layernorm(_L0_ffn_ref(_layernorm(x, axis=-1), L0_ffn_wqkv, L0_ffn_q_scale, L0_ffn_k_scale, L0_ffn_wo, L0_ffn_ln_g, L0_ffn_ln_b, L0_ffn_w1, L0_ffn_b1, L0_ffn_w2, L0_ffn_b2), axis=-1)
    x = x + _layernorm(_L1_attn_ref(_layernorm(x, axis=-1), L1_attn_W_kqv, L1_attn_m), axis=-1)
    x = x + _layernorm(_L1_ffn_ref(_layernorm(x, axis=-1), L1_ffn_Wg, L1_ffn_bg, L1_ffn_W1, L1_ffn_W2), axis=-1)
    return x

_drawn_inputs = setup_inputs


def setup_inputs(seed=0):
    import zlib

    import numpy as np

    out = dict(_drawn_inputs(seed))
    spreads = {'L0_ffn_q_scale': (1.0, 0.6),
     'L0_ffn_k_scale': (1.0, 0.6),
     'L0_ffn_ln_g': (1.0, 0.6),
     'L0_ffn_ln_b': (0.0, 0.655),
     'L0_ffn_b1': (0.0, 0.31),
     'L0_ffn_b2': (0.0, 0.1),
     'L1_ffn_bg': (0.0, 0.1)}
    factors = {'L0_attn_bk': 8.0}
    for name, (base, spread) in spreads.items():
        noise = np.random.default_rng([zlib.crc32(name.encode()), seed]).standard_normal(out[name].shape)
        drawn = base * np.exp(spread * noise) if base else spread * noise
        out[name] = jnp.asarray(drawn.astype(out[name].dtype))
    for name, factor in factors.items():
        out[name] = (out[name] * factor).astype(out[name].dtype)
    return out
```

```python
import math
from contextlib import ExitStack

import numpy as np
import concourse.bass as bass
from concourse import mybir

F32 = mybir.dt.float32
ALU = mybir.AluOpType
ACT = mybir.ActivationFunctionType
AX = mybir.AxisListType

P = 128
SEQ = 256
TPS = SEQ // P
LANES = 4
BANK = 512
LN_EPS = 1e-5
LOWEST = -3.0e38
MASKED = -1.0e30

HEADS_A, HD_A = 16, 8
QUADS = HEADS_A // 4
ITERS = 6
HEADS_B, HD_B, WIN = 8, 64, 64
INNER = HEADS_B * HD_B
HID = 341
EXPERTS, RANK = 8, 64
KEYS = 3 * P


class Queue:

    FIXED = {"pe": 3.0, "act": 90.0, "dve": 70.0, "pool": 70.0, "sp": 50.0}
    PER_COLUMN = {"act": 0.83, "dve": 1.04, "pool": 2.2}

    def __init__(self, name, engine):
        self.name, self.engine, self.clock = name, engine, 0.0
        self.wait_ge, self.dma_start = engine.wait_ge, engine.dma_start

    def took(self, instruction, columns):
        self.clock += self.FIXED[self.name] + self.PER_COLUMN[self.name] * columns
        return instruction

    def matmul(self, out, lhsT, rhs, **kw):
        m, n = lhsT.free_size(), rhs.free_size()
        self.clock += self.FIXED["pe"] + 4 * (n / 2.4 if n >= 96 else max(n / 2.4, m / 1.2))
        return self.engine.matmul(out, lhsT, rhs, **kw)

    def transpose(self, out, in_, identity):
        self.clock += self.FIXED["pe"] + in_.free_size() / 1.2
        return self.engine.transpose(out, in_, identity)

    def activation(self, out, in_, func, **kw):
        extra = 186 if "accum_out" in kw else 0
        return self.took(self.engine.activation(out, in_, func, **kw), extra + out.free_size())

    def memset(self, out, value):
        return self.took(self.engine.memset(out, value), out.free_size())

    def tensor_copy(self, out, in_):
        return self.took(self.engine.tensor_copy(out, in_), out.free_size())

    def reciprocal(self, out, in_):
        return self.took(self.engine.reciprocal(out, in_), out.free_size())

    def tensor_tensor(self, out, in0, in1, op):
        slow = 70 if op == ALU.pow else 1
        return self.took(self.engine.tensor_tensor(out, in0, in1, op), slow * out.free_size())

    def tensor_scalar(self, out, in_, scalar1, scalar2, *ops):
        return self.took(self.engine.tensor_scalar(out, in_, scalar1, scalar2, *ops), out.free_size() / 2)

    def scalar_tensor_tensor(self, out, **kw):
        return self.took(self.engine.scalar_tensor_tensor(out=out, **kw), out.free_size())

    def tensor_tensor_reduce(self, out, **kw):
        return self.took(self.engine.tensor_tensor_reduce(out=out, **kw), out.free_size())

    def tensor_reduce(self, out, in_, **kw):
        return self.took(self.engine.tensor_reduce(out=out, in_=in_, **kw), in_.free_size())

    def bn_stats(self, out, in_):
        return self.took(self.engine.bn_stats(out, in_), in_.free_size())

    def bn_aggr(self, out, in_):
        return self.took(self.engine.bn_aggr(out, in_), in_.free_size())


class Engines:

    LATENCY = 170.0

    def __init__(self, nc, ctx):
        self.nc, self.ctx = nc, ctx
        self.queues = {n: Queue(n, e) for n, e in (("pe", nc.tensor), ("act", nc.scalar), ("dve", nc.vector),
                                                   ("pool", nc.gpsimd), ("sp", nc.sync))}
        self.sems = {n: ctx.enter_context(nc.semaphore(f"done_{n}")) for n in self.queues if n != "sp"}
        self.count = dict.fromkeys(self.sems, 0)
        self.seen = {}
        self.end = {}

    def done(self, name, instruction):
        instruction.then_inc(self.sems[name], 1)
        self.count[name] += 1
        mark = (name, self.count[name])
        self.end[mark] = self.queues[name].clock + self.LATENCY
        return mark

    def ready(self, marks):
        if isinstance(marks, list):
            return max((self.ready(m) for m in marks), default=0.0)
        return self.end.get(marks, 0.0)

    def after(self, name, *marks):
        queue = self.queues[name]
        for mark in marks:
            if mark is None:
                continue
            if isinstance(mark, list):
                self.after(name, *mark)
                continue
            queue.clock = max(queue.clock, self.ready(mark))
            source, value = mark
            if self.seen.get((name, source), 0) < value:
                queue.wait_ge(self.sems[source], value)
                self.seen[(name, source)] = value

    def dma(self, group, out, in_):
        if group not in self.sems:
            self.sems[group] = self.ctx.enter_context(self.nc.semaphore(group))
            self.count[group] = 0
        self.queues["sp"].dma_start(out, in_).then_inc(self.sems[group], 16)
        self.count[group] += 16
        return (group, self.count[group])

    def barrier(self):
        marks = [(n, self.count[n]) for n in self.queues if self.count.get(n)]
        for name in self.queues:
            self.after(name, marks)

    def in_lanes(self, tasks):
        queues = [list(tasks[n::LANES]) for n in range(LANES)]
        running, marks, since, turn = [None] * LANES, [[]] * LANES, [0] * LANES, 0

        def advance(lane):
            if running[lane] is not None:
                try:
                    marks[lane] = list(next(running[lane]))
                    return
                except StopIteration:
                    running[lane] = None
            if queues[lane]:
                running[lane] = queues[lane].pop(0)(lane)
                marks[lane] = list(next(running[lane]))

        for lane in range(LANES):
            advance(lane)
        while any(r is not None for r in running):
            now = self.queues["pe"].clock
            lane = min((n for n in range(LANES) if running[n] is not None),
                       key=lambda n: (max(now, self.ready(marks[n])), since[n]))
            self.after("pe", *marks[lane])
            turn += 1
            since[lane] = turn
            advance(lane)


def bc(ap, width):
    return ap.unsqueeze(len(ap.shape)).broadcast_to([*ap.shape, width])


def bass_four_blocks(nc, io):
    n_seq = io["x"].shape[0]
    n_tiles = n_seq * TPS
    top = ExitStack()
    with top:
        E = Engines(nc, top)
        pe, act, dve, pool = (E.queues[n] for n in ("pe", "act", "dve", "pool"))

        def sb(ctx, name, shape, dt=F32):
            return ctx.enter_context(nc.sbuf_tensor(name, shape, dt))

        psum = top.enter_context(nc.psum_tensor("psum", [P, 2 * LANES, BANK], F32))

        stream = sb(top, "stream", [P, n_tiles, P])
        ident = sb(top, "ident", [P, P])
        ones = sb(top, "ones", [P, P])
        stats = sb(top, "stats", [P, n_tiles, 6])
        moments = sb(top, "moments", [P, n_tiles, 2])
        deviation = sb(top, "deviation", [P, n_tiles])
        rstd = sb(top, "rstd", [P, n_tiles])
        eps = sb(top, "eps", [P, 1])
        quad_mask = sb(top, "quad_mask", [P, 4])
        ident_in = E.dma("load_ident", ident[:, :], io["ident"])
        ones_set = E.done("dve", dve.memset(ones[:, :], 1.0))
        eps_set = E.done("dve", dve.memset(eps[:, :], LN_EPS))
        x_dram = io["x"].rearrange("b (i p) d -> p (b i) d", p=P)
        out_dram = io["out"].rearrange("b (i p) d -> p (b i) d", p=P)
        TG = min(8, n_tiles)

        def norm_stats(src, ready):
            for t in range(n_tiles):
                E.after("dve", ready[t])
                last = E.done("dve", dve.bn_stats(stats[:, t, :], src[:, t, :]))
            E.after("dve", last)
            for t in range(n_tiles):
                last = E.done("dve", dve.bn_aggr(moments[:, t, :], stats[:, t, :]))
            E.after("act", last, eps_set)
            root = E.done("act", act.activation(deviation[:, :], moments[:, :, 1], ACT.Sqrt, bias=eps[:, 0:1]))
            E.after("dve", root)
            ready_rstd = E.done("dve", dve.reciprocal(rstd[:, :], deviation[:, :]))
            E.after("dve", ready_rstd)
            return ready_rstd

        def norm_apply(dst, src):
            return [E.done("dve", dve.tensor_scalar(dst[:, t, :], src[:, t, :], moments[:, t, 0:1],
                                                    rstd[:, t:t + 1], ALU.subtract, ALU.mult))
                    for t in range(n_tiles)]

        def residual_norm(x, ready, final=False):
            norm_stats(stream, ready)
            normed = norm_apply(stream, stream)
            added = []
            for g in range(0, n_tiles, TG):
                E.after("dve", normed[g + TG - 1])
                added += [E.done("dve", dve.tensor_tensor(x[:, g:g + TG, :], x[:, g:g + TG, :],
                                                          stream[:, g:g + TG, :], ALU.add))] * TG
            if final:
                return added
            norm_stats(x, added)
            return norm_apply(stream, x)

        def both(lane):
            return psum[:, 2 * lane:2 * lane + 2, :]

        def separate(mask, dst, src, ready):
            n = src.shape[1]
            E.after("pool", ready)
            return E.done("pool", pool.tensor_tensor(dst, src.unsqueeze(1).broadcast_to([P, 4, n]), bc(mask[:, :], n), ALU.mult))

        def diagonal(t):
            flat = t.rearrange("p j c -> p (j c)")
            return bass.AP(flat.tensor, flat.offset, [flat.ap[0], [32 + HD_A, 4], [1, HD_A]])

        lane_free = [None] * LANES

        def transposed_input(lane, b, dst):
            bank = psum[:, 2 * lane, :]
            for i in range(TPS):
                mm = pe.transpose(bank[:, i * P:(i + 1) * P], stream[:, TPS * b + i, :], ident[:, :])
            turned = E.done("pe", mm)
            E.after("act", turned)
            return turned, E.done("act", act.activation(dst, bank[:, 0:SEQ], ACT.Copy))

        with ExitStack() as a:
            wq = sb(a, "a_wq", [P, QUADS, P])
            wk = sb(a, "a_wk", [P, QUADS, P])
            wv = sb(a, "a_wv", [P, P])
            bq = sb(a, "a_bq", [P, QUADS])
            bk = sb(a, "a_bk", [P, QUADS])
            bv = sb(a, "a_bv", [P, P])
            for dst, src in ((wq[:, :, :], "a_wq"), (wk[:, :, :], "a_wk"), (wv[:, :], "a_wv"),
                             (bq[:, :], "a_bq"), (bk[:, :], "a_bk"), (bv[:, :], "a_bv"),
                             (quad_mask[:, :], "quad_mask")):
                loaded = E.dma("load_a", dst, io[src])
            kern2 = sb(a, "kern2", [P, n_seq * HEADS_A, P])
            colsum = sb(a, "colsum", [1, n_seq * QUADS])
            inv_c = sb(a, "inv_c", [P, 1])
            peak_one = sb(a, "peak_one", [1, 1])
            raw = [sb(a, f"a_raw{n}", [P, 8, P]) for n in range(LANES)]
            turn = [sb(a, f"a_turn{n}", [P, 8 * (P + HD_A)]) for n in range(LANES)]
            feat = [t[:, 4 * P:4 * P + SEQ] for t in turn]
            state = [sb(a, f"a_state{n}", [P, 4, P + HD_A]) for n in range(LANES)]
            q_t = [sb(a, f"a_q{n}", [P, SEQ]) for n in range(LANES)]
            k_lm = [sb(a, f"a_klm{n}", [P, P]) for n in range(LANES)]
            small = [sb(a, f"a_small{n}", [P, 48]) for n in range(LANES)]
            apart = [sb(a, f"a_apart{n}", [P, TPS, 4, 32]) for n in range(LANES)]
            for n in range(LANES):
                apart_zero = E.done("dve", dve.memset(apart[n][:, :, :, :], 0.0))

            MW = P + HD_A

            x_ready = []
            for g in range(0, n_tiles, TG):
                x_ready += [E.dma(f"load_x{g}", stream[:, g:g + TG, :], x_dram[:, g:g + TG, :])] * TG
            norm_stats(stream, x_ready)
            normed = norm_apply(stream, stream)

            root_scale = 1.0 / math.sqrt(math.sqrt(HD_A))
            E.after("dve", loaded)
            dve.tensor_scalar(bq[:, :], bq[:, :], root_scale, None, ALU.mult)
            scaled_bias = E.done("dve", dve.tensor_scalar(bk[:, :], bk[:, :], root_scale, None, ALU.mult))
            E.after("act", scaled_bias)
            E.after("pool", loaded)

            def softmax_rows(lane, banks, n_rows, width, scale, dst, maxes, negs, sums, scored):
                E.after("dve", scored)
                peaked = E.done("dve", dve.tensor_reduce(out=maxes, in_=banks, axis=AX.X, op=ALU.max))
                E.after("dve", peaked)
                negated = E.done("dve", dve.tensor_scalar(negs, maxes, -scale, None, ALU.mult))
                E.after("act", negated)
                for r in range(n_rows):
                    mark = E.done("act", act.activation(dst[:, r, :], banks[:, r, :], ACT.Exp, bias=negs[:, r:r + 1],
                                                        scale=scale, accum_out=sums[:, r:r + 1]))
                return mark

            def kernel2_task(b, g):
                def steps(lane):
                    b0, b1 = psum[:, 2 * lane, :], psum[:, 2 * lane + 1, :]
                    lm = raw[lane][:, 0, :]
                    q_lm, kk_lm = raw[lane][:, 1, :], raw[lane][:, 2, :]
                    expd = turn[lane][:, 0:4 * P].rearrange("p (j m) -> p j m", j=4)
                    sm = small[lane]
                    maxes, negs, sums, inv = sm[:, 0:4], sm[:, 4:8], sm[:, 8:12], sm[:, 12:16]
                    yield normed[TPS * b + TPS - 1], lane_free[lane]
                    turned, copied = transposed_input(lane, b, feat[lane])
                    E.after("dve", copied)
                    pairs = feat[lane].rearrange("p (m s) -> p m s", s=2)
                    summed = E.done("dve", dve.tensor_tensor(lm, pairs[:, :, 0], pairs[:, :, 1], ALU.add))
                    yield summed,
                    pe.matmul(b0[:, 0:P], wq[:, g, :], lm, start=True, stop=True)
                    projected = E.done("pe", pe.matmul(b0[:, P:2 * P], wk[:, g, :], lm, start=True, stop=True))
                    E.after("act", projected)
                    E.done("act", act.activation(q_lm, b0[:, 0:P], ACT.Identity, bias=bq[:, g:g + 1], scale=0.5 * root_scale))
                    kk_ready = E.done("act", act.activation(kk_lm, b0[:, P:2 * P], ACT.Identity, bias=bk[:, g:g + 1], scale=0.5 * root_scale))
                    kk_sep = raw[lane][:, 4:8, :]
                    ready = separate(quad_mask, kk_sep, kk_lm, kk_ready)
                    yield kk_ready, ready,
                    scored = E.done("pe", pe.matmul(b1, q_lm, kk_sep, start=True, stop=True))
                    scores = b1.rearrange("p (j m) -> p j m", j=4)
                    expd_all = softmax_rows(lane, scores, 4, P, 1.0, expd, maxes, negs, sums, scored)
                    E.after("dve", expd_all)
                    inverted = E.done("dve", dve.reciprocal(inv, sums))
                    E.after("dve", inverted)
                    h0 = HEADS_A * b + 4 * g
                    normalized = E.done("dve", dve.tensor_tensor(kern2[:, h0:h0 + 4, :], expd, bc(inv, P), ALU.mult))
                    yield normalized,
                    sums_ready = E.done("pe", pe.matmul(b0[0:1, :], ones[:, 0:1], kern2[:, h0:h0 + 4, :], start=True, stop=True))
                    E.after("dve", sums_ready)
                    n = QUADS * b + g
                    lane_free[lane] = last_colsum[0] = E.done("dve", dve.tensor_reduce(out=colsum[:, n:n + 1], in_=b0[0:1, :], axis=AX.X, op=ALU.max))
                return steps

            last_colsum = [None]
            E.in_lanes([kernel2_task(b, g) for b in range(n_seq) for g in range(QUADS)])

            E.after("dve", last_colsum[0])
            peaked = E.done("dve", dve.tensor_reduce(out=peak_one[:, :], in_=colsum[:, :], axis=AX.X, op=ALU.max))
            E.barrier()
            spread = E.done("pe", pe.matmul(psum[:, 1, 0:1], ones[0:1, :], peak_one[:, :], start=True, stop=True))
            E.after("dve", spread)
            c_ready = E.done("dve", dve.reciprocal(inv_c[:, :], psum[:, 1, 0:1]))
            E.barrier()

            BETA = 2.75 / 13.0
            turned_by = {}

            def nystrom_task(b, g):
                def steps(lane):
                    b0, b1, two = psum[:, 2 * lane, :], psum[:, 2 * lane + 1, :], both(lane)
                    st, sm = state[lane], small[lane]
                    halves = lambda bank: bank.rearrange("p (j m) -> p j m", j=4)
                    k_t = st[:, :, :].rearrange("p j c -> p (j c)")[:, 0:SEQ]
                    q_lm = st[:, :, :].rearrange("p j c -> p (j c)")[:, SEQ:SEQ + P]
                    v_wide = apart[lane][:, :, :, :]
                    z_wide, w_wide = apart[lane][:, 0, :, :], apart[lane][:, 1, :, :]
                    rows_ = raw[lane][0:32, 4:6, :].rearrange("p r m -> p (r m)")
                    h0 = HEADS_A * b + 4 * g
                    head = lambda j: kern2[:, h0 + j, :]
                    yield lane_free[lane],
                    turned, copied = transposed_input(lane, b, feat[lane])
                    turned_by[b, g] = turned
                    yield copied,
                    pe.matmul(b0[:, 0:SEQ], wq[:, g, :], feat[lane], start=True, stop=True)
                    pe.matmul(b0[:, SEQ:2 * SEQ], wk[:, g, :], feat[lane], start=True, stop=True)
                    for i in range(TPS):
                        mm = pe.matmul(b1[:, P * i:P * (i + 1)], feat[lane][:, i * P:(i + 1) * P], wv[:, :], start=True, stop=True)
                    projected = E.done("pe", mm)
                    E.after("act", projected)
                    E.done("act", act.activation(q_t[lane][:, :], b0[:, 0:SEQ], ACT.Identity, bias=bq[:, g:g + 1], scale=root_scale))
                    qk_ready = E.done("act", act.activation(k_t, b0[:, SEQ:2 * SEQ], ACT.Identity, bias=bk[:, g:g + 1], scale=root_scale))
                    E.after("dve", projected)
                    for i in range(TPS):
                        cols = slice(P * i + 32 * g, P * i + 32 * g + 32)
                        v_ready = E.done("dve", dve.tensor_tensor(
                            diagonal(v_wide[:, i, :, :]), b1[:, cols].rearrange("p (j d) -> p j d", j=4),
                            bv[:, 32 * g:32 * g + 32].rearrange("p (j d) -> p j d", j=4), ALU.add))
                    E.after("dve", qk_ready)
                    q2 = q_t[lane][:, :].rearrange("p (m s) -> p m s", s=2)
                    k2 = k_t.rearrange("p (m s) -> p m s", s=2)
                    dve.tensor_tensor(q_lm, q2[:, :, 0], q2[:, :, 1], ALU.add)
                    lm_ready = E.done("dve", dve.tensor_tensor(k_lm[lane][:, :], k2[:, :, 0], k2[:, :, 1], ALU.add))
                    q_sep = turn[lane][:, 0:4 * P].rearrange("p (j m) -> p j m", j=4)
                    sep_ready = separate(quad_mask, q_sep, q_lm, lm_ready)
                    yield sep_ready,
                    for j in range(4):
                        mm = pe.matmul(two[:, j // 2, SEQ * (j % 2):SEQ * (j % 2) + SEQ], q_sep[:, j, :], k_t,
                                       start=True, stop=True)
                    scored = E.done("pe", mm)
                    maxes, negs, sums3, inv3 = sm[:, 0:4], sm[:, 4:8], sm[:, 8:12], sm[:, 12:16]
                    expd3 = raw[lane][:, :, :].rearrange("p (j i) m -> p j (i m)", i=TPS)
                    exped = softmax_rows(lane, two.rearrange("p k (j m) -> p (k j) m", j=2), 4, SEQ, 0.5, expd3,
                                         maxes, negs, sums3, scored)
                    E.after("dve", exped)
                    inv3_ready = E.done("dve", dve.reciprocal(inv3, sums3))
                    yield exped,
                    for i in range(TPS):
                        for j in range(4):
                            mm = pe.transpose(two[:, i, j * P:(j + 1) * P], raw[lane][:, TPS * j + i, :], ident[:, :])
                    turned = E.done("pe", mm)
                    turn3 = turn[lane][:, 0:8 * P].rearrange("p (i c) -> p i c", i=TPS)
                    E.after("act", turned)
                    half0 = E.done("act", act.activation(turn3[:, 0, :], b0[:, :], ACT.Copy))
                    E.after("dve", turned)
                    half1 = E.done("dve", dve.tensor_copy(turn3[:, 1, :], b1[:, :]))
                    yield half0, half1, v_ready
                    for i in range(TPS):
                        for j in range(4):
                            mm = pe.matmul(b0[0:32, 0:P], v_wide[:, i, j, :], turn3[:, i, j * P:(j + 1) * P],
                                           start=(i == 0 and j == 0), stop=(i == TPS - 1 and j == 3))
                    y_raw = E.done("pe", mm)
                    for j in range(4):
                        mm = pe.transpose(b1[:, j * P:(j + 1) * P], head(j), ident[:, :])
                    turned = E.done("pe", mm)
                    E.after("dve", y_raw)
                    y_rows = E.done("dve", dve.tensor_copy(rows_[:, 0:P], b0[0:32, 0:P]))
                    E.after("act", turned)
                    k2t_ready = E.done("act", act.activation(raw[lane][:, 0:4, :], halves(b1), ACT.Copy))
                    yield k2t_ready, y_rows,
                    y_turned = E.done("pe", pe.transpose(b1[:, 0:32], rows_[:, 0:P], ident[0:32, 0:32]))
                    for j in range(4):
                        mm = pe.matmul(b0[:, j * P:(j + 1) * P], raw[lane][:, j, :], raw[lane][:, j, :], start=True, stop=True)
                    squared = E.done("pe", mm)
                    E.after("dve", y_turned, inv3_ready)
                    y_ready = E.done("dve", dve.tensor_tensor(st[:, :, P:MW], b1[:, 0:32].rearrange("p (j d) -> p j d", j=4),
                                                              bc(inv3, HD_A), ALU.mult))
                    E.after("act", squared, c_ready)
                    state_ready = E.done("act", act.activation(st[:, :, 0:P], halves(b0), ACT.Copy, scale=inv_c[:, 0:1]))
                    yield state_ready, y_ready
                    s = 1.0
                    n4 = 4 * MW
                    bu = turn[lane][:, 0:n4].rearrange("p (j c) -> p j c", j=4)
                    diff = raw[lane][:, :, :].rearrange("p r m -> p (r m)")[:, 0:n4].rearrange("p (j c) -> p j c", j=4)
                    lin = turn[lane][:, n4:2 * n4].rearrange("p (j c) -> p j c", j=4)
                    pairs_of = lambda t: t.rearrange("p (k j) c -> p k (j c)", k=2)
                    out_of = lambda j: two[:, j // 2, MW * (j % 2):MW * (j % 2) + MW]
                    for k in range(ITERS):
                        for j in range(4):
                            mm = pe.matmul(out_of(j), st[:, j, 0:P], st[:, j, :], start=True, stop=True)
                        produced = E.done("pe", mm)
                        E.after("act", produced)
                        bu_ready = E.done("act", act.activation(pairs_of(bu), two[:, :, 0:2 * MW], ACT.Copy, scale=BETA / s))
                        E.after("dve", bu_ready, y_ready)
                        diff_ready = E.done("dve", dve.scalar_tensor_tensor(out=diff, in0=st[:, :, :], scalar=-3.5 * BETA,
                                                                            in1=bu, op0=ALU.mult, op1=ALU.add))
                        E.after("pool", bu_ready, y_ready, state_ready)
                        lin_ready = E.done("pool", pool.tensor_tensor(lin, st[:, :, :], bu, ALU.subtract))
                        yield diff_ready,
                        for j in range(4):
                            mm = pe.matmul(out_of(j), diff[:, j, 0:P], diff[:, j, :], start=True, stop=True)
                        produced = E.done("pe", mm)
                        E.after("dve", produced, lin_ready)
                        if k < ITERS - 1:
                            state_ready = E.done("dve", dve.scalar_tensor_tensor(
                                out=pairs_of(st[:, :, :]), in0=two[:, :, 0:2 * MW], scalar=-1.0 / (13.0 * BETA * BETA * s), in1=pairs_of(lin),
                                op0=ALU.mult, op1=ALU.add))
                            y_ready = state_ready
                        else:
                            for q in range(2):
                                z_ready = E.done("dve", dve.scalar_tensor_tensor(
                                    out=diagonal(z_wide)[:, 2 * q:2 * q + 2, :], scalar=-1.0 / (13.0 * BETA * BETA * s), op0=ALU.mult, op1=ALU.add,
                                    in0=two[:, q, 0:2 * MW].rearrange("p (j c) -> p j c", j=2)[:, :, P:MW],
                                    in1=lin[:, 2 * q:2 * q + 2, P:MW]))
                            y_ready = state_ready = z_ready
                        s *= 4.0 / 13.0
                        yield state_ready,
                    for j in range(4):
                        mm = pe.matmul(b1[0:32, 0:P], z_wide[:, j, :], head(j), start=(j == 0), stop=(j == 3))
                    produced = E.done("pe", mm)
                    E.after("dve", produced, c_ready)
                    w_rows = E.done("dve", dve.tensor_scalar(rows_[:, 0:P], b1[0:32, 0:P], inv_c[0:32, 0:1], 1.0 / s, ALU.mult, ALU.mult))
                    k_sep = turn[lane][:, 0:4 * P].rearrange("p (j m) -> p j m", j=4)
                    sep_ready = separate(quad_mask, k_sep, k_lm[lane][:, :], [z_ready, lm_ready])
                    yield w_rows,
                    turned = E.done("pe", pe.transpose(b0[:, 0:32], rows_[:, 0:P], ident[0:32, 0:32]))
                    E.after("dve", turned)
                    w_ready = E.done("dve", dve.tensor_copy(diagonal(w_wide), b0[:, 0:32].rearrange("p (j d) -> p j d", j=4)))
                    yield w_ready, sep_ready,
                    for i in range(TPS):
                        mm = pe.matmul(two[:, i, :], q_t[lane][:, i * P:(i + 1) * P], k_sep, start=True, stop=True)
                    scored = E.done("pe", mm)
                    maxes1, negs1, sums1, inv1 = sm[:, 16:24], sm[:, 24:32], sm[:, 32:40], sm[:, 40:48]
                    exped = softmax_rows(lane, two.rearrange("p k (j m) -> p (k j) m", j=4), 8, P, 0.5, raw[lane],
                                         maxes1, negs1, sums1, scored)
                    E.after("dve", exped)
                    inv1_ready = E.done("dve", dve.reciprocal(inv1, sums1))
                    yield exped,
                    for r in range(8):
                        mm = pe.transpose(two[:, r // 4, (r % 4) * P:(r % 4 + 1) * P], raw[lane][:, r, :], ident[:, :])
                    turned = E.done("pe", mm)
                    turn1 = turn[lane][:, 0:8 * P].rearrange("p (i c) -> p i c", i=TPS)
                    E.after("act", turned)
                    half0 = E.done("act", act.activation(turn1[:, 0, :], b0[:, :], ACT.Copy))
                    E.after("dve", turned)
                    half1 = E.done("dve", dve.tensor_copy(turn1[:, 1, :], b1[:, :]))
                    yield half0, half1,
                    for i in range(TPS):
                        for j in range(4):
                            mm = pe.matmul(b0[0:32, i * P:(i + 1) * P], w_wide[:, j, :], turn1[:, i, j * P:(j + 1) * P],
                                           start=(j == 0), stop=(j == 3))
                    produced = E.done("pe", mm)
                    E.after("act", produced)
                    x_rows = E.done("act", act.activation(rows_, b0[0:32, 0:SEQ], ACT.Copy))
                    yield x_rows,
                    for i in range(TPS):
                        mm = pe.transpose(b1[:, 32 * i:32 * i + 32], rows_[:, i * P:(i + 1) * P], ident[0:32, 0:32])
                    produced = E.done("pe", mm)
                    E.after("dve", produced, inv1_ready, [turned_by[b, q] for q in range(QUADS)])
                    out_view = stream[:, TPS * b:TPS * b + TPS, 32 * g:32 * g + 32].rearrange("p i (j d) -> p i j d", d=HD_A)
                    lane_free[lane] = written[b, g] = E.done("dve", dve.tensor_tensor(
                        out_view, b1[:, 0:64].rearrange("p (i j d) -> p i j d", i=TPS, j=4),
                        bc(inv1.rearrange("p (i j) -> p i j", i=TPS), HD_A), ALU.mult))
                return steps

            written = {}
            E.in_lanes([nystrom_task(b, g) for b in range(n_seq) for g in range(QUADS)])
            block_out = [[written[t // TPS, g] for g in range(QUADS)] for t in range(n_tiles)]
            E.barrier()

        x = sb(top, "x", [P, n_tiles, P])
        x_ready = []
        for g in range(0, n_tiles, TG):
            mark = E.dma("load_x_again", x[:, g:g + TG, :], x_dram[:, g:g + TG, :])
        E.after("dve", mark)
        dump = io.get("dump")

        def debug(n, src):
            if dump is not None:
                E.barrier()
                m = E.dma(f"dump{n}", dump[n].rearrange("b (i p) d -> p (b i) d", p=P), src[:, :, :])
                for e in ("pe", "act", "dve", "pool", "sp"):
                    E.after(e, m)

        debug(0, stream)
        stream_ready = residual_norm(x, block_out)
        debug(1, stream)

        def soft_scores(lane, q_of, k_of, bias_of, scale, sc, ex, et, sm, sums, weighted):
            two = both(lane)
            for h in range(2):
                pe.matmul(two[:, h, 0:P], q_of(h, 0), k_of(h)[:, 0:P], start=True, stop=True)
                mm = pe.matmul(two[:, h, P:KEYS], q_of(h, 1), k_of(h), start=True, stop=True)
            scored = E.done("pe", mm)
            E.after("dve", scored)
            maxes, negs, inv = sm[:, 0:4], sm[:, 4:8], sm[:, 8:12]
            spans = [(0, P), (P, KEYS)]
            for h in range(2):
                for i, (lo, hi) in enumerate(spans):
                    r = TPS * h + i
                    mark = E.done("dve", dve.tensor_tensor_reduce(
                        out=sc[:, h, lo:hi], in0=two[:, h, lo:hi], in1=bias_of(h)[:, lo:hi], scale=1.0, scalar=LOWEST,
                        op0=ALU.add, op1=ALU.max, accum_out=maxes[:, r:r + 1]))
            E.after("dve", mark)
            negated = E.done("dve", dve.tensor_scalar(negs, maxes, -scale, None, ALU.mult))
            E.after("act", negated)
            ready = []
            for h in range(2):
                for i, (lo, hi) in enumerate(spans):
                    r = TPS * h + i
                    exped = E.done("act", act.activation(ex[:, h, lo:hi], sc[:, h, lo:hi], ACT.Exp, bias=negs[:, r:r + 1],
                                                         scale=scale, accum_out=sums[:, i, h:h + 1]))
                if weighted:
                    E.after("dve", exped)
                    invs = E.done("dve", dve.reciprocal(inv[:, TPS * h:TPS * h + TPS], sums[:, :, h]))
                    E.after("dve", invs)
                    for i, (lo, hi) in enumerate(spans):
                        exped = E.done("dve", dve.tensor_scalar(ex[:, h, lo:hi], ex[:, h, lo:hi], inv[:, TPS * h + i:TPS * h + i + 1],
                                                                None, ALU.mult))
                ready.append(exped)
            yield ready
            for h in range(2):
                for c in range(3):
                    mm = pe.transpose(two[:, h, c * P:(c + 1) * P], ex[:, h, c * P:(c + 1) * P], ident[:, :])
            turned = E.done("pe", mm)
            E.after("act", turned)
            half0 = E.done("act", act.activation(et[:, 0, :], two[:, 0, 0:KEYS], ACT.Copy))
            E.after("dve", turned)
            half1 = E.done("dve", dve.tensor_copy(et[:, 1, :], two[:, 1, 0:KEYS]))
            return [half0, half1]

        for layer in range(2):
            E.barrier()
            with ExitStack() as s_:
                wqkv = sb(s_, f"b_wqkv{layer}", [P, 3 * INNER])
                wo = sb(s_, f"b_wo{layer}", [P, INNER // P, P])
                rope = sb(s_, f"b_rope{layer}", [P, 4, TPS, HD_B])
                gain = sb(s_, f"b_gain{layer}", [P, 4, HD_B])
                band = sb(s_, f"b_band{layer}", [P, KEYS])
                half_neg = sb(s_, f"b_half{layer}", [P, 2 * HEADS_B])
                for dst, src in ((wqkv[:, :], io["b_wqkv"][layer]), (wo[:, :, :], io["b_wo"][layer]),
                                 (rope[:, :, :, :], io["b_rope"]), (gain[:, :, :], io["b_gain"][layer]),
                                 (band[:, :], io["b_band"])):
                    loaded = E.dma(f"load_b{layer}", dst, src)
                E.after("dve", loaded)
                tabled = E.done("dve", dve.tensor_tensor(rope[:, :, :, :], rope[:, :, :, :],
                                                         gain[:, :, :].unsqueeze(2).broadcast_to([P, 4, TPS, HD_B]), ALU.mult))
                half_set = E.done("dve", dve.memset(half_neg[:, :], -0.5))
                E.after("pe", loaded, ident_in)
                E.after("pool", tabled, half_set)
                E.after("dve", tabled)
                feat = [sb(s_, f"b_feat{layer}{n}", [P, SEQ])[:, :] for n in range(LANES)]
                work = [sb(s_, f"b_work{layer}{n}", [P, 3, TPS, INNER]) for n in range(LANES)]
                q_t = [sb(s_, f"b_q{layer}{n}", [P, HEADS_B // 2, SEQ]) for n in range(LANES)]
                k_sep = [sb(s_, f"b_k{layer}{n}", [P, 2, HEADS_B // 2, SEQ]) for n in range(LANES)]
                v_sb = [sb(s_, f"b_v{layer}{n}", [P, TPS, INNER]) for n in range(LANES)]
                o_t = [sb(s_, f"b_o{layer}{n}", [P, HEADS_B // 2, SEQ]) for n in range(LANES)]
                small = [sb(s_, f"b_small{layer}{n}", [P, 48]) for n in range(LANES)]
                for n in range(LANES):
                    E.done("dve", dve.memset(feat[n][64:P, 0:1], 0.0))
                    E.done("dve", dve.memset(k_sep[n][64:P, 0, :, :], 0.0))
                    zeroed = E.done("dve", dve.memset(k_sep[n][0:64, 1, :, :], 0.0))

                def shifted_input(lane, b, dst):
                    bank = psum[:, 2 * lane, :]
                    for i in range(TPS):
                        mm = pe.transpose(bank[:, i * P:(i + 1) * P], stream[:, TPS * b + i, :], ident[:, :])
                    turned = E.done("pe", mm)
                    E.after("act", turned)
                    E.done("act", act.activation(dst[0:64, :], bank[0:64, 0:SEQ], ACT.Copy))
                    return E.done("act", act.activation(dst[64:P, 1:SEQ], bank[64:P, 0:SEQ - 1], ACT.Copy))

                def local_task(b):
                    def steps(lane):
                        b0, b1, two = psum[:, 2 * lane, :], psum[:, 2 * lane + 1, :], both(lane)
                        hT, wk_, sm = feat[lane], work[lane], small[lane]
                        x_, t1, t2 = wk_[:, 0, :, :], wk_[:, 1, :, :], wk_[:, 2, :, :]
                        yield stream_ready[TPS * b + TPS - 1], zeroed, lane_free[lane]
                        shifted = shifted_input(lane, b, hT)
                        yield shifted,

                        def project(kind):
                            for i in range(TPS):
                                mm = pe.matmul(two[:, i, :], hT[:, i * P:(i + 1) * P], wqkv[:, kind * INNER:(kind + 1) * INNER],
                                               start=True, stop=True)
                            return E.done("pe", mm)

                        for kind in range(2):
                            produced = project(kind)
                            E.after("act", produced)
                            copied = E.done("act", act.activation(x_, two, ACT.Copy))
                            E.after("pool", copied)
                            squared = E.done("pool", pool.tensor_tensor(t1, x_, x_, ALU.mult))
                            ss, rn = sm[:, 16:32], sm[:, 32:48]
                            E.after("dve", squared)
                            ssed = E.done("dve", dve.tensor_reduce(out=ss, in_=t1.rearrange("p i (h d) -> p (i h) d", d=HD_B),
                                                                   axis=AX.X, op=ALU.add))
                            E.after("dve", ssed)
                            clipped = E.done("dve", dve.tensor_scalar(ss, ss, 1e-24, None, ALU.max))
                            E.after("pool", clipped)
                            inv_norm = E.done("pool", pool.tensor_tensor(rn, ss, half_neg[:, :], ALU.pow))
                            E.after("dve", inv_norm)
                            heads = lambda t: t.rearrange("p i (h d) -> p (i h) d", d=HD_B)
                            normed_ = E.done("dve", dve.tensor_tensor(heads(x_), heads(x_), bc(rn, HD_B), ALU.mult))
                            by_head = lambda t: t.rearrange("p i (h d) -> p i h d", d=HD_B)
                            cos = rope[:, 2 * kind, :, :].unsqueeze(2).broadcast_to([P, TPS, HEADS_B, HD_B])
                            sin = rope[:, 2 * kind + 1, :, :].unsqueeze(2).broadcast_to([P, TPS, HEADS_B, HD_B])
                            E.after("dve", normed_)
                            cosed = E.done("dve", dve.tensor_tensor(by_head(t1), by_head(x_), cos, ALU.mult))
                            E.after("pool", normed_)
                            hh = HD_B // 2
                            pool.tensor_tensor(by_head(t2)[:, :, :, 0:hh], by_head(x_)[:, :, :, hh:], sin[:, :, :, 0:hh], ALU.mult)
                            sined = E.done("pool", pool.tensor_tensor(by_head(t2)[:, :, :, hh:], by_head(x_)[:, :, :, 0:hh],
                                                                      sin[:, :, :, hh:], ALU.mult))
                            E.after("dve", cosed, sined)
                            roped = E.done("dve", dve.tensor_tensor(x_, t1, t2, ALU.add))
                            yield roped,
                            for i in range(TPS):
                                for c in range(4):
                                    mm = pe.transpose(two[:, i, c * P:(c + 1) * P], x_[:, i, c * P:(c + 1) * P], ident[:, :])
                            turned = E.done("pe", mm)
                            E.after("act", turned)
                            by_pair = lambda t: t.rearrange("p c (i t) -> p i c t", i=TPS)
                            source = two.rearrange("p i (c t) -> p i c t", c=4)
                            if kind == 0:
                                copied = E.done("act", act.activation(by_pair(q_t[lane][:, :, :]), source, ACT.Copy))
                            else:
                                for h in range(2):
                                    half = slice(64 * h, 64 * h + 64)
                                    copied = E.done("act", act.activation(by_pair(k_sep[lane][half, h, :, :]), source[half], ACT.Copy))
                            yield copied,
                        produced = project(2)
                        E.after("act", produced)
                        v_ready = E.done("act", act.activation(v_sb[lane][:, :, :], two, ACT.Copy))
                        yield v_ready,
                        flat = lambda n: work[lane][:, n, :, :].rearrange("p i n -> p (i n)")[:, 0:2 * KEYS].rearrange("p (h k) -> p h k", h=2)
                        sc, ex, et = flat(0), flat(1), flat(2)
                        sums = sm[:, 12:16].rearrange("p (i h) -> p i h", i=TPS)
                        for c in range(HEADS_B // 2):
                            halves = yield from soft_scores(
                                lane, lambda h, i: q_t[lane][:, c, i * P:(i + 1) * P], lambda h: k_sep[lane][:, h, c, :],
                                lambda h: band[:, :], 8.0, sc, ex, et, sm, sums, True)
                            yield halves
                            for h in range(2):
                                v_of = lambda i: v_sb[lane][:, i, c * P + 64 * h:c * P + 64 * h + 64]
                                pe.matmul(two[0:64, h, 0:SEQ], v_of(0), et[:, h, 0:SEQ], start=True, stop=False)
                                mm = pe.matmul(two[0:64, h, P:SEQ], v_of(1), et[:, h, SEQ:KEYS], start=False, stop=True)
                            produced = E.done("pe", mm)
                            E.after("act", produced)
                            half0 = E.done("act", act.activation(o_t[lane][0:64, c, :], two[0:64, 0, 0:SEQ], ACT.Copy))
                            E.after("dve", produced)
                            half1 = E.done("dve", dve.tensor_copy(o_t[lane][64:P, c, :], two[0:64, 1, 0:SEQ]))
                            yield half0, half1
                        for i in range(TPS):
                            for c in range(4):
                                mm = pe.matmul(b0[:, i * P:(i + 1) * P], o_t[lane][:, c, i * P:(i + 1) * P], wo[:, c, :],
                                               start=(c == 0), stop=(c == 3))
                        produced = E.done("pe", mm)
                        E.after("dve", produced)
                        here = stream[:, TPS * b:TPS * b + TPS, :]
                        mark = E.done("dve", dve.tensor_tensor(here, here, b0[:, 0:SEQ].rearrange("p (i d) -> p i d", i=TPS), ALU.add))
                        for i in range(TPS):
                            stream_ready[TPS * b + i] = mark
                        lane_free[lane] = mark
                    return steps

                E.in_lanes([local_task(b) for b in range(n_seq)])
                E.barrier()
            debug(2 + 2 * layer, stream)

            with ExitStack() as s_:
                w1 = sb(s_, f"f_w1{layer}", [P, 2 * HID])
                w2 = sb(s_, f"f_w2{layer}", [P, 3, P])
                b1_ = sb(s_, f"f_b1{layer}", [P, 2, 3])
                b2_ = sb(s_, f"f_b2{layer}", [P, P])
                ln_g = sb(s_, f"f_g{layer}", [P, 1])
                ln_b = sb(s_, f"f_b{layer}", [P, 1])
                for dst, src in ((w1[:, :], io["f_w1"][layer]), (w2[:, :, :], io["f_w2"][layer]), (b1_[:, :, :], io["f_b1"][layer]),
                                 (b2_[:, :], io["f_b2"][layer]), (ln_g[:, :], io["f_g"][layer]), (ln_b[:, :], io["f_b"][layer])):
                    loaded = E.dma(f"load_f{layer}", dst, src)
                shifted_tok = sb(s_, f"f_h{layer}", [P, n_tiles, P])
                feat = [sb(s_, f"f_feat{layer}{n}", [P, SEQ])[:, :] for n in range(LANES)]
                gate = [sb(s_, f"f_gate{layer}{n}", [P, 3, SEQ]) for n in range(LANES)]
                for n in range(LANES):
                    zeroed = E.done("dve", dve.memset(feat[n][64:P, 0:1], 0.0))
                copied_back = {}

                def shift_task(b):
                    def steps(lane):
                        b1 = psum[:, 2 * lane + 1, :]
                        yield stream_ready[TPS * b], zeroed, lane_free[lane]
                        shifted = shifted_input(lane, b, feat[lane])
                        yield shifted,
                        for i in range(TPS):
                            mm = pe.transpose(b1[:, i * P:(i + 1) * P], feat[lane][:, i * P:(i + 1) * P], ident[:, :])
                        turned = E.done("pe", mm)
                        E.after("act", turned)
                        mark = E.done("act", act.activation(shifted_tok[:, TPS * b:TPS * b + TPS, :],
                                                            b1[:, 0:SEQ].rearrange("p (i d) -> p i d", i=TPS), ACT.Copy))
                        for i in range(TPS):
                            copied_back[TPS * b + i] = mark
                        lane_free[lane] = mark
                    return steps

                E.in_lanes([shift_task(b) for b in range(n_seq)])
                norm_stats(shifted_tok, copied_back)
                normed = norm_apply(shifted_tok, shifted_tok)
                E.after("pe", loaded)
                E.after("act", loaded)
                E.after("dve", loaded)
                E.after("pool", loaded)
                chunks = [(0, P), (P, P), (2 * P, HID - 2 * P)]

                def ffn_task(b):
                    def steps(lane):
                        b0, b1, two = psum[:, 2 * lane, :], psum[:, 2 * lane + 1, :], both(lane)
                        here = stream[:, TPS * b:TPS * b + TPS, :]
                        yield normed[TPS * b + TPS - 1], lane_free[lane]
                        for i in range(TPS):
                            mm = pe.transpose(b0[:, i * P:(i + 1) * P], shifted_tok[:, TPS * b + i, :], ident[:, :])
                        turned = E.done("pe", mm)
                        E.after("dve", turned)
                        scaled = E.done("dve", dve.tensor_scalar(feat[lane], b0[:, 0:SEQ], ln_g[:, 0:1], ln_b[:, 0:1], ALU.mult, ALU.add))
                        E.after("pool", stream_ready[TPS * b], normed[TPS * b])
                        biased = E.done("pool", pool.tensor_tensor(here, here, b2_[:, :].unsqueeze(1).broadcast_to([P, TPS, P]), ALU.add))
                        yield scaled,
                        used = []
                        for c, (lo, n) in enumerate(chunks):
                            bank = two[:, c % 2, :]
                            for part in range(2):
                                mm = pe.matmul(bank[0:n, part * SEQ:(part + 1) * SEQ], w1[:, part * HID + lo:part * HID + lo + n],
                                               feat[lane][:, :], start=True, stop=True)
                            produced = E.done("pe", mm)
                            E.after("act", produced)
                            g_ = gate[lane][0:n, c, :]
                            gated = E.done("act", act.activation(g_, bank[0:n, SEQ:2 * SEQ], ACT.Gelu, bias=b1_[0:n, 1, c:c + 1]))
                            E.after("dve", gated)
                            used.append(E.done("dve", dve.scalar_tensor_tensor(
                                out=g_, in0=bank[0:n, 0:SEQ], scalar=b1_[0:n, 0, c:c + 1], in1=g_, op0=ALU.add, op1=ALU.mult)))
                            yield used[:-1] if c < 2 else used
                        for i in range(TPS):
                            for c, (lo, n) in enumerate(chunks):
                                mm = pe.matmul(b1[:, i * P:(i + 1) * P], gate[lane][0:n, c, i * P:(i + 1) * P], w2[0:n, c, :],
                                               start=(c == 0), stop=(c == 2))
                        produced = E.done("pe", mm)
                        E.after("dve", produced, biased)
                        mark = E.done("dve", dve.tensor_tensor(here, here, b1[:, 0:SEQ].rearrange("p (i d) -> p i d", i=TPS), ALU.add))
                        for i in range(TPS):
                            stream_ready[TPS * b + i] = mark
                        lane_free[lane] = mark
                    return steps

                E.in_lanes([ffn_task(b) for b in range(n_seq)])
                E.barrier()
            debug(3 + 2 * layer, stream)
        stream_ready = residual_norm(x, stream_ready)
        debug(6, stream)
        E.barrier()

        with ExitStack() as s_:
            wq = sb(s_, "c_wq", [P, QUADS, P])
            wk = sb(s_, "c_wk", [P, QUADS, P])
            wv = sb(s_, "c_wv", [P, P])
            slope = sb(s_, "c_slope", [P, HEADS_A])
            rel = sb(s_, "c_rel", [P, KEYS])
            causal = sb(s_, "c_causal", [P, KEYS])
            bias = sb(s_, "c_bias", [P, HEADS_A, KEYS])
            for dst, src in ((wq[:, :, :], "c_wq"), (wk[:, :, :], "c_wk"), (wv[:, :], "c_wv"), (slope[:, :], "c_slope"),
                             (rel[:, :], "c_rel"), (causal[:, :], "c_causal")):
                loaded = E.dma("load_c", dst, io[src])
            E.after("pe", loaded)
            E.after("dve", loaded)
            for h in range(HEADS_A):
                biases = E.done("dve", dve.scalar_tensor_tensor(out=bias[:, h, :], in0=rel[:, :], scalar=slope[:, h:h + 1],
                                                                in1=causal[:, :], op0=ALU.mult, op1=ALU.add))
            E.after("dve", biases)
            feat = [sb(s_, f"c_feat{n}", [P, SEQ])[:, :] for n in range(LANES)]
            q_t = [sb(s_, f"c_q{n}", [P, SEQ]) for n in range(LANES)]
            k_t = [sb(s_, f"c_k{n}", [P, SEQ]) for n in range(LANES)]
            k_sep = [sb(s_, f"c_ksep{n}", [P, 4, SEQ]) for n in range(LANES)]
            v_wide = [sb(s_, f"c_v{n}", [P, TPS, 4, 32]) for n in range(LANES)]
            work = [sb(s_, f"c_work{n}", [P, 2, 2, KEYS]) for n in range(LANES)]
            exp_t = [sb(s_, f"c_expt{n}", [P, 4, KEYS]) for n in range(LANES)]
            small = [sb(s_, f"c_small{n}", [P, 32]) for n in range(LANES)]
            rows_sb = [sb(s_, f"c_rows{n}", [32, SEQ]) for n in range(LANES)]
            for n in range(LANES):
                zeroed = E.done("dve", dve.memset(v_wide[n][:, :, :, :], 0.0))
            E.after("dve", zeroed)
            E.after("pool", loaded)
            turned_by, written = {}, {}

            def causal_task(b, g):
                def steps(lane):
                    b0, b1, two = psum[:, 2 * lane, :], psum[:, 2 * lane + 1, :], both(lane)
                    sm = small[lane]
                    yield stream_ready[TPS * b + TPS - 1], lane_free[lane]
                    turned, copied = transposed_input(lane, b, feat[lane])
                    turned_by[b, g] = turned
                    yield copied,
                    pe.matmul(b0[:, 0:SEQ], wq[:, g, :], feat[lane], start=True, stop=True)
                    pe.matmul(b0[:, SEQ:2 * SEQ], wk[:, g, :], feat[lane], start=True, stop=True)
                    for i in range(TPS):
                        mm = pe.matmul(b1[:, P * i:P * (i + 1)], feat[lane][:, i * P:(i + 1) * P], wv[:, :], start=True, stop=True)
                    projected = E.done("pe", mm)
                    E.after("act", projected)
                    E.done("act", act.activation(q_t[lane][:, :], b0[:, 0:SEQ], ACT.Copy, scale=1.0 / math.sqrt(P)))
                    qk_ready = E.done("act", act.activation(k_t[lane][:, :], b0[:, SEQ:2 * SEQ], ACT.Copy))
                    sep_ready = separate(quad_mask, k_sep[lane][:, :, :], k_t[lane][:, :], qk_ready)
                    E.after("dve", projected)
                    for i in range(TPS):
                        cols = slice(P * i + 32 * g, P * i + 32 * g + 32)
                        v_ready = E.done("dve", dve.tensor_copy(diagonal(v_wide[lane][:, i, :, :]),
                                                                b1[:, cols].rearrange("p (j d) -> p j d", j=4)))
                    yield sep_ready, v_ready
                    sums, inv = sm[:, 12:20].rearrange("p (i j) -> p i j", i=TPS), sm[:, 20:28]
                    for c in range(2):
                        halves = yield from soft_scores(
                            lane, lambda h, i: q_t[lane][:, i * P:(i + 1) * P], lambda h: k_sep[lane][:, 2 * c + h, :],
                            lambda h: bias[:, 4 * g + 2 * c + h, :], 1.0, work[lane][:, 0, :, :], work[lane][:, 1, :, :],
                            exp_t[lane][:, 2 * c:2 * c + 2, :], sm, sums[:, :, 2 * c:2 * c + 2], False)
                        yield halves
                    for j in range(4):
                        pe.matmul(b0[0:32, 0:SEQ], v_wide[lane][:, 0, j, :], exp_t[lane][:, j, 0:SEQ], start=(j == 0), stop=False)
                        mm = pe.matmul(b0[0:32, P:SEQ], v_wide[lane][:, 1, j, :], exp_t[lane][:, j, SEQ:KEYS], start=False, stop=(j == 3))
                    produced = E.done("pe", mm)
                    E.after("act", produced)
                    x_rows = E.done("act", act.activation(rows_sb[lane][:, :], b0[0:32, 0:SEQ], ACT.Copy))
                    inv_ready = E.done("dve", dve.reciprocal(inv, sm[:, 12:20]))
                    yield x_rows,
                    for i in range(TPS):
                        mm = pe.transpose(b1[:, 32 * i:32 * i + 32], rows_sb[lane][:, i * P:(i + 1) * P], ident[0:32, 0:32])
                    produced = E.done("pe", mm)
                    E.after("dve", produced, inv_ready, [turned_by[b, q] for q in range(QUADS)])
                    out_view = stream[:, TPS * b:TPS * b + TPS, 32 * g:32 * g + 32].rearrange("p i (j d) -> p i j d", d=HD_A)
                    lane_free[lane] = written[b, g] = E.done("dve", dve.tensor_tensor(
                        out_view, b1[:, 0:64].rearrange("p (i j d) -> p i j d", i=TPS, j=4),
                        bc(inv.rearrange("p (i j) -> p i j", i=TPS), HD_A), ALU.mult))
                return steps

            E.in_lanes([causal_task(b, g) for b in range(n_seq) for g in range(QUADS)])
            block_out = [[written[t // TPS, g] for g in range(QUADS)] for t in range(n_tiles)]
            E.barrier()
        debug(7, stream)
        stream_ready = residual_norm(x, block_out)
        debug(8, stream)
        E.barrier()

        with ExitStack() as s_:
            wg = sb(s_, "d_wg", [P, EXPERTS])
            bg = sb(s_, "d_bg", [P, EXPERTS])
            w1 = sb(s_, "d_w1", [P, EXPERTS * RANK])
            w2 = sb(s_, "d_w2", [P, EXPERTS * RANK // P, P])
            order = sb(s_, "d_order", [P, EXPERTS])
            for dst, src in ((wg[:, :], "d_wg"), (bg[:, :], "d_bg"), (w1[:, :], "d_w1"), (w2[:, :, :], "d_w2"), (order[:, :], "d_order")):
                loaded = E.dma("load_d", dst, io[src])
            E.after("pe", loaded)
            E.after("dve", loaded)
            feat = sb(s_, "d_feat", [P, n_seq, SEQ])
            logits = sb(s_, "d_logits", [P, n_tiles, EXPERTS])
            gates = sb(s_, "d_gates", [P, n_tiles, EXPERTS])
            pick = [sb(s_, f"d_pick{n}", [P, n_tiles, EXPERTS]) for n in range(3)]
            best = [sb(s_, f"d_best{n}", [P, n_tiles]) for n in range(5)]
            hid = [sb(s_, f"d_hid{n}", [P, TPS, EXPERTS * RANK]) for n in range(LANES)]
            hid_t = [sb(s_, f"d_hidt{n}", [P, TPS, EXPERTS * RANK]) for n in range(LANES)]
            logit_marks = []

            def logit_task(b):
                def steps(lane):
                    b1 = psum[:, 2 * lane + 1, :]
                    yield stream_ready[TPS * b + TPS - 1], lane_free[lane]
                    turned, copied = transposed_input(lane, b, feat[:, b, :])
                    yield copied,
                    for i in range(TPS):
                        mm = pe.matmul(b1[:, EXPERTS * i:EXPERTS * (i + 1)], feat[:, b, i * P:(i + 1) * P], wg[:, :], start=True, stop=True)
                    produced = E.done("pe", mm)
                    E.after("dve", produced)
                    mark = E.done("dve", dve.tensor_tensor(logits[:, TPS * b:TPS * b + TPS, :],
                                                           b1[:, 0:TPS * EXPERTS].rearrange("p (i e) -> p i e", i=TPS),
                                                           bg[:, :].unsqueeze(1).broadcast_to([P, TPS, EXPERTS]), ALU.add))
                    logit_marks.append(mark)
                    lane_free[lane] = mark
                return steps

            E.in_lanes([logit_task(b) for b in range(n_seq)])
            v1, v2, m_, gap, e_ = (t[:, :] for t in best)
            hot1, hot2, rest = (t[:, :, :] for t in pick)
            order_all = order[:, :].unsqueeze(1).broadcast_to([P, n_tiles, EXPERTS])

            def step(instruction):
                mark = E.done("dve", instruction)
                E.after("dve", mark)
                return mark

            def one_hot(dst, values, v):
                step(dve.tensor_tensor(dst, values, bc(v, EXPERTS), ALU.is_equal))
                step(dve.tensor_tensor(dst, dst, order_all, ALU.mult))
                step(dve.tensor_reduce(out=m_, in_=dst, axis=AX.X, op=ALU.max))
                step(dve.tensor_tensor(dst, dst, bc(m_, EXPERTS), ALU.is_equal))

            E.after("dve", logit_marks[-1])
            step(dve.tensor_reduce(out=v1, in_=logits[:, :, :], axis=AX.X, op=ALU.max))
            one_hot(hot1, logits[:, :, :], v1)
            step(dve.scalar_tensor_tensor(out=rest, in0=hot1, scalar=LOWEST, in1=logits[:, :, :], op0=ALU.mult, op1=ALU.add))
            step(dve.tensor_reduce(out=v2, in_=rest, axis=AX.X, op=ALU.max))
            one_hot(hot2, rest, v2)
            gap_ready = step(dve.tensor_tensor(gap, v2, v1, ALU.subtract))
            E.after("act", gap_ready)
            e_ready = E.done("act", act.activation(e_, gap, ACT.Exp))
            E.after("dve", e_ready)
            step(dve.tensor_scalar(m_, e_, 1.0, None, ALU.add))
            step(dve.reciprocal(v1, m_))
            step(dve.tensor_tensor(v2, e_, v1, ALU.mult))
            step(dve.tensor_tensor(hot1, hot1, bc(v1, EXPERTS), ALU.mult))
            step(dve.tensor_tensor(hot2, hot2, bc(v2, EXPERTS), ALU.mult))
            gates_ready = step(dve.tensor_tensor(gates[:, :, :], hot1, hot2, ALU.add))
            E.after("pool", gates_ready)
            d_out = {}

            def expert_task(b):
                def steps(lane):
                    b0, two = psum[:, 2 * lane, :], both(lane)
                    yield lane_free[lane],
                    for i in range(TPS):
                        mm = pe.matmul(two[:, i, :], feat[:, b, i * P:(i + 1) * P], w1[:, :], start=True, stop=True)
                    produced = E.done("pe", mm)
                    E.after("act", produced)
                    gelued = E.done("act", act.activation(hid[lane][:, :, :], two, ACT.Gelu))
                    name, engine = (("dve", dve), ("pool", pool))[b % 4 == 3]
                    E.after(name, gelued)
                    by_e = hid[lane][:, :, :].rearrange("p i (e r) -> p i e r", r=RANK)
                    weighted = E.done(name, engine.tensor_tensor(by_e, by_e, bc(gates[:, TPS * b:TPS * b + TPS, :], RANK), ALU.mult))
                    yield weighted,
                    for i in range(TPS):
                        for c in range(4):
                            mm = pe.transpose(two[:, i, c * P:(c + 1) * P], hid[lane][:, i, c * P:(c + 1) * P], ident[:, :])
                    turned = E.done("pe", mm)
                    E.after("dve", turned)
                    half1 = E.done("dve", dve.tensor_copy(hid_t[lane][:, 1, :], two[:, 1, :]))
                    E.after("act", turned)
                    half0 = E.done("act", act.activation(hid_t[lane][:, 0, :], two[:, 0, :], ACT.Copy))
                    yield half0, half1,
                    for i in range(TPS):
                        for c in range(4):
                            mm = pe.matmul(b0[:, i * P:(i + 1) * P], hid_t[lane][:, i, c * P:(c + 1) * P], w2[:, c, :],
                                           start=(c == 0), stop=(c == 3))
                    produced = E.done("pe", mm)
                    E.after("dve", produced)
                    mark = E.done("dve", dve.tensor_scalar(stream[:, TPS * b:TPS * b + TPS, :],
                                                           b0[:, 0:SEQ].rearrange("p (i d) -> p i d", i=TPS), 2.0, None, ALU.mult))
                    for i in range(TPS):
                        d_out[TPS * b + i] = mark
                    lane_free[lane] = mark
                return steps

            E.in_lanes([expert_task(b) for b in range(n_seq)])
        debug(9, stream)
        added = residual_norm(x, d_out, final=True)
        for g in range(0, n_tiles, TG):
            E.after("sp", added[g])
            stored = E.dma("store", out_dram[:, g:g + TG, :], x[:, g:g + TG, :])
        E.after("sp", stored)


def layouts(inputs):
    a = {k: np.asarray(v) for k, v in inputs.items()}
    f = np.float32

    def quads(w):
        out = np.zeros((w.shape[0], QUADS, 4, 32), f)
        out[:, :, :, :HD_A] = w.reshape(w.shape[0], QUADS, 4, HD_A)
        return out.reshape(w.shape[0], QUADS, P)

    def rows(v):
        return np.ascontiguousarray(np.broadcast_to(v, (P, *v.shape)))

    t = {"x": a["L0_attn_x"], "ident": np.eye(P, dtype=f)}
    t["a_wq"], t["a_wk"] = quads(a["L0_attn_Wq"].T), quads(a["L0_attn_Wk"].T)
    t["a_wv"] = a["L0_attn_Wv"].T
    t["a_bq"] = quads(a["L0_attn_bq"][None])[0].T
    t["a_bk"] = quads(a["L0_attn_bk"][None])[0].T
    t["a_bv"] = rows(a["L0_attn_bv"])
    t["quad_mask"] = np.repeat(np.eye(4, dtype=f), 32, axis=0)
    t["b_wqkv"] = a["L0_ffn_wqkv"]
    t["b_wo"] = a["L0_ffn_wo"].reshape(2, INNER // P, P, P).transpose(0, 2, 1, 3)
    half = np.arange(0, HD_B, 2, dtype=f)
    inv_freq = (1.0 / f(10000.0) ** (half / f(HD_B))).astype(f)
    pos = np.arange(SEQ, dtype=f)
    freqs = pos[:, None] * inv_freq[None, :]
    freqs = np.concatenate([freqs, freqs], -1)
    base = (half + f(0.4 * HD_B)) / f(1.4 * HD_B)
    power = (pos - SEQ // 2) / f(WIN // 2)
    scale = base[None, :] ** power[:, None]
    scale = np.concatenate([scale, scale], -1).astype(f)
    sign = np.concatenate([-np.ones(HD_B // 2), np.ones(HD_B // 2)]).astype(f)
    cos, sin = np.cos(freqs), np.sin(freqs) * sign
    rope = np.stack([cos * scale, sin * scale, cos / scale, sin / scale])
    t["b_rope"] = rope.reshape(4, TPS, P, HD_B).transpose(2, 0, 1, 3).astype(f)

    def rotated(v):
        return np.concatenate([v[..., HD_B // 2:], v[..., :HD_B // 2]], -1)

    qs, ks = a["L0_ffn_q_scale"], a["L0_ffn_k_scale"]
    gain = np.stack([qs, rotated(qs), ks, rotated(ks)], 1)
    t["b_gain"] = np.broadcast_to(gain[:, None], (2, P, 4, HD_B))
    q = np.arange(P)[:, None]
    delta = np.concatenate([q - np.arange(P)[None], q + P - np.arange(SEQ)[None]], 1)
    t["b_band"] = np.where((delta < 0) | (delta > WIN), MASKED, 0.0).astype(f)
    t["f_w1"] = a["L0_ffn_w1"]
    w2 = np.zeros((2, 3 * P, P), f)
    w2[:, :HID] = a["L0_ffn_w2"]
    t["f_w2"] = w2.reshape(2, 3, P, P).transpose(0, 2, 1, 3)
    b1 = np.zeros((2, 2, 3 * P), f)
    b1[:, :, :HID] = a["L0_ffn_b1"].reshape(2, 2, HID)
    t["f_b1"] = b1.reshape(2, 2, 3, P).transpose(0, 3, 1, 2)
    t["f_b2"] = np.broadcast_to(a["L0_ffn_b2"][:, None], (2, P, P))
    t["f_g"], t["f_b"] = a["L0_ffn_ln_g"][:, :, None], a["L0_ffn_ln_b"][:, :, None]
    w = a["L1_attn_W_kqv"]
    t["c_wk"], t["c_wq"], t["c_wv"] = quads(w[:, 0:P]), quads(w[:, P:2 * P]), w[:, 2 * P:]
    t["c_slope"] = rows(a["L1_attn_m"].reshape(HEADS_A))
    t["c_rel"] = (-delta).astype(f)
    t["c_causal"] = np.where(delta < 0, MASKED, 0.0).astype(f)
    t["d_wg"], t["d_bg"] = a["L1_ffn_Wg"].T, rows(a["L1_ffn_bg"])
    t["d_w1"] = a["L1_ffn_W1"].reshape(EXPERTS * RANK, P).T
    t["d_w2"] = a["L1_ffn_W2"].transpose(0, 2, 1).reshape(4, P, P).transpose(1, 0, 2)
    t["d_order"] = rows(np.arange(EXPERTS, 0, -1).astype(f))
    return {k: np.ascontiguousarray(v) for k, v in t.items()}


def kernel(**inputs):
    import concourse.bacc as bacc
    from concourse.bass_utils import run_bass_kernel_spmd

    arrays = layouts(inputs)
    nc = bacc.Bacc("TRN2", target_bir_lowering=False, num_devices=1)
    io = {n: nc.dram_tensor(f"in_{n}", v.shape, mybir.dt.from_np(v.dtype), kind="ExternalInput").ap() for n, v in arrays.items()}
    io["out"] = nc.dram_tensor("out", arrays["x"].shape, F32, kind="ExternalOutput").ap()
    bass_four_blocks(nc, io)
    run = run_bass_kernel_spmd(nc, [{f"in_{n}": v for n, v in arrays.items()}], core_ids=[0])
    return run.results[0]["out"]
```

```python
import math
from contextlib import ExitStack

import numpy as np
import concourse.bass as bass
from concourse import mybir

F32 = mybir.dt.float32
ALU = mybir.AluOpType
ACT = mybir.ActivationFunctionType
AX = mybir.AxisListType

P = 128
SEQ = 256
TPS = SEQ // P
LANES = 4
BANK = 512
LN_EPS = 1e-5
LOWEST = -3.0e38
MASKED = -1.0e30

HEADS_A, HD_A = 16, 8
QUADS = HEADS_A // 4
ITERS = 6
HEADS_B, HD_B, WIN = 8, 64, 64
INNER = HEADS_B * HD_B
HID = 341
EXPERTS, RANK = 8, 64
KEYS = 3 * P


class Queue:

    FIXED = {"pe": 3.0, "act": 90.0, "dve": 70.0, "pool": 70.0, "sp": 50.0}
    PER_COLUMN = {"act": 0.83, "dve": 1.04, "pool": 2.2}

    def __init__(self, name, engine):
        self.name, self.engine, self.clock = name, engine, 0.0
        self.wait_ge, self.dma_start = engine.wait_ge, engine.dma_start

    def took(self, instruction, columns):
        self.clock += self.FIXED[self.name] + self.PER_COLUMN[self.name] * columns
        return instruction

    def matmul(self, out, lhsT, rhs, **kw):
        m, n = lhsT.free_size(), rhs.free_size()
        self.clock += self.FIXED["pe"] + 4 * (n / 2.4 if n >= 96 else max(n / 2.4, m / 1.2))
        return self.engine.matmul(out, lhsT, rhs, **kw)

    def transpose(self, out, in_, identity):
        self.clock += self.FIXED["pe"] + in_.free_size() / 1.2
        return self.engine.transpose(out, in_, identity)

    def activation(self, out, in_, func, **kw):
        extra = 186 if "accum_out" in kw else 0
        return self.took(self.engine.activation(out, in_, func, **kw), extra + out.free_size())

    def memset(self, out, value):
        return self.took(self.engine.memset(out, value), out.free_size())

    def tensor_copy(self, out, in_):
        return self.took(self.engine.tensor_copy(out, in_), out.free_size())

    def reciprocal(self, out, in_):
        return self.took(self.engine.reciprocal(out, in_), out.free_size())

    def tensor_tensor(self, out, in0, in1, op):
        slow = 70 if op == ALU.pow else 1
        return self.took(self.engine.tensor_tensor(out, in0, in1, op), slow * out.free_size())

    def tensor_scalar(self, out, in_, scalar1, scalar2, *ops):
        return self.took(self.engine.tensor_scalar(out, in_, scalar1, scalar2, *ops), out.free_size() / 2)

    def scalar_tensor_tensor(self, out, **kw):
        return self.took(self.engine.scalar_tensor_tensor(out=out, **kw), out.free_size())

    def tensor_tensor_reduce(self, out, **kw):
        return self.took(self.engine.tensor_tensor_reduce(out=out, **kw), out.free_size())

    def tensor_reduce(self, out, in_, **kw):
        return self.took(self.engine.tensor_reduce(out=out, in_=in_, **kw), in_.free_size())

    def bn_stats(self, out, in_):
        return self.took(self.engine.bn_stats(out, in_), in_.free_size())

    def bn_aggr(self, out, in_):
        return self.took(self.engine.bn_aggr(out, in_), in_.free_size())


class Engines:

    LATENCY = 250.0

    def __init__(self, nc, ctx):
        self.nc, self.ctx = nc, ctx
        self.queues = {n: Queue(n, e) for n, e in (("pe", nc.tensor), ("act", nc.scalar), ("dve", nc.vector),
                                                   ("pool", nc.gpsimd), ("sp", nc.sync))}
        self.sems = {n: ctx.enter_context(nc.semaphore(f"done_{n}")) for n in self.queues if n != "sp"}
        self.count = dict.fromkeys(self.sems, 0)
        self.seen = {}
        self.end = {}

    def done(self, name, instruction):
        instruction.then_inc(self.sems[name], 1)
        self.count[name] += 1
        mark = (name, self.count[name])
        self.end[mark] = self.queues[name].clock + self.LATENCY
        return mark

    def ready(self, marks):
        if isinstance(marks, list):
            return max((self.ready(m) for m in marks), default=0.0)
        return self.end.get(marks, 0.0)

    def after(self, name, *marks):
        queue = self.queues[name]
        for mark in marks:
            if mark is None:
                continue
            if isinstance(mark, list):
                self.after(name, *mark)
                continue
            queue.clock = max(queue.clock, self.ready(mark))
            source, value = mark
            if self.seen.get((name, source), 0) < value:
                queue.wait_ge(self.sems[source], value)
                self.seen[(name, source)] = value

    def dma(self, group, out, in_):
        if group not in self.sems:
            self.sems[group] = self.ctx.enter_context(self.nc.semaphore(group))
            self.count[group] = 0
        self.queues["sp"].dma_start(out, in_).then_inc(self.sems[group], 16)
        self.count[group] += 16
        return (group, self.count[group])

    def barrier(self):
        marks = [(n, self.count[n]) for n in self.queues if self.count.get(n)]
        for name in self.queues:
            self.after(name, marks)

    def in_lanes(self, tasks):
        queues = [list(tasks[n::LANES]) for n in range(LANES)]
        running, marks, since, turn = [None] * LANES, [[]] * LANES, [0] * LANES, 0
        engine = ["pe"] * LANES

        def take(lane):
            yielded = list(next(running[lane]))
            engine[lane] = yielded.pop(0) if isinstance(yielded[0], str) else "pe"
            marks[lane] = yielded

        def advance(lane):
            if running[lane] is not None:
                try:
                    take(lane)
                    return
                except StopIteration:
                    running[lane] = None
            if queues[lane]:
                running[lane] = queues[lane].pop(0)(lane)
                take(lane)

        for lane in range(LANES):
            advance(lane)
        while any(r is not None for r in running):
            lane = min((n for n in range(LANES) if running[n] is not None),
                       key=lambda n: (max(self.queues[engine[n]].clock, self.ready(marks[n])), since[n]))
            self.after(engine[lane], *marks[lane])
            turn += 1
            since[lane] = turn
            advance(lane)


def bc(ap, width):
    return ap.unsqueeze(len(ap.shape)).broadcast_to([*ap.shape, width])


def bass_four_blocks(nc, io):
    n_seq = io["x"].shape[0]
    n_tiles = n_seq * TPS
    top = ExitStack()
    with top:
        E = Engines(nc, top)
        pe, act, dve, pool = (E.queues[n] for n in ("pe", "act", "dve", "pool"))

        def sb(ctx, name, shape, dt=F32):
            return ctx.enter_context(nc.sbuf_tensor(name, shape, dt))

        psum = top.enter_context(nc.psum_tensor("psum", [P, 2 * LANES, BANK], F32))

        stream = sb(top, "stream", [P, n_tiles, P])
        ident = sb(top, "ident", [P, P])
        ones = sb(top, "ones", [P, P])
        stats = sb(top, "stats", [P, n_tiles, 6])
        moments = sb(top, "moments", [P, n_tiles, 2])
        deviation = sb(top, "deviation", [P, n_tiles])
        rstd = sb(top, "rstd", [P, n_tiles])
        eps = sb(top, "eps", [P, 1])
        quad_mask = sb(top, "quad_mask", [P, 4])
        ident_in = E.dma("load_ident", ident[:, :], io["ident"])
        ones_set = E.done("dve", dve.memset(ones[:, :], 1.0))
        eps_set = E.done("dve", dve.memset(eps[:, :], LN_EPS))
        x_dram = io["x"].rearrange("b (i p) d -> p (b i) d", p=P)
        out_dram = io["out"].rearrange("b (i p) d -> p (b i) d", p=P)
        TG = min(8, n_tiles)

        def norm_stats(src, ready):
            for t in range(n_tiles):
                E.after("dve", ready[t])
                last = E.done("dve", dve.bn_stats(stats[:, t, :], src[:, t, :]))
            E.after("dve", last)
            for t in range(n_tiles):
                last = E.done("dve", dve.bn_aggr(moments[:, t, :], stats[:, t, :]))
            E.after("act", last, eps_set)
            root = E.done("act", act.activation(deviation[:, :], moments[:, :, 1], ACT.Sqrt, bias=eps[:, 0:1]))
            E.after("dve", root)
            ready_rstd = E.done("dve", dve.reciprocal(rstd[:, :], deviation[:, :]))
            E.after("dve", ready_rstd)
            return ready_rstd

        def norm_apply(dst, src):
            return [E.done("dve", dve.tensor_scalar(dst[:, t, :], src[:, t, :], moments[:, t, 0:1],
                                                    rstd[:, t:t + 1], ALU.subtract, ALU.mult))
                    for t in range(n_tiles)]

        def both(lane):
            return psum[:, 2 * lane:2 * lane + 2, :]

        def separate(mask, dst, src, ready):
            n = src.shape[1]
            E.after("pool", ready)
            return E.done("pool", pool.tensor_tensor(dst, src.unsqueeze(1).broadcast_to([P, 4, n]), bc(mask[:, :], n), ALU.mult))

        def diagonal(t):
            flat = t.rearrange("p j c -> p (j c)")
            return bass.AP(flat.tensor, flat.offset, [flat.ap[0], [32 + HD_A, 4], [1, HD_A]])

        lane_free = [None] * LANES

        def transposed_input(lane, b, dst):
            bank = psum[:, 2 * lane, :]
            for i in range(TPS):
                mm = pe.transpose(bank[:, i * P:(i + 1) * P], stream[:, TPS * b + i, :], ident[:, :])
            turned = E.done("pe", mm)
            yield "act", turned
            return turned, E.done("act", act.activation(dst, bank[:, 0:SEQ], ACT.Copy))

        with ExitStack() as a:
            wq = sb(a, "a_wq", [P, QUADS, P])
            wk = sb(a, "a_wk", [P, QUADS, P])
            wv = sb(a, "a_wv", [P, P])
            bq = sb(a, "a_bq", [P, QUADS])
            bk = sb(a, "a_bk", [P, QUADS])
            bv = sb(a, "a_bv", [P, P])
            for dst, src in ((wq[:, :, :], "a_wq"), (wk[:, :, :], "a_wk"), (wv[:, :], "a_wv"),
                             (bq[:, :], "a_bq"), (bk[:, :], "a_bk"), (bv[:, :], "a_bv"),
                             (quad_mask[:, :], "quad_mask")):
                loaded = E.dma("load_a", dst, io[src])
            kern2 = sb(a, "kern2", [P, n_seq * HEADS_A, P])
            colsum = sb(a, "colsum", [1, n_seq * QUADS])
            inv_c = sb(a, "inv_c", [P, 1])
            peak_one = sb(a, "peak_one", [1, 1])
            raw = [sb(a, f"a_raw{n}", [P, 8, P]) for n in range(LANES)]
            turn = [sb(a, f"a_turn{n}", [P, 8 * (P + HD_A)]) for n in range(LANES)]
            feat = [t[:, 4 * P:4 * P + SEQ] for t in turn]
            state = [sb(a, f"a_state{n}", [P, 4, P + HD_A]) for n in range(LANES)]
            q_t = [sb(a, f"a_q{n}", [P, SEQ]) for n in range(LANES)]
            k_lm = [sb(a, f"a_klm{n}", [P, P]) for n in range(LANES)]
            small = [sb(a, f"a_small{n}", [P, 48]) for n in range(LANES)]
            apart = [sb(a, f"a_apart{n}", [P, TPS, 4, 32]) for n in range(LANES)]
            for n in range(LANES):
                apart_zero = E.done("dve", dve.memset(apart[n][:, :, :, :], 0.0))

            MW = P + HD_A

            x_ready = []
            for g in range(0, n_tiles, TG):
                x_ready += [E.dma(f"load_x{g}", stream[:, g:g + TG, :], x_dram[:, g:g + TG, :])] * TG
            norm_stats(stream, x_ready)
            normed = norm_apply(stream, stream)

            root_scale = 1.0 / math.sqrt(math.sqrt(HD_A))
            E.after("dve", loaded)
            dve.tensor_scalar(bq[:, :], bq[:, :], root_scale, None, ALU.mult)
            scaled_bias = E.done("dve", dve.tensor_scalar(bk[:, :], bk[:, :], root_scale, None, ALU.mult))
            E.after("act", scaled_bias)
            E.after("pool", loaded)

            def softmax_rows(lane, banks, n_rows, width, scale, dst, maxes, negs, sums, scored):
                yield "dve", scored
                peaked = E.done("dve", dve.tensor_reduce(out=maxes, in_=banks, axis=AX.X, op=ALU.max))
                E.after("dve", peaked)
                negated = E.done("dve", dve.tensor_scalar(negs, maxes, -scale, None, ALU.mult))
                yield "act", negated
                for r in range(n_rows):
                    mark = E.done("act", act.activation(dst[:, r, :], banks[:, r, :], ACT.Exp, bias=negs[:, r:r + 1],
                                                        scale=scale, accum_out=sums[:, r:r + 1]))
                return mark

            def kernel2_task(b, g):
                def steps(lane):
                    b0, b1 = psum[:, 2 * lane, :], psum[:, 2 * lane + 1, :]
                    lm = raw[lane][:, 0, :]
                    q_lm, kk_lm = raw[lane][:, 1, :], raw[lane][:, 2, :]
                    expd = turn[lane][:, 0:4 * P].rearrange("p (j m) -> p j m", j=4)
                    sm = small[lane]
                    maxes, negs, sums, inv = sm[:, 0:4], sm[:, 4:8], sm[:, 8:12], sm[:, 12:16]
                    yield normed[TPS * b + TPS - 1], lane_free[lane]
                    turned, copied = yield from transposed_input(lane, b, feat[lane])
                    yield "dve", copied
                    pairs = feat[lane].rearrange("p (m s) -> p m s", s=2)
                    summed = E.done("dve", dve.tensor_tensor(lm, pairs[:, :, 0], pairs[:, :, 1], ALU.add))
                    yield summed,
                    pe.matmul(b0[:, 0:P], wq[:, g, :], lm, start=True, stop=True)
                    projected = E.done("pe", pe.matmul(b0[:, P:2 * P], wk[:, g, :], lm, start=True, stop=True))
                    yield "act", projected
                    E.done("act", act.activation(q_lm, b0[:, 0:P], ACT.Identity, bias=bq[:, g:g + 1], scale=0.5 * root_scale))
                    kk_ready = E.done("act", act.activation(kk_lm, b0[:, P:2 * P], ACT.Identity, bias=bk[:, g:g + 1], scale=0.5 * root_scale))
                    kk_sep = raw[lane][:, 4:8, :]
                    ready = separate(quad_mask, kk_sep, kk_lm, kk_ready)
                    yield kk_ready, ready,
                    scored = E.done("pe", pe.matmul(b1, q_lm, kk_sep, start=True, stop=True))
                    scores = b1.rearrange("p (j m) -> p j m", j=4)
                    expd_all = yield from softmax_rows(lane, scores, 4, P, 1.0, expd, maxes, negs, sums, scored)
                    yield "dve", expd_all
                    inverted = E.done("dve", dve.reciprocal(inv, sums))
                    E.after("dve", inverted)
                    h0 = HEADS_A * b + 4 * g
                    normalized = E.done("dve", dve.tensor_tensor(kern2[:, h0:h0 + 4, :], expd, bc(inv, P), ALU.mult))
                    yield normalized,
                    sums_ready = E.done("pe", pe.matmul(b0[0:1, :], ones[:, 0:1], kern2[:, h0:h0 + 4, :], start=True, stop=True))
                    yield "dve", sums_ready
                    n = QUADS * b + g
                    lane_free[lane] = last_colsum[0] = E.done("dve", dve.tensor_reduce(out=colsum[:, n:n + 1], in_=b0[0:1, :], axis=AX.X, op=ALU.max))
                return steps

            last_colsum = [None]
            E.in_lanes([kernel2_task(b, g) for b in range(n_seq) for g in range(QUADS)])

            E.after("dve", last_colsum[0])
            peaked = E.done("dve", dve.tensor_reduce(out=peak_one[:, :], in_=colsum[:, :], axis=AX.X, op=ALU.max))
            E.barrier()
            spread = E.done("pe", pe.matmul(psum[:, 1, 0:1], ones[0:1, :], peak_one[:, :], start=True, stop=True))
            E.after("dve", spread)
            c_ready = E.done("dve", dve.reciprocal(inv_c[:, :], psum[:, 1, 0:1]))
            E.barrier()

            BETA = 2.75 / 13.0
            turned_by = {}

            def nystrom_task(b, g):
                def steps(lane):
                    b0, b1, two = psum[:, 2 * lane, :], psum[:, 2 * lane + 1, :], both(lane)
                    st, sm = state[lane], small[lane]
                    halves = lambda bank: bank.rearrange("p (j m) -> p j m", j=4)
                    k_t = st[:, :, :].rearrange("p j c -> p (j c)")[:, 0:SEQ]
                    q_lm = st[:, :, :].rearrange("p j c -> p (j c)")[:, SEQ:SEQ + P]
                    v_wide = apart[lane][:, :, :, :]
                    z_wide, w_wide = apart[lane][:, 0, :, :], apart[lane][:, 1, :, :]
                    rows_ = raw[lane][0:32, 4:6, :].rearrange("p r m -> p (r m)")
                    h0 = HEADS_A * b + 4 * g
                    head = lambda j: kern2[:, h0 + j, :]
                    yield lane_free[lane],
                    turned, copied = yield from transposed_input(lane, b, feat[lane])
                    turned_by[b, g] = turned
                    yield copied,
                    pe.matmul(b0[:, 0:SEQ], wq[:, g, :], feat[lane], start=True, stop=True)
                    pe.matmul(b0[:, SEQ:2 * SEQ], wk[:, g, :], feat[lane], start=True, stop=True)
                    for i in range(TPS):
                        mm = pe.matmul(b1[:, P * i:P * (i + 1)], feat[lane][:, i * P:(i + 1) * P], wv[:, :], start=True, stop=True)
                    projected = E.done("pe", mm)
                    yield "act", projected
                    E.done("act", act.activation(q_t[lane][:, :], b0[:, 0:SEQ], ACT.Identity, bias=bq[:, g:g + 1], scale=root_scale))
                    qk_ready = E.done("act", act.activation(k_t, b0[:, SEQ:2 * SEQ], ACT.Identity, bias=bk[:, g:g + 1], scale=root_scale))
                    E.after("dve", projected)
                    for i in range(TPS):
                        cols = slice(P * i + 32 * g, P * i + 32 * g + 32)
                        v_ready = E.done("dve", dve.tensor_tensor(
                            diagonal(v_wide[:, i, :, :]), b1[:, cols].rearrange("p (j d) -> p j d", j=4),
                            bv[:, 32 * g:32 * g + 32].rearrange("p (j d) -> p j d", j=4), ALU.add))
                    yield "dve", qk_ready
                    q2 = q_t[lane][:, :].rearrange("p (m s) -> p m s", s=2)
                    k2 = k_t.rearrange("p (m s) -> p m s", s=2)
                    dve.tensor_tensor(q_lm, q2[:, :, 0], q2[:, :, 1], ALU.add)
                    lm_ready = E.done("dve", dve.tensor_tensor(k_lm[lane][:, :], k2[:, :, 0], k2[:, :, 1], ALU.add))
                    q_sep = turn[lane][:, 0:4 * P].rearrange("p (j m) -> p j m", j=4)
                    sep_ready = separate(quad_mask, q_sep, q_lm, lm_ready)
                    yield sep_ready,
                    for j in range(4):
                        mm = pe.matmul(two[:, j // 2, SEQ * (j % 2):SEQ * (j % 2) + SEQ], q_sep[:, j, :], k_t,
                                       start=True, stop=True)
                    scored = E.done("pe", mm)
                    maxes, negs, sums3, inv3 = sm[:, 0:4], sm[:, 4:8], sm[:, 8:12], sm[:, 12:16]
                    expd3 = raw[lane][:, :, :].rearrange("p (j i) m -> p j (i m)", i=TPS)
                    exped = yield from softmax_rows(lane, two.rearrange("p k (j m) -> p (k j) m", j=2), 4, SEQ, 0.5, expd3,
                                         maxes, negs, sums3, scored)
                    yield "dve", exped
                    inv3_ready = E.done("dve", dve.reciprocal(inv3, sums3))
                    yield exped,
                    for i in range(TPS):
                        for j in range(4):
                            mm = pe.transpose(two[:, i, j * P:(j + 1) * P], raw[lane][:, TPS * j + i, :], ident[:, :])
                    turned = E.done("pe", mm)
                    turn3 = turn[lane][:, 0:8 * P].rearrange("p (i c) -> p i c", i=TPS)
                    yield "act", turned
                    half0 = E.done("act", act.activation(turn3[:, 0, :], b0[:, :], ACT.Copy))
                    E.after("dve", turned)
                    half1 = E.done("dve", dve.tensor_copy(turn3[:, 1, :], b1[:, :]))
                    yield half0, half1, v_ready
                    for i in range(TPS):
                        for j in range(4):
                            mm = pe.matmul(b0[0:32, 0:P], v_wide[:, i, j, :], turn3[:, i, j * P:(j + 1) * P],
                                           start=(i == 0 and j == 0), stop=(i == TPS - 1 and j == 3))
                    y_raw = E.done("pe", mm)
                    for j in range(4):
                        mm = pe.transpose(b1[:, j * P:(j + 1) * P], head(j), ident[:, :])
                    turned = E.done("pe", mm)
                    yield "dve", y_raw
                    y_rows = E.done("dve", dve.tensor_copy(rows_[:, 0:P], b0[0:32, 0:P]))
                    E.after("act", turned)
                    k2t_ready = E.done("act", act.activation(raw[lane][:, 0:4, :], halves(b1), ACT.Copy))
                    yield k2t_ready, y_rows,
                    y_turned = E.done("pe", pe.transpose(b1[:, 0:32], rows_[:, 0:P], ident[0:32, 0:32]))
                    for j in range(4):
                        mm = pe.matmul(b0[:, j * P:(j + 1) * P], raw[lane][:, j, :], raw[lane][:, j, :], start=True, stop=True)
                    squared = E.done("pe", mm)
                    E.after("dve", y_turned, inv3_ready)
                    y_ready = E.done("dve", dve.tensor_tensor(st[:, :, P:MW], b1[:, 0:32].rearrange("p (j d) -> p j d", j=4),
                                                              bc(inv3, HD_A), ALU.mult))
                    E.after("act", squared, c_ready)
                    state_ready = E.done("act", act.activation(st[:, :, 0:P], halves(b0), ACT.Copy, scale=inv_c[:, 0:1]))
                    yield state_ready, y_ready
                    s = 1.0
                    n4 = 4 * MW
                    bu = turn[lane][:, 0:n4].rearrange("p (j c) -> p j c", j=4)
                    diff = raw[lane][:, :, :].rearrange("p r m -> p (r m)")[:, 0:n4].rearrange("p (j c) -> p j c", j=4)
                    lin = turn[lane][:, n4:2 * n4].rearrange("p (j c) -> p j c", j=4)
                    pairs_of = lambda t: t.rearrange("p (k j) c -> p k (j c)", k=2)
                    out_of = lambda j: two[:, j // 2, MW * (j % 2):MW * (j % 2) + MW]
                    for k in range(ITERS):
                        for j in range(4):
                            mm = pe.matmul(out_of(j), st[:, j, 0:P], st[:, j, :], start=True, stop=True)
                        produced = E.done("pe", mm)
                        yield "act", produced
                        bu_ready = E.done("act", act.activation(pairs_of(bu), two[:, :, 0:2 * MW], ACT.Copy, scale=BETA / s))
                        E.after("dve", bu_ready, y_ready)
                        diff_ready = E.done("dve", dve.scalar_tensor_tensor(out=diff, in0=st[:, :, :], scalar=-3.5 * BETA,
                                                                            in1=bu, op0=ALU.mult, op1=ALU.add))
                        E.after("pool", bu_ready, y_ready, state_ready)
                        lin_ready = E.done("pool", pool.tensor_tensor(lin, st[:, :, :], bu, ALU.subtract))
                        yield diff_ready,
                        for j in range(4):
                            mm = pe.matmul(out_of(j), diff[:, j, 0:P], diff[:, j, :], start=True, stop=True)
                        produced = E.done("pe", mm)
                        yield "dve", produced, lin_ready
                        if k < ITERS - 1:
                            state_ready = E.done("dve", dve.scalar_tensor_tensor(
                                out=pairs_of(st[:, :, :]), in0=two[:, :, 0:2 * MW], scalar=-1.0 / (13.0 * BETA * BETA * s), in1=pairs_of(lin),
                                op0=ALU.mult, op1=ALU.add))
                            y_ready = state_ready
                        else:
                            for q in range(2):
                                z_ready = E.done("dve", dve.scalar_tensor_tensor(
                                    out=diagonal(z_wide)[:, 2 * q:2 * q + 2, :], scalar=-1.0 / (13.0 * BETA * BETA * s), op0=ALU.mult, op1=ALU.add,
                                    in0=two[:, q, 0:2 * MW].rearrange("p (j c) -> p j c", j=2)[:, :, P:MW],
                                    in1=lin[:, 2 * q:2 * q + 2, P:MW]))
                            y_ready = state_ready = z_ready
                        s *= 4.0 / 13.0
                        yield state_ready,
                    for j in range(4):
                        mm = pe.matmul(b1[0:32, 0:P], z_wide[:, j, :], head(j), start=(j == 0), stop=(j == 3))
                    produced = E.done("pe", mm)
                    yield "dve", produced, c_ready
                    w_rows = E.done("dve", dve.tensor_scalar(rows_[:, 0:P], b1[0:32, 0:P], inv_c[0:32, 0:1], 1.0 / s, ALU.mult, ALU.mult))
                    k_sep = turn[lane][:, 0:4 * P].rearrange("p (j m) -> p j m", j=4)
                    sep_ready = separate(quad_mask, k_sep, k_lm[lane][:, :], [z_ready, lm_ready])
                    yield w_rows,
                    turned = E.done("pe", pe.transpose(b0[:, 0:32], rows_[:, 0:P], ident[0:32, 0:32]))
                    yield "dve", turned
                    w_ready = E.done("dve", dve.tensor_copy(diagonal(w_wide), b0[:, 0:32].rearrange("p (j d) -> p j d", j=4)))
                    yield w_ready, sep_ready,
                    for i in range(TPS):
                        mm = pe.matmul(two[:, i, :], q_t[lane][:, i * P:(i + 1) * P], k_sep, start=True, stop=True)
                    scored = E.done("pe", mm)
                    maxes1, negs1, sums1, inv1 = sm[:, 16:24], sm[:, 24:32], sm[:, 32:40], sm[:, 40:48]
                    exped = yield from softmax_rows(lane, two.rearrange("p k (j m) -> p (k j) m", j=4), 8, P, 0.5, raw[lane],
                                         maxes1, negs1, sums1, scored)
                    yield "dve", exped
                    inv1_ready = E.done("dve", dve.reciprocal(inv1, sums1))
                    yield exped,
                    for r in range(8):
                        mm = pe.transpose(two[:, r // 4, (r % 4) * P:(r % 4 + 1) * P], raw[lane][:, r, :], ident[:, :])
                    turned = E.done("pe", mm)
                    turn1 = turn[lane][:, 0:8 * P].rearrange("p (i c) -> p i c", i=TPS)
                    yield "act", turned
                    half0 = E.done("act", act.activation(turn1[:, 0, :], b0[:, :], ACT.Copy))
                    E.after("dve", turned)
                    half1 = E.done("dve", dve.tensor_copy(turn1[:, 1, :], b1[:, :]))
                    yield half0, half1,
                    for i in range(TPS):
                        for j in range(4):
                            mm = pe.matmul(b0[0:32, i * P:(i + 1) * P], w_wide[:, j, :], turn1[:, i, j * P:(j + 1) * P],
                                           start=(j == 0), stop=(j == 3))
                    produced = E.done("pe", mm)
                    yield "act", produced
                    x_rows = E.done("act", act.activation(rows_, b0[0:32, 0:SEQ], ACT.Copy))
                    yield x_rows,
                    for i in range(TPS):
                        mm = pe.transpose(b1[:, 32 * i:32 * i + 32], rows_[:, i * P:(i + 1) * P], ident[0:32, 0:32])
                    produced = E.done("pe", mm)
                    yield "dve", produced, inv1_ready, [turned_by[b, q] for q in range(QUADS)]
                    out_view = stream[:, TPS * b:TPS * b + TPS, 32 * g:32 * g + 32].rearrange("p i (j d) -> p i j d", d=HD_A)
                    lane_free[lane] = written[b, g] = E.done("dve", dve.tensor_tensor(
                        out_view, b1[:, 0:64].rearrange("p (i j d) -> p i j d", i=TPS, j=4),
                        bc(inv1.rearrange("p (i j) -> p i j", i=TPS), HD_A), ALU.mult))
                return steps

            written = {}
            E.in_lanes([nystrom_task(b, g) for b in range(n_seq) for g in range(QUADS)])
            block_out = [[written[t // TPS, g] for g in range(QUADS)] for t in range(n_tiles)]
            E.barrier()

        wqkv = [sb(top, f"b_wqkv{n}", [P, 3 * INNER]) for n in range(2)]
        wo = [sb(top, f"b_wo{n}", [P, INNER // P, P]) for n in range(2)]
        rope = [sb(top, f"b_rope{n}", [P, 4, TPS, HD_B]) for n in range(2)]
        band = sb(top, "b_band", [P, KEYS])
        minus_half = sb(top, "minus_half", [P, 2 * HEADS_B])
        f_w1 = [sb(top, f"f_w1{n}", [P, 2 * HID]) for n in range(2)]
        f_w2 = [sb(top, f"f_w2{n}", [P, 3, P]) for n in range(2)]
        f_b1 = [sb(top, f"f_b1{n}", [P, 2, 3]) for n in range(2)]
        f_b2 = [sb(top, f"f_b2{n}", [P, P]) for n in range(2)]
        f_g = [sb(top, f"f_g{n}", [P, 1]) for n in range(2)]
        f_b = [sb(top, f"f_b{n}", [P, 1]) for n in range(2)]
        c_wq, c_wk = sb(top, "c_wq", [P, QUADS, P]), sb(top, "c_wk", [P, QUADS, P])
        c_wv = sb(top, "c_wv", [P, P])
        c_bias = sb(top, "c_bias", [P, HEADS_A, KEYS])
        d_wg, d_bg, d_order = (sb(top, f"d_{n}", [P, EXPERTS]) for n in ("wg", "bg", "order"))
        d_w1 = sb(top, "d_w1", [P, EXPERTS * RANK])
        d_w2 = sb(top, "d_w2", [P, EXPERTS * RANK // P, P])
        x_buf = [sb(top, f"x{n}", [P, TPS, P]) for n in range(LANES)]
        feats = [sb(top, f"feat{n}", [P, SEQ]) for n in range(LANES)]
        work = [sb(top, f"work{n}", [P, 3, TPS * INNER]) for n in range(LANES)]
        four = [sb(top, f"four{n}", [P, HEADS_B // 2, SEQ]) for n in range(LANES)]
        eight = [sb(top, f"eight{n}", [P, 2, HEADS_B // 2, SEQ]) for n in range(LANES)]
        small = [sb(top, f"small{n}", [P, 128]) for n in range(LANES)]

        with ExitStack() as first:
            gain = [sb(first, f"b_gain{n}", [P, 4, HD_B]) for n in range(2)]
            slope, rel, causal = sb(first, "c_slope", [P, HEADS_A]), sb(first, "c_rel", [P, KEYS]), sb(first, "c_causal", [P, KEYS])
            for n in range(2):
                for dst, src in ((wqkv[n][:, :], "b_wqkv"), (rope[n][:, :, :, :], None), (gain[n][:, :, :], "b_gain"),
                                 (wo[n][:, :, :], "b_wo"), (f_w1[n][:, :], "f_w1"), (f_w2[n][:, :, :], "f_w2"),
                                 (f_b1[n][:, :, :], "f_b1"), (f_b2[n][:, :], "f_b2"), (f_g[n][:, :], "f_g"), (f_b[n][:, :], "f_b")):
                    loaded_b = E.dma(f"load_b{n}", dst, io[src][n] if src else io["b_rope"])
                if n == 0:
                    loaded = [loaded_b, E.dma("load_band", band[:, :], io["b_band"])]
                else:
                    loaded.append(loaded_b)
            for dst, src in ((slope[:, :], "c_slope"), (rel[:, :], "c_rel"), (causal[:, :], "c_causal"), (c_wq[:, :, :], "c_wq"),
                             (c_wk[:, :, :], "c_wk"), (c_wv[:, :], "c_wv"), (d_wg[:, :], "d_wg"), (d_bg[:, :], "d_bg"),
                             (d_order[:, :], "d_order"), (d_w1[:, :], "d_w1"), (d_w2[:, :, :], "d_w2")):
                loaded_cd = E.dma("load_cd", dst, io[src])
            half_set = E.done("dve", dve.memset(minus_half[:, :], -0.5))
            tabled = []
            for n in range(2):
                E.after("dve", loaded[0] if n == 0 else loaded[2])
                tabled.append(E.done("dve", dve.tensor_tensor(rope[n][:, :, :, :], rope[n][:, :, :, :],
                                                              gain[n][:, :, :].unsqueeze(2).broadcast_to([P, 4, TPS, HD_B]), ALU.mult)))
            E.after("dve", loaded_cd)
            for h in range(HEADS_A):
                biased = E.done("dve", dve.scalar_tensor_tensor(out=c_bias[:, h, :], in0=rel[:, :], scalar=slope[:, h:h + 1],
                                                                in1=causal[:, :], op0=ALU.mult, op1=ALU.add))
        E.after("pe", loaded, loaded_cd)
        E.after("act", loaded)
        E.after("dve", loaded, tabled, biased)
        E.after("pool", half_set, tabled, loaded)

        def normalized(dst, src, sm, ready):
            stats_, mv, var, rs = (sm[:, 64:76].rearrange("p (i s) -> p i s", i=TPS), sm[:, 76:80].rearrange("p (i s) -> p i s", i=TPS),
                                   sm[:, 80:82], sm[:, 82:84])
            yield "dve", ready
            for i in range(TPS):
                mark = E.done("dve", dve.bn_stats(stats_[:, i, :], src[:, i, :]))
            E.after("dve", mark)
            for i in range(TPS):
                mark = E.done("dve", dve.bn_aggr(mv[:, i, :], stats_[:, i, :]))
            E.after("dve", mark)
            mark = E.done("dve", dve.tensor_scalar(var, mv[:, :, 1], LN_EPS, None, ALU.add))
            E.after("pool", mark)
            mark = E.done("pool", pool.tensor_tensor(rs, var, minus_half[:, 0:TPS], ALU.pow))
            yield "dve", mark
            for i in range(TPS):
                mark = E.done("dve", dve.tensor_scalar(dst[:, i, :], src[:, i, :], mv[:, i, 0:1], rs[:, i:i + 1], ALU.subtract, ALU.mult))
            return mark

        def residual(x, here, sm, ready):
            mark = yield from normalized(here, here, sm, ready)
            E.after("dve", mark)
            return E.done("dve", dve.tensor_tensor(x, x, here, ALU.add))

        def turn_input(lane, src, ready, shift):
            yield ready,
            bank, dst = psum[:, 2 * lane, :], feats[lane]
            for i in range(TPS):
                mm = pe.transpose(bank[:, i * P:(i + 1) * P], src[:, i, :], ident[:, :])
            turned = E.done("pe", mm)
            yield "act", turned
            if shift:
                E.done("act", act.activation(dst[0:64, :], bank[0:64, 0:SEQ], ACT.Copy))
                return E.done("act", act.activation(dst[64:P, 1:SEQ], bank[64:P, 0:SEQ - 1], ACT.Copy))
            return E.done("act", act.activation(dst[:, :], bank[:, 0:SEQ], ACT.Copy))

        def soft_scores(lane, q_of, k_of, bias_of, scale, ex, et, sm, sums, weighted):
            two = both(lane)
            for h in range(2):
                pe.matmul(two[:, h, 0:P], q_of(h, 0), k_of(h)[:, 0:P], start=True, stop=True)
                mm = pe.matmul(two[:, h, P:KEYS], q_of(h, 1), k_of(h), start=True, stop=True)
            scored = E.done("pe", mm)
            yield "dve", scored
            maxes, negs, inv = sm[:, 0:4], sm[:, 4:8], sm[:, 8:12]
            spans = [(0, P), (P, KEYS)]
            for h in range(2):
                for i, (lo, hi) in enumerate(spans):
                    r = TPS * h + i
                    mark = E.done("dve", dve.tensor_tensor_reduce(
                        out=ex[:, h, lo:hi], in0=two[:, h, lo:hi], in1=bias_of(h)[:, lo:hi], scale=1.0, scalar=LOWEST,
                        op0=ALU.add, op1=ALU.max, accum_out=maxes[:, r:r + 1]))
            E.after("dve", mark)
            negated = E.done("dve", dve.tensor_scalar(negs, maxes, -scale, None, ALU.mult))
            yield "act", negated
            ready = []
            for h in range(2):
                for i, (lo, hi) in enumerate(spans):
                    r = TPS * h + i
                    exped = E.done("act", act.activation(ex[:, h, lo:hi], ex[:, h, lo:hi], ACT.Exp, bias=negs[:, r:r + 1],
                                                         scale=scale, accum_out=sums[:, i, h:h + 1]))
                if weighted:
                    yield "dve", exped
                    invs = E.done("dve", dve.reciprocal(inv[:, TPS * h:TPS * h + TPS], sums[:, :, h]))
                    name = ("pool", "dve")[h]
                    E.after(name, invs)
                    for i, (lo, hi) in enumerate(spans):
                        exped = E.done(name, E.queues[name].tensor_scalar(ex[:, h, lo:hi], ex[:, h, lo:hi],
                                                                          inv[:, TPS * h + i:TPS * h + i + 1], None, ALU.mult))
                ready.append(exped)
            yield ready
            for h in range(2):
                for c in range(3):
                    mm = pe.transpose(two[:, h, c * P:(c + 1) * P], ex[:, h, c * P:(c + 1) * P], ident[:, :])
            turned = E.done("pe", mm)
            yield "act", turned
            half0 = E.done("act", act.activation(et[:, 0, :], two[:, 0, 0:KEYS], ACT.Copy))
            E.after("dve", turned)
            half1 = E.done("dve", dve.tensor_copy(et[:, 1, :], two[:, 1, 0:KEYS]))
            return [half0, half1]

        def local_attention(lane, layer, here, ready):
            b0, two, sm, hT = psum[:, 2 * lane, :], both(lane), small[lane], feats[lane]
            x_, t1, t2 = (work[lane][:, n, :].rearrange("p (i c) -> p i c", i=TPS) for n in range(3))
            v_sb = t2
            q_t, k_sep = four[lane], eight[lane]
            o_t = q_t
            k_zeroed = None
            if layer == 0:
                E.after("pool", ready)
                k_zeroed = E.done("pool", pool.memset(k_sep[:, :, :, :], 0.0))
            shifted = yield from turn_input(lane, here, ready, True)
            yield shifted,

            def project(kind):
                for i in range(TPS):
                    mm = pe.matmul(two[:, i, :], hT[:, i * P:(i + 1) * P], wqkv[layer][:, kind * INNER:(kind + 1) * INNER],
                                   start=True, stop=True)
                return E.done("pe", mm)

            for kind in range(2):
                produced = project(kind)
                yield "act", produced
                copied = E.done("act", act.activation(x_, two, ACT.Copy))
                E.after("act", copied)
                squared = E.done("act", act.activation(t1, x_, ACT.Square))
                by_head = lambda t: t.rearrange("p i (h d) -> p i h d", d=HD_B)
                cos = rope[layer][:, 2 * kind, :, :].unsqueeze(2).broadcast_to([P, TPS, HEADS_B, HD_B])
                sin = rope[layer][:, 2 * kind + 1, :, :].unsqueeze(2).broadcast_to([P, TPS, HEADS_B, HD_B])
                hh = HD_B // 2
                E.after("pool", copied)
                pool.tensor_tensor(by_head(t2)[:, :, :, 0:hh], by_head(x_)[:, :, :, hh:], sin[:, :, :, 0:hh], ALU.mult)
                sined = E.done("pool", pool.tensor_tensor(by_head(t2)[:, :, :, hh:], by_head(x_)[:, :, :, 0:hh],
                                                          sin[:, :, :, hh:], ALU.mult))
                ss, rn = sm[:, 16:32], sm[:, 32:48]
                heads = lambda t: t.rearrange("p i (h d) -> p (i h) d", d=HD_B)
                yield "dve", squared
                ssed = E.done("dve", dve.tensor_reduce(out=ss, in_=heads(t1), axis=AX.X, op=ALU.add))
                E.after("dve", ssed)
                clipped = E.done("dve", dve.tensor_scalar(ss, ss, 1e-24, None, ALU.max))
                E.after("pool", clipped)
                inv_norm = E.done("pool", pool.tensor_tensor(rn, ss, minus_half[:, :], ALU.pow))
                cosed = E.done("dve", dve.tensor_tensor(by_head(t1), by_head(x_), cos, ALU.mult))
                yield "dve", cosed, sined
                roped = E.done("dve", dve.tensor_tensor(x_, t1, t2, ALU.add))
                E.after("dve", roped, inv_norm)
                roped = E.done("dve", dve.tensor_tensor(heads(x_), heads(x_), bc(rn, HD_B), ALU.mult))
                yield roped,
                for i in range(TPS):
                    for c in range(4):
                        mm = pe.transpose(two[:, i, c * P:(c + 1) * P], x_[:, i, c * P:(c + 1) * P], ident[:, :])
                turned = E.done("pe", mm)
                yield "act", turned, k_zeroed
                by_pair = lambda t: t.rearrange("p c (i t) -> p i c t", i=TPS)
                source = two.rearrange("p i (c t) -> p i c t", c=4)
                if kind == 0:
                    copied = E.done("act", act.activation(by_pair(q_t[:, :, :]), source, ACT.Copy))
                else:
                    for h in range(2):
                        half = slice(64 * h, 64 * h + 64)
                        copied = E.done("act", act.activation(by_pair(k_sep[half, h, :, :]), source[half], ACT.Copy))
                yield copied,
            produced = project(2)
            yield "act", produced, roped
            v_ready = E.done("act", act.activation(v_sb, two, ACT.Copy))
            yield v_ready,
            ex, et = (work[lane][:, n, 0:2 * KEYS].rearrange("p (h k) -> p h k", h=2) for n in range(2))
            sums = sm[:, 12:16].rearrange("p (i h) -> p i h", i=TPS)
            for c in range(HEADS_B // 2):
                halves = yield from soft_scores(
                    lane, lambda h, i: q_t[:, c, i * P:(i + 1) * P], lambda h: k_sep[:, h, c, :],
                    lambda h: band[:, :], 8.0, ex, et, sm, sums, True)
                yield halves
                for h in range(2):
                    v_of = lambda i: v_sb[:, i, c * P + 64 * h:c * P + 64 * h + 64]
                    pe.matmul(two[0:64, h, 0:SEQ], v_of(0), et[:, h, 0:SEQ], start=True, stop=False)
                    mm = pe.matmul(two[0:64, h, P:SEQ], v_of(1), et[:, h, SEQ:KEYS], start=False, stop=True)
                produced = E.done("pe", mm)
                yield "act", produced
                half0 = E.done("act", act.activation(o_t[0:64, c, :], two[0:64, 0, 0:SEQ], ACT.Copy))
                E.after("dve", produced)
                half1 = E.done("dve", dve.tensor_copy(o_t[64:P, c, :], two[0:64, 1, 0:SEQ]))
                yield half0, half1
            for i in range(TPS):
                for c in range(4):
                    mm = pe.matmul(b0[:, i * P:(i + 1) * P], o_t[:, c, i * P:(i + 1) * P], wo[layer][:, c, :],
                                   start=(c == 0), stop=(c == 3))
            produced = E.done("pe", mm)
            yield "dve", produced
            return E.done("dve", dve.tensor_tensor(here, here, b0[:, 0:SEQ].rearrange("p (i d) -> p i d", i=TPS), ALU.add))

        def feed_forward(lane, layer, here, ready):
            b0, b1, two, sm, hT = psum[:, 2 * lane, :], psum[:, 2 * lane + 1, :], both(lane), small[lane], feats[lane]
            h_tok = work[lane][:, 0, 0:SEQ].rearrange("p (i d) -> p i d", i=TPS)
            gate = work[lane][:, 1, 0:3 * SEQ].rearrange("p (c t) -> p c t", c=3)
            normed_t = work[lane][:, 2, 0:SEQ]
            chunks = [(0, P), (P, P), (2 * P, HID - 2 * P)]
            shifted = yield from turn_input(lane, here, ready, True)
            yield shifted,
            for i in range(TPS):
                mm = pe.transpose(b1[:, i * P:(i + 1) * P], hT[:, i * P:(i + 1) * P], ident[:, :])
            turned = E.done("pe", mm)
            yield "act", turned
            copied = E.done("act", act.activation(h_tok, b1[:, 0:SEQ].rearrange("p (i d) -> p i d", i=TPS), ACT.Copy))
            E.after("pool", turned)
            biased = E.done("pool", pool.tensor_tensor(here, here, f_b2[layer][:, :].unsqueeze(1).broadcast_to([P, TPS, P]), ALU.add))
            mark = yield from normalized(h_tok, h_tok, sm, copied)
            yield mark,
            for i in range(TPS):
                mm = pe.transpose(b0[:, i * P:(i + 1) * P], h_tok[:, i, :], ident[:, :])
            turned = E.done("pe", mm)
            yield "dve", turned
            scaled = E.done("dve", dve.tensor_scalar(normed_t, b0[:, 0:SEQ], f_g[layer][:, 0:1], f_b[layer][:, 0:1], ALU.mult, ALU.add))
            yield scaled,

            def chunk(c, part):
                lo, n = chunks[c]
                out = two[0:n, c // 2, (c % 2) * SEQ:(c % 2) * SEQ + SEQ]
                lo += part * HID
                return out, pe.matmul(out, f_w1[layer][:, lo:lo + n], normed_t, start=True, stop=True)

            outs = [chunk(c, 1) for c in range(3)]
            produced = E.done("pe", outs[-1][1])
            yield "act", produced
            for c, (lo, n) in enumerate(chunks):
                gated = E.done("act", act.activation(gate[0:n, c, :], outs[c][0], ACT.Gelu, bias=f_b1[layer][0:n, 1, c:c + 1]))
            yield gated,
            outs = [chunk(c, 0) for c in range(3)]
            produced = E.done("pe", outs[-1][1])
            yield "dve", produced, gated
            for c, (lo, n) in enumerate(chunks):
                used = E.done("dve", dve.scalar_tensor_tensor(out=gate[0:n, c, :], in0=outs[c][0], scalar=f_b1[layer][0:n, 0, c:c + 1],
                                                              in1=gate[0:n, c, :], op0=ALU.add, op1=ALU.mult))
            yield used,
            for i in range(TPS):
                for c, (lo, n) in enumerate(chunks):
                    mm = pe.matmul(b1[:, i * P:(i + 1) * P], gate[0:n, c, i * P:(i + 1) * P], f_w2[layer][0:n, c, :],
                                   start=(c == 0), stop=(c == 2))
            produced = E.done("pe", mm)
            yield "dve", produced, biased
            return E.done("dve", dve.tensor_tensor(here, here, b1[:, 0:SEQ].rearrange("p (i d) -> p i d", i=TPS), ALU.add))

        def causal_attention(lane, here, ready):
            b0, b1, two, sm, hT = psum[:, 2 * lane, :], psum[:, 2 * lane + 1, :], both(lane), small[lane], feats[lane]
            k_sep, k_t, q_t = four[lane][:, :, :], eight[lane][:, 0, 0, :], eight[lane][:, 0, 1, :]
            rows_sb = eight[lane][0:32, 0, 2, :]
            v_wide = eight[lane][:, 1, :, :].rearrange("p c t -> p (c t)").rearrange("p (i h c) -> p i h c", i=TPS, h=HEADS_A)
            ex = work[lane][:, 0, 0:2 * KEYS].rearrange("p (h k) -> p h k", h=2)
            exp_t = work[lane][:, 1:3, 0:2 * KEYS].rearrange("p n (h k) -> p n h k", h=2)
            E.after("pool", ready)
            v_zeroed = E.done("pool", pool.memset(v_wide, 0.0))
            turned = yield from turn_input(lane, here, ready, False)
            yield turned,
            for i in range(TPS):
                mm = pe.matmul(b0[:, P * i:P * (i + 1)], hT[:, i * P:(i + 1) * P], c_wv[:, :], start=True, stop=True)
            produced = E.done("pe", mm)
            yield "dve", produced, v_zeroed
            for i in range(TPS):
                for g in range(QUADS):
                    cols = slice(P * i + 32 * g, P * i + 32 * g + 32)
                    v_ready = E.done("dve", dve.tensor_copy(diagonal(v_wide[:, i, 4 * g:4 * g + 4, :]),
                                                            b0[:, cols].rearrange("p (j d) -> p j d", j=4)))
            yield v_ready,
            for g in range(QUADS):
                pe.matmul(b0[:, 0:SEQ], c_wq[:, g, :], hT[:, :], start=True, stop=True)
                projected = E.done("pe", pe.matmul(b0[:, SEQ:2 * SEQ], c_wk[:, g, :], hT[:, :], start=True, stop=True))
                yield "act", projected
                q_ready = E.done("act", act.activation(q_t, b0[:, 0:SEQ], ACT.Copy, scale=1.0 / math.sqrt(P)))
                k_ready = E.done("act", act.activation(k_t, b0[:, SEQ:2 * SEQ], ACT.Copy))
                sep_ready = separate(quad_mask, k_sep, k_t, k_ready)
                yield sep_ready,
                sums, inv = sm[:, 12:20].rearrange("p (i j) -> p i j", i=TPS), sm[:, 20:28]
                for c in range(2):
                    halves = yield from soft_scores(
                        lane, lambda h, i: q_t[:, i * P:(i + 1) * P], lambda h: k_sep[:, 2 * c + h, :],
                        lambda h: c_bias[:, 4 * g + 2 * c + h, :], 1.0, ex, exp_t[:, c, :, :], sm, sums[:, :, 2 * c:2 * c + 2], False)
                    yield halves
                for j in range(4):
                    e = exp_t[:, j // 2, j % 2, :]
                    pe.matmul(b0[0:32, 0:SEQ], v_wide[:, 0, 4 * g + j, :], e[:, 0:SEQ], start=(j == 0), stop=False)
                    mm = pe.matmul(b0[0:32, P:SEQ], v_wide[:, 1, 4 * g + j, :], e[:, SEQ:KEYS], start=False, stop=(j == 3))
                produced = E.done("pe", mm)
                yield "act", produced
                x_rows = E.done("act", act.activation(rows_sb, b0[0:32, 0:SEQ], ACT.Copy))
                E.after("dve", produced)
                inv_ready = E.done("dve", dve.reciprocal(inv, sm[:, 12:20]))
                yield x_rows,
                for i in range(TPS):
                    mm = pe.transpose(b1[:, 32 * i:32 * i + 32], rows_sb[:, i * P:(i + 1) * P], ident[0:32, 0:32])
                produced = E.done("pe", mm)
                yield "dve", produced, inv_ready
                out_view = here[:, :, 32 * g:32 * g + 32].rearrange("p i (j d) -> p i j d", d=HD_A)
                written = E.done("dve", dve.tensor_tensor(
                    out_view, b1[:, 0:64].rearrange("p (i j d) -> p i j d", i=TPS, j=4),
                    bc(inv.rearrange("p (i j) -> p i j", i=TPS), HD_A), ALU.mult))
                if g < QUADS - 1:
                    yield written,
            return written

        def experts(lane, here, ready):
            b0, b1, two, sm, hT = psum[:, 2 * lane, :], psum[:, 2 * lane + 1, :], both(lane), small[lane], feats[lane]
            hid, hid_t = (work[lane][:, n, :].rearrange("p (i c) -> p i c", i=TPS) for n in range(2))
            by_tile = lambda n: work[lane][:, 2, 16 * n:16 * n + 16].rearrange("p (i e) -> p i e", i=TPS)
            logits, gates, hot1, hot2, rest = (by_tile(n) for n in range(5))
            v1, v2, m_, gap, e_ = (work[lane][:, 2, 128 + TPS * n:128 + TPS * (n + 1)] for n in range(5))
            turned = yield from turn_input(lane, here, ready, False)
            yield turned,
            for i in range(TPS):
                mm = pe.matmul(b0[:, EXPERTS * i:EXPERTS * (i + 1)], hT[:, i * P:(i + 1) * P], d_wg[:, :], start=True, stop=True)
            produced = E.done("pe", mm)
            yield "dve", produced
            all_tiles = lambda t: t[:, :].unsqueeze(1).broadcast_to([P, TPS, EXPERTS])

            def step(instruction):
                mark = E.done("dve", instruction)
                E.after("dve", mark)
                return mark

            def one_hot(dst, values, v):
                step(dve.tensor_tensor(dst, values, bc(v, EXPERTS), ALU.is_equal))
                step(dve.tensor_tensor(dst, dst, all_tiles(d_order), ALU.mult))
                step(dve.tensor_reduce(out=m_, in_=dst, axis=AX.X, op=ALU.max))
                step(dve.tensor_tensor(dst, dst, bc(m_, EXPERTS), ALU.is_equal))

            read = step(dve.tensor_tensor(logits, b0[:, 0:TPS * EXPERTS].rearrange("p (i e) -> p i e", i=TPS), all_tiles(d_bg), ALU.add))
            step(dve.tensor_reduce(out=v1, in_=logits, axis=AX.X, op=ALU.max))
            one_hot(hot1, logits, v1)
            step(dve.scalar_tensor_tensor(out=rest, in0=hot1, scalar=LOWEST, in1=logits, op0=ALU.mult, op1=ALU.add))
            step(dve.tensor_reduce(out=v2, in_=rest, axis=AX.X, op=ALU.max))
            one_hot(hot2, rest, v2)
            gap_ready = step(dve.tensor_tensor(gap, v2, v1, ALU.subtract))
            E.after("act", gap_ready)
            e_ready = E.done("act", act.activation(e_, gap, ACT.Exp))
            E.after("dve", e_ready)
            step(dve.tensor_scalar(m_, e_, 1.0, None, ALU.add))
            step(dve.reciprocal(v1, m_))
            step(dve.tensor_tensor(v2, e_, v1, ALU.mult))
            step(dve.tensor_tensor(hot1, hot1, bc(v1, EXPERTS), ALU.mult))
            step(dve.tensor_tensor(hot2, hot2, bc(v2, EXPERTS), ALU.mult))
            step(dve.tensor_tensor(gates, hot1, hot2, ALU.add))
            yield read,
            for i in range(TPS):
                mm = pe.matmul(two[:, i, :], hT[:, i * P:(i + 1) * P], d_w1[:, :], start=True, stop=True)
            produced = E.done("pe", mm)
            yield "act", produced
            gelued = E.done("act", act.activation(hid, two, ACT.Gelu))
            E.after("dve", gelued)
            by_e = hid.rearrange("p i (e r) -> p i e r", r=RANK)
            weighted = E.done("dve", dve.tensor_tensor(by_e, by_e, bc(gates, RANK), ALU.mult))
            yield weighted,
            for i in range(TPS):
                for c in range(4):
                    mm = pe.transpose(two[:, i, c * P:(c + 1) * P], hid[:, i, c * P:(c + 1) * P], ident[:, :])
            turned = E.done("pe", mm)
            yield "dve", turned
            half1 = E.done("dve", dve.tensor_copy(hid_t[:, 1, :], two[:, 1, :]))
            E.after("act", turned)
            half0 = E.done("act", act.activation(hid_t[:, 0, :], two[:, 0, :], ACT.Copy))
            yield half0, half1
            for i in range(TPS):
                for c in range(4):
                    mm = pe.matmul(b0[:, i * P:(i + 1) * P], hid_t[:, i, c * P:(c + 1) * P], d_w2[:, c, :],
                                   start=(c == 0), stop=(c == 3))
            produced = E.done("pe", mm)
            yield "dve", produced
            return E.done("dve", dve.tensor_scalar(here, b0[:, 0:SEQ].rearrange("p (i d) -> p i d", i=TPS), 2.0, None, ALU.mult))

        stored = [None] * LANES

        def sequence_task(b):
            def steps(lane):
                x, here, sm = x_buf[lane][:, :, :], stream[:, TPS * b:TPS * b + TPS, :], small[lane]
                tiles = slice(TPS * b, TPS * b + TPS)
                E.after("sp", stored[lane])
                x_loaded = E.dma(f"load_x_lane{lane}", x, x_dram[:, tiles, :])

                added = yield from residual(x, here, sm, [block_out[TPS * b], x_loaded, lane_free[lane]])
                zeroed = E.done("dve", dve.memset(feats[lane][64:P, 0:1], 0.0))
                mark = yield from normalized(here, x, sm, added)
                for layer in range(2):
                    mark = yield from local_attention(lane, layer, here, [mark, zeroed])
                    mark = yield from feed_forward(lane, layer, here, mark)
                mark = yield from residual(x, here, sm, mark)
                mark = yield from normalized(here, x, sm, mark)
                mark = yield from causal_attention(lane, here, mark)
                mark = yield from residual(x, here, sm, mark)
                mark = yield from normalized(here, x, sm, mark)
                mark = yield from experts(lane, here, mark)
                lane_free[lane] = yield from residual(x, here, sm, mark)
                E.after("sp", lane_free[lane])
                stored[lane] = E.dma(f"store_lane{lane}", out_dram[:, tiles, :], x)
            return steps

        E.in_lanes([sequence_task(b) for b in range(n_seq)])
        E.after("sp", [m for m in stored if m])


def layouts(inputs):
    a = {k: np.asarray(v) for k, v in inputs.items()}
    f = np.float32

    def quads(w):
        out = np.zeros((w.shape[0], QUADS, 4, 32), f)
        out[:, :, :, :HD_A] = w.reshape(w.shape[0], QUADS, 4, HD_A)
        return out.reshape(w.shape[0], QUADS, P)

    def rows(v):
        return np.ascontiguousarray(np.broadcast_to(v, (P, *v.shape)))

    t = {"x": a["L0_attn_x"], "ident": np.eye(P, dtype=f)}
    t["a_wq"], t["a_wk"] = quads(a["L0_attn_Wq"].T), quads(a["L0_attn_Wk"].T)
    t["a_wv"] = a["L0_attn_Wv"].T
    t["a_bq"] = quads(a["L0_attn_bq"][None])[0].T
    t["a_bk"] = quads(a["L0_attn_bk"][None])[0].T
    t["a_bv"] = rows(a["L0_attn_bv"])
    t["quad_mask"] = np.repeat(np.eye(4, dtype=f), 32, axis=0)
    t["b_wqkv"] = a["L0_ffn_wqkv"]
    t["b_wo"] = a["L0_ffn_wo"].reshape(2, INNER // P, P, P).transpose(0, 2, 1, 3)
    half = np.arange(0, HD_B, 2, dtype=f)
    inv_freq = (1.0 / f(10000.0) ** (half / f(HD_B))).astype(f)
    pos = np.arange(SEQ, dtype=f)
    freqs = pos[:, None] * inv_freq[None, :]
    freqs = np.concatenate([freqs, freqs], -1)
    base = (half + f(0.4 * HD_B)) / f(1.4 * HD_B)
    power = (pos - SEQ // 2) / f(WIN // 2)
    scale = base[None, :] ** power[:, None]
    scale = np.concatenate([scale, scale], -1).astype(f)
    sign = np.concatenate([-np.ones(HD_B // 2), np.ones(HD_B // 2)]).astype(f)
    cos, sin = np.cos(freqs), np.sin(freqs) * sign
    rope = np.stack([cos * scale, sin * scale, cos / scale, sin / scale])
    t["b_rope"] = rope.reshape(4, TPS, P, HD_B).transpose(2, 0, 1, 3).astype(f)

    def rotated(v):
        return np.concatenate([v[..., HD_B // 2:], v[..., :HD_B // 2]], -1)

    qs, ks = a["L0_ffn_q_scale"], a["L0_ffn_k_scale"]
    gain = np.stack([qs, rotated(qs), ks, rotated(ks)], 1)
    t["b_gain"] = np.broadcast_to(gain[:, None], (2, P, 4, HD_B))
    q = np.arange(P)[:, None]
    delta = np.concatenate([q - np.arange(P)[None], q + P - np.arange(SEQ)[None]], 1)
    t["b_band"] = np.where((delta < 0) | (delta > WIN), MASKED, 0.0).astype(f)
    t["f_w1"] = a["L0_ffn_w1"]
    w2 = np.zeros((2, 3 * P, P), f)
    w2[:, :HID] = a["L0_ffn_w2"]
    t["f_w2"] = w2.reshape(2, 3, P, P).transpose(0, 2, 1, 3)
    b1 = np.zeros((2, 2, 3 * P), f)
    b1[:, :, :HID] = a["L0_ffn_b1"].reshape(2, 2, HID)
    t["f_b1"] = b1.reshape(2, 2, 3, P).transpose(0, 3, 1, 2)
    t["f_b2"] = np.broadcast_to(a["L0_ffn_b2"][:, None], (2, P, P))
    t["f_g"], t["f_b"] = a["L0_ffn_ln_g"][:, :, None], a["L0_ffn_ln_b"][:, :, None]
    w = a["L1_attn_W_kqv"]
    t["c_wk"], t["c_wq"], t["c_wv"] = quads(w[:, 0:P]), quads(w[:, P:2 * P]), w[:, 2 * P:]
    t["c_slope"] = rows(a["L1_attn_m"].reshape(HEADS_A))
    t["c_rel"] = (-delta).astype(f)
    t["c_causal"] = np.where(delta < 0, MASKED, 0.0).astype(f)
    t["d_wg"], t["d_bg"] = a["L1_ffn_Wg"].T, rows(a["L1_ffn_bg"])
    t["d_w1"] = a["L1_ffn_W1"].reshape(EXPERTS * RANK, P).T
    t["d_w2"] = a["L1_ffn_W2"].transpose(0, 2, 1).reshape(4, P, P).transpose(1, 0, 2)
    t["d_order"] = rows(np.arange(EXPERTS, 0, -1).astype(f))
    return {k: np.ascontiguousarray(v) for k, v in t.items()}


def kernel(**inputs):
    import concourse.bacc as bacc
    from concourse.bass_utils import run_bass_kernel_spmd

    arrays = layouts(inputs)
    nc = bacc.Bacc("TRN2", target_bir_lowering=False, num_devices=1)
    io = {n: nc.dram_tensor(f"in_{n}", v.shape, mybir.dt.from_np(v.dtype), kind="ExternalInput").ap() for n, v in arrays.items()}
    io["out"] = nc.dram_tensor("out", arrays["x"].shape, F32, kind="ExternalOutput").ap()
    bass_four_blocks(nc, io)
    run = run_bass_kernel_spmd(nc, [{f"in_{n}": v for n, v in arrays.items()}], core_ids=[0])
    return run.results[0]["out"]
```

```python
import math
from contextlib import ExitStack

import numpy as np
import concourse.bass as bass
from concourse import mybir

F32 = mybir.dt.float32
ALU = mybir.AluOpType
ACT = mybir.ActivationFunctionType
AX = mybir.AxisListType

P = 128
SEQ = 256
TPS = SEQ // P
LANES = 4
BANK = 512
LN_EPS = 1e-5
LOWEST = -3.0e38
MASKED = -1.0e30

HEADS_A, HD_A = 16, 8
QUADS = HEADS_A // 4
ITERS = 6
HEADS_B, HD_B, WIN = 8, 64, 64
INNER = HEADS_B * HD_B
HID = 341
EXPERTS, RANK = 8, 64
KEYS = 3 * P


class Queue:

    FIXED = {"pe": 3.0, "act": 90.0, "dve": 70.0, "pool": 70.0, "sp": 50.0}
    PER_COLUMN = {"act": 0.83, "dve": 1.04, "pool": 2.2}

    def __init__(self, name, engine):
        self.name, self.engine, self.clock = name, engine, 0.0
        self.wait_ge, self.dma_start = engine.wait_ge, engine.dma_start

    def took(self, instruction, columns):
        self.clock += self.FIXED[self.name] + self.PER_COLUMN[self.name] * columns
        return instruction

    def matmul(self, out, lhsT, rhs, **kw):
        m, n = lhsT.free_size(), rhs.free_size()
        self.clock += self.FIXED["pe"] + 4 * (n / 2.4 if n >= 96 else max(n / 2.4, m / 1.2))
        return self.engine.matmul(out, lhsT, rhs, **kw)

    def transpose(self, out, in_, identity):
        self.clock += self.FIXED["pe"] + in_.free_size() / 1.2
        return self.engine.transpose(out, in_, identity)

    def activation(self, out, in_, func, **kw):
        extra = 186 if "accum_out" in kw else 0
        return self.took(self.engine.activation(out, in_, func, **kw), extra + out.free_size())

    def memset(self, out, value):
        return self.took(self.engine.memset(out, value), out.free_size())

    def tensor_copy(self, out, in_):
        return self.took(self.engine.tensor_copy(out, in_), out.free_size())

    def reciprocal(self, out, in_):
        return self.took(self.engine.reciprocal(out, in_), out.free_size())

    def tensor_tensor(self, out, in0, in1, op):
        slow = 70 if op == ALU.pow else 1
        return self.took(self.engine.tensor_tensor(out, in0, in1, op), slow * out.free_size())

    def tensor_scalar(self, out, in_, scalar1, scalar2, *ops):
        return self.took(self.engine.tensor_scalar(out, in_, scalar1, scalar2, *ops), out.free_size() / 2)

    def scalar_tensor_tensor(self, out, **kw):
        return self.took(self.engine.scalar_tensor_tensor(out=out, **kw), out.free_size())

    def tensor_tensor_reduce(self, out, **kw):
        return self.took(self.engine.tensor_tensor_reduce(out=out, **kw), out.free_size())

    def tensor_reduce(self, out, in_, **kw):
        return self.took(self.engine.tensor_reduce(out=out, in_=in_, **kw), in_.free_size())

    def bn_stats(self, out, in_):
        return self.took(self.engine.bn_stats(out, in_), in_.free_size())

    def bn_aggr(self, out, in_):
        return self.took(self.engine.bn_aggr(out, in_), in_.free_size())


class Engines:

    LATENCY = 250.0

    def __init__(self, nc, ctx):
        self.nc, self.ctx = nc, ctx
        self.queues = {n: Queue(n, e) for n, e in (("pe", nc.tensor), ("act", nc.scalar), ("dve", nc.vector),
                                                   ("pool", nc.gpsimd), ("sp", nc.sync))}
        self.sems = {n: ctx.enter_context(nc.semaphore(f"done_{n}")) for n in self.queues if n != "sp"}
        self.count = dict.fromkeys(self.sems, 0)
        self.seen = {}
        self.end = {}

    def done(self, name, instruction):
        instruction.then_inc(self.sems[name], 1)
        self.count[name] += 1
        mark = (name, self.count[name])
        self.end[mark] = self.queues[name].clock + self.LATENCY
        return mark

    def ready(self, marks):
        if isinstance(marks, list):
            return max((self.ready(m) for m in marks), default=0.0)
        return self.end.get(marks, 0.0)

    def after(self, name, *marks):
        queue = self.queues[name]
        for mark in marks:
            if mark is None:
                continue
            if isinstance(mark, list):
                self.after(name, *mark)
                continue
            queue.clock = max(queue.clock, self.ready(mark))
            source, value = mark
            if self.seen.get((name, source), 0) < value:
                queue.wait_ge(self.sems[source], value)
                self.seen[(name, source)] = value

    def dma(self, group, out, in_):
        if group not in self.sems:
            self.sems[group] = self.ctx.enter_context(self.nc.semaphore(group))
            self.count[group] = 0
        self.queues["sp"].dma_start(out, in_).then_inc(self.sems[group], 16)
        self.count[group] += 16
        return (group, self.count[group])

    def barrier(self):
        marks = [(n, self.count[n]) for n in self.queues if self.count.get(n)]
        for name in self.queues:
            self.after(name, marks)

    def in_lanes(self, tasks):
        queues = [list(tasks[n::LANES]) for n in range(LANES)]
        running, marks, since, turn = [None] * LANES, [[]] * LANES, [0] * LANES, 0
        engine = ["pe"] * LANES

        def take(lane):
            yielded = list(next(running[lane]))
            engine[lane] = yielded.pop(0) if isinstance(yielded[0], str) else "pe"
            marks[lane] = yielded

        def advance(lane):
            if running[lane] is not None:
                try:
                    take(lane)
                    return
                except StopIteration:
                    running[lane] = None
            if queues[lane]:
                running[lane] = queues[lane].pop(0)(lane)
                take(lane)

        for lane in range(LANES):
            advance(lane)
        while any(r is not None for r in running):
            lane = min((n for n in range(LANES) if running[n] is not None),
                       key=lambda n: (max(self.queues[engine[n]].clock, self.ready(marks[n])), since[n]))
            self.after(engine[lane], *marks[lane])
            turn += 1
            since[lane] = turn
            advance(lane)


def bc(ap, width):
    return ap.unsqueeze(len(ap.shape)).broadcast_to([*ap.shape, width])


def bass_four_blocks(nc, io):
    n_seq = io["x"].shape[0]
    n_tiles = n_seq * TPS
    top = ExitStack()
    with top:
        E = Engines(nc, top)
        pe, act, dve, pool = (E.queues[n] for n in ("pe", "act", "dve", "pool"))

        def sb(ctx, name, shape, dt=F32):
            return ctx.enter_context(nc.sbuf_tensor(name, shape, dt))

        psum = top.enter_context(nc.psum_tensor("psum", [P, 2 * LANES, BANK], F32))

        stream = sb(top, "stream", [P, n_tiles, P])
        ident = sb(top, "ident", [P, P])
        ones = sb(top, "ones", [P, P])
        stats = sb(top, "stats", [P, n_tiles, 6])
        moments = sb(top, "moments", [P, n_tiles, 2])
        deviation = sb(top, "deviation", [P, n_tiles])
        rstd = sb(top, "rstd", [P, n_tiles])
        eps = sb(top, "eps", [P, 1])
        head_mask = sb(top, "head_mask", [P, HEADS_A])
        ident_in = E.dma("load_ident", ident[:, :], io["ident"])
        ones_set = E.done("dve", dve.memset(ones[:, :], 1.0))
        eps_set = E.done("dve", dve.memset(eps[:, :], LN_EPS))
        x_dram = io["x"].rearrange("b (i p) d -> p (b i) d", p=P)
        out_dram = io["out"].rearrange("b (i p) d -> p (b i) d", p=P)
        TG = min(8, n_tiles)

        def norm_stats(src, ready):
            for t in range(n_tiles):
                E.after("dve", ready[t])
                last = E.done("dve", dve.bn_stats(stats[:, t, :], src[:, t, :]))
            E.after("dve", last)
            for t in range(n_tiles):
                last = E.done("dve", dve.bn_aggr(moments[:, t, :], stats[:, t, :]))
            E.after("act", last, eps_set)
            root = E.done("act", act.activation(deviation[:, :], moments[:, :, 1], ACT.Sqrt, bias=eps[:, 0:1]))
            E.after("dve", root)
            ready_rstd = E.done("dve", dve.reciprocal(rstd[:, :], deviation[:, :]))
            E.after("dve", ready_rstd)
            return ready_rstd

        def norm_apply(dst, src):
            return [E.done("dve", dve.tensor_scalar(dst[:, t, :], src[:, t, :], moments[:, t, 0:1],
                                                    rstd[:, t:t + 1], ALU.subtract, ALU.mult))
                    for t in range(n_tiles)]

        def both(lane):
            return psum[:, 2 * lane:2 * lane + 2, :]

        def separate(g, dst, src, ready):
            n = src.shape[1]
            E.after("pool", ready)
            return E.done("pool", pool.tensor_tensor(dst, src.unsqueeze(1).broadcast_to([P, 4, n]), bc(head_mask[:, 4 * g:4 * g + 4], n), ALU.mult))

        def diagonal(t):
            flat = t.rearrange("p j c -> p (j c)")
            return bass.AP(flat.tensor, flat.offset, [flat.ap[0], [32 + HD_A, 4], [1, HD_A]])

        lane_free = [None] * LANES

        def transposed_input(lane, b, dst):
            bank = psum[:, 2 * lane, :]
            for i in range(TPS):
                mm = pe.transpose(bank[:, i * P:(i + 1) * P], stream[:, TPS * b + i, :], ident[:, :])
            turned = E.done("pe", mm)
            yield "act", turned
            return turned, E.done("act", act.activation(dst, bank[:, 0:SEQ], ACT.Copy))

        with ExitStack() as a:
            wq = sb(a, "a_wq", [P, P])
            wk = sb(a, "a_wk", [P, P])
            wv = sb(a, "a_wv", [P, P])
            bq = sb(a, "a_bq", [P, 1])
            bk = sb(a, "a_bk", [P, 1])
            bv = sb(a, "a_bv", [P, P])
            for dst, src in ((wq[:, :], "a_wq"), (wk[:, :], "a_wk"), (wv[:, :], "a_wv"),
                             (bq[:, :], "a_bq"), (bk[:, :], "a_bk"), (bv[:, :], "a_bv"),
                             (head_mask[:, :], "head_mask")):
                loaded = E.dma("load_a", dst, io[src])
            kern2 = sb(a, "kern2", [P, n_seq * HEADS_A, P])
            colsum = sb(a, "colsum", [1, n_seq * QUADS])
            inv_c = sb(a, "inv_c", [P, 1])
            peak_one = sb(a, "peak_one", [1, 1])
            raw = [sb(a, f"a_raw{n}", [P, 8, P]) for n in range(LANES)]
            turn = [sb(a, f"a_turn{n}", [P, 8 * (P + HD_A)]) for n in range(LANES)]
            feat = [t[:, 4 * P:4 * P + SEQ] for t in turn]
            state = [sb(a, f"a_state{n}", [P, 4, P + HD_A]) for n in range(LANES)]
            q_t = [sb(a, f"a_q{n}", [P, SEQ]) for n in range(LANES)]
            k_all = [sb(a, f"a_k{n}", [P, SEQ]) for n in range(LANES)]
            q_lm = [sb(a, f"a_qlm{n}", [P, P]) for n in range(LANES)]
            k_lm = [sb(a, f"a_klm{n}", [P, P]) for n in range(LANES)]
            small = [sb(a, f"a_small{n}", [P, 48]) for n in range(LANES)]
            apart = [sb(a, f"a_apart{n}", [P, TPS, 4, 32]) for n in range(LANES)]
            for n in range(LANES):
                apart_zero = E.done("dve", dve.memset(apart[n][:, :, :, :], 0.0))

            MW = P + HD_A

            x_ready = []
            for g in range(0, n_tiles, TG):
                x_ready += [E.dma(f"load_x{g}", stream[:, g:g + TG, :], x_dram[:, g:g + TG, :])] * TG
            norm_stats(stream, x_ready)
            normed = norm_apply(stream, stream)

            root_scale = 1.0 / math.sqrt(math.sqrt(HD_A))
            E.after("dve", loaded)
            dve.tensor_scalar(bq[:, :], bq[:, :], root_scale, None, ALU.mult)
            scaled_bias = E.done("dve", dve.tensor_scalar(bk[:, :], bk[:, :], root_scale, None, ALU.mult))
            E.after("act", scaled_bias)
            E.after("pool", loaded)

            def softmax_rows(lane, banks, n_rows, width, scale, dst, maxes, negs, sums, scored):
                yield "dve", scored
                peaked = E.done("dve", dve.tensor_reduce(out=maxes, in_=banks, axis=AX.X, op=ALU.max))
                E.after("dve", peaked)
                negated = E.done("dve", dve.tensor_scalar(negs, maxes, -scale, None, ALU.mult))
                yield "act", negated
                for r in range(n_rows):
                    mark = E.done("act", act.activation(dst[:, r, :], banks[:, r, :], ACT.Exp, bias=negs[:, r:r + 1],
                                                        scale=scale, accum_out=sums[:, r:r + 1]))
                return mark

            def kernel2_task(b):
                def steps(lane):
                    b0, b1 = psum[:, 2 * lane, :], psum[:, 2 * lane + 1, :]
                    lm = raw[lane][:, 0, :]
                    kk_sep = raw[lane][:, 4:8, :]
                    expd = turn[lane][:, 0:4 * P].rearrange("p (j m) -> p j m", j=4)
                    sm = small[lane]
                    maxes, negs, sums, inv = sm[:, 0:4], sm[:, 4:8], sm[:, 8:12], sm[:, 12:16]
                    yield normed[TPS * b + TPS - 1], lane_free[lane]
                    turned, copied = yield from transposed_input(lane, b, feat[lane])
                    yield "dve", copied
                    pairs = feat[lane].rearrange("p (m s) -> p m s", s=2)
                    summed = E.done("dve", dve.tensor_tensor(lm, pairs[:, :, 0], pairs[:, :, 1], ALU.add))
                    yield summed,
                    pe.matmul(b0[:, 0:P], wq[:, :], lm, start=True, stop=True)
                    projected = E.done("pe", pe.matmul(b0[:, P:2 * P], wk[:, :], lm, start=True, stop=True))
                    yield "act", projected
                    E.done("act", act.activation(q_lm[lane][:, :], b0[:, 0:P], ACT.Identity, bias=bq[:, 0:1], scale=0.5 * root_scale))
                    kk_ready = E.done("act", act.activation(k_lm[lane][:, :], b0[:, P:2 * P], ACT.Identity, bias=bk[:, 0:1], scale=0.5 * root_scale))
                    ready = separate(0, kk_sep, k_lm[lane][:, :], kk_ready)
                    for g in range(QUADS):
                        yield kk_ready, ready, lane_free[lane]
                        scored = E.done("pe", pe.matmul(b1, q_lm[lane][:, :], kk_sep, start=True, stop=True))
                        if g < QUADS - 1:
                            ready = separate(g + 1, kk_sep, k_lm[lane][:, :], scored)
                        scores = b1.rearrange("p (j m) -> p j m", j=4)
                        expd_all = yield from softmax_rows(lane, scores, 4, P, 1.0, expd, maxes, negs, sums, scored)
                        yield "dve", expd_all
                        inverted = E.done("dve", dve.reciprocal(inv, sums))
                        E.after("dve", inverted)
                        h0 = HEADS_A * b + 4 * g
                        normalized = E.done("dve", dve.tensor_tensor(kern2[:, h0:h0 + 4, :], expd, bc(inv, P), ALU.mult))
                        yield normalized,
                        sums_ready = E.done("pe", pe.matmul(b0[0:1, :], ones[:, 0:1], kern2[:, h0:h0 + 4, :], start=True, stop=True))
                        yield "dve", sums_ready
                        n = QUADS * b + g
                        lane_free[lane] = last_colsum[0] = E.done("dve", dve.tensor_reduce(out=colsum[:, n:n + 1], in_=b0[0:1, :], axis=AX.X, op=ALU.max))
                return steps

            last_colsum = [None]
            E.in_lanes([kernel2_task(b) for b in range(n_seq)])

            E.after("dve", last_colsum[0])
            peaked = E.done("dve", dve.tensor_reduce(out=peak_one[:, :], in_=colsum[:, :], axis=AX.X, op=ALU.max))
            E.barrier()
            spread = E.done("pe", pe.matmul(psum[:, 1, 0:1], ones[0:1, :], peak_one[:, :], start=True, stop=True))
            E.after("dve", spread)
            c_ready = E.done("dve", dve.reciprocal(inv_c[:, :], psum[:, 1, 0:1]))
            E.barrier()

            BETA = 2.75 / 13.0

            def nystrom_task(b):
                def steps(lane):
                    b0, b1, two = psum[:, 2 * lane, :], psum[:, 2 * lane + 1, :], both(lane)
                    st, sm, k_t = state[lane], small[lane], k_all[lane][:, :]
                    halves = lambda bank: bank.rearrange("p (j m) -> p j m", j=4)
                    here = stream[:, TPS * b:TPS * b + TPS, :]
                    v_wide = apart[lane][:, :, :, :]
                    z_wide, w_wide = apart[lane][:, 0, :, :], apart[lane][:, 1, :, :]
                    rows_ = raw[lane][0:32, 4:6, :].rearrange("p r m -> p (r m)")
                    yield lane_free[lane],
                    turned, copied = yield from transposed_input(lane, b, feat[lane])
                    yield copied,
                    pe.matmul(b0[:, 0:SEQ], wq[:, :], feat[lane], start=True, stop=True)
                    pe.matmul(b0[:, SEQ:2 * SEQ], wk[:, :], feat[lane], start=True, stop=True)
                    for i in range(TPS):
                        mm = pe.matmul(b1[:, P * i:P * (i + 1)], feat[lane][:, i * P:(i + 1) * P], wv[:, :], start=True, stop=True)
                    projected = E.done("pe", mm)
                    yield "act", projected
                    E.done("act", act.activation(q_t[lane][:, :], b0[:, 0:SEQ], ACT.Identity, bias=bq[:, 0:1], scale=root_scale))
                    qk_ready = E.done("act", act.activation(k_t, b0[:, SEQ:2 * SEQ], ACT.Identity, bias=bk[:, 0:1], scale=root_scale))
                    E.after("dve", projected)
                    v_all = E.done("dve", dve.tensor_tensor(here, b1[:, 0:SEQ].rearrange("p (i c) -> p i c", i=TPS),
                                                            bv[:, :].unsqueeze(1).broadcast_to([P, TPS, P]), ALU.add))
                    yield "dve", qk_ready
                    q2 = q_t[lane][:, :].rearrange("p (m s) -> p m s", s=2)
                    k2 = k_t.rearrange("p (m s) -> p m s", s=2)
                    dve.tensor_tensor(q_lm[lane][:, :], q2[:, :, 0], q2[:, :, 1], ALU.add)
                    lm_ready = E.done("dve", dve.tensor_tensor(k_lm[lane][:, :], k2[:, :, 0], k2[:, :, 1], ALU.add))
                    lane_free[lane] = lm_ready
                    for g in range(QUADS):
                        h0 = HEADS_A * b + 4 * g
                        head = lambda j: kern2[:, h0 + j, :]
                        E.after("dve", v_all)
                        for i in range(TPS):
                            v_ready = E.done("dve", dve.tensor_copy(
                                diagonal(v_wide[:, i, :, :]), here[:, i, 32 * g:32 * g + 32].rearrange("p (j d) -> p j d", j=4)))
                        q_sep = turn[lane][:, 0:4 * P].rearrange("p (j m) -> p j m", j=4)
                        sep_ready = separate(g, q_sep, q_lm[lane][:, :], lane_free[lane])
                        yield sep_ready,
                        for j in range(4):
                            mm = pe.matmul(two[:, j // 2, SEQ * (j % 2):SEQ * (j % 2) + SEQ], q_sep[:, j, :], k_t,
                                           start=True, stop=True)
                        scored = E.done("pe", mm)
                        maxes, negs, sums3, inv3 = sm[:, 0:4], sm[:, 4:8], sm[:, 8:12], sm[:, 12:16]
                        expd3 = raw[lane][:, :, :].rearrange("p (j i) m -> p j (i m)", i=TPS)
                        exped = yield from softmax_rows(lane, two.rearrange("p k (j m) -> p (k j) m", j=2), 4, SEQ, 0.5, expd3,
                                             maxes, negs, sums3, scored)
                        yield "dve", exped
                        inv3_ready = E.done("dve", dve.reciprocal(inv3, sums3))
                        yield exped,
                        for i in range(TPS):
                            for j in range(4):
                                mm = pe.transpose(two[:, i, j * P:(j + 1) * P], raw[lane][:, TPS * j + i, :], ident[:, :])
                        turned = E.done("pe", mm)
                        turn3 = turn[lane][:, 0:8 * P].rearrange("p (i c) -> p i c", i=TPS)
                        yield "act", turned
                        half0 = E.done("act", act.activation(turn3[:, 0, :], b0[:, :], ACT.Copy))
                        E.after("dve", turned)
                        half1 = E.done("dve", dve.tensor_copy(turn3[:, 1, :], b1[:, :]))
                        yield half0, half1, v_ready
                        for i in range(TPS):
                            for j in range(4):
                                mm = pe.matmul(b0[0:32, 0:P], v_wide[:, i, j, :], turn3[:, i, j * P:(j + 1) * P],
                                               start=(i == 0 and j == 0), stop=(i == TPS - 1 and j == 3))
                        y_raw = E.done("pe", mm)
                        for j in range(4):
                            mm = pe.transpose(b1[:, j * P:(j + 1) * P], head(j), ident[:, :])
                        turned = E.done("pe", mm)
                        yield "dve", y_raw
                        y_rows = E.done("dve", dve.tensor_copy(rows_[:, 0:P], b0[0:32, 0:P]))
                        E.after("act", turned)
                        k2t_ready = E.done("act", act.activation(raw[lane][:, 0:4, :], halves(b1), ACT.Copy))
                        yield k2t_ready, y_rows,
                        y_turned = E.done("pe", pe.transpose(b1[:, 0:32], rows_[:, 0:P], ident[0:32, 0:32]))
                        for j in range(4):
                            mm = pe.matmul(b0[:, j * P:(j + 1) * P], raw[lane][:, j, :], raw[lane][:, j, :], start=True, stop=True)
                        squared = E.done("pe", mm)
                        E.after("dve", y_turned, inv3_ready)
                        y_ready = E.done("dve", dve.tensor_tensor(st[:, :, P:MW], b1[:, 0:32].rearrange("p (j d) -> p j d", j=4),
                                                                  bc(inv3, HD_A), ALU.mult))
                        E.after("act", squared, c_ready)
                        state_ready = E.done("act", act.activation(st[:, :, 0:P], halves(b0), ACT.Copy, scale=inv_c[:, 0:1]))
                        yield state_ready, y_ready
                        s = 1.0
                        n4 = 4 * MW
                        bu = turn[lane][:, 0:n4].rearrange("p (j c) -> p j c", j=4)
                        diff = raw[lane][:, :, :].rearrange("p r m -> p (r m)")[:, 0:n4].rearrange("p (j c) -> p j c", j=4)
                        lin = turn[lane][:, n4:2 * n4].rearrange("p (j c) -> p j c", j=4)
                        pairs_of = lambda t: t.rearrange("p (k j) c -> p k (j c)", k=2)
                        out_of = lambda j: two[:, j // 2, MW * (j % 2):MW * (j % 2) + MW]
                        for k in range(ITERS):
                            for j in range(4):
                                mm = pe.matmul(out_of(j), st[:, j, 0:P], st[:, j, :], start=True, stop=True)
                            produced = E.done("pe", mm)
                            yield "act", produced
                            bu_ready = E.done("act", act.activation(pairs_of(bu), two[:, :, 0:2 * MW], ACT.Copy, scale=BETA / s))
                            E.after("dve", bu_ready, y_ready)
                            diff_ready = E.done("dve", dve.scalar_tensor_tensor(out=diff, in0=st[:, :, :], scalar=-3.5 * BETA,
                                                                                in1=bu, op0=ALU.mult, op1=ALU.add))
                            E.after("pool", bu_ready, y_ready, state_ready)
                            lin_ready = E.done("pool", pool.tensor_tensor(lin, st[:, :, :], bu, ALU.subtract))
                            yield diff_ready,
                            for j in range(4):
                                mm = pe.matmul(out_of(j), diff[:, j, 0:P], diff[:, j, :], start=True, stop=True)
                            produced = E.done("pe", mm)
                            yield "dve", produced, lin_ready
                            if k < ITERS - 1:
                                state_ready = E.done("dve", dve.scalar_tensor_tensor(
                                    out=pairs_of(st[:, :, :]), in0=two[:, :, 0:2 * MW], scalar=-1.0 / (13.0 * BETA * BETA * s), in1=pairs_of(lin),
                                    op0=ALU.mult, op1=ALU.add))
                                y_ready = state_ready
                            else:
                                for q in range(2):
                                    z_ready = E.done("dve", dve.scalar_tensor_tensor(
                                        out=diagonal(z_wide)[:, 2 * q:2 * q + 2, :], scalar=-1.0 / (13.0 * BETA * BETA * s), op0=ALU.mult, op1=ALU.add,
                                        in0=two[:, q, 0:2 * MW].rearrange("p (j c) -> p j c", j=2)[:, :, P:MW],
                                        in1=lin[:, 2 * q:2 * q + 2, P:MW]))
                                y_ready = state_ready = z_ready
                            s *= 4.0 / 13.0
                            yield state_ready,
                        for j in range(4):
                            mm = pe.matmul(b1[0:32, 0:P], z_wide[:, j, :], head(j), start=(j == 0), stop=(j == 3))
                        produced = E.done("pe", mm)
                        yield "dve", produced, c_ready
                        w_rows = E.done("dve", dve.tensor_scalar(rows_[:, 0:P], b1[0:32, 0:P], inv_c[0:32, 0:1], 1.0 / s, ALU.mult, ALU.mult))
                        k_sep = turn[lane][:, 0:4 * P].rearrange("p (j m) -> p j m", j=4)
                        sep_ready = separate(g, k_sep, k_lm[lane][:, :], [z_ready, lm_ready])
                        yield w_rows,
                        turned = E.done("pe", pe.transpose(b0[:, 0:32], rows_[:, 0:P], ident[0:32, 0:32]))
                        yield "dve", turned
                        w_ready = E.done("dve", dve.tensor_copy(diagonal(w_wide), b0[:, 0:32].rearrange("p (j d) -> p j d", j=4)))
                        yield w_ready, sep_ready,
                        for i in range(TPS):
                            mm = pe.matmul(two[:, i, :], q_t[lane][:, i * P:(i + 1) * P], k_sep, start=True, stop=True)
                        scored = E.done("pe", mm)
                        maxes1, negs1, sums1, inv1 = sm[:, 16:24], sm[:, 24:32], sm[:, 32:40], sm[:, 40:48]
                        exped = yield from softmax_rows(lane, two.rearrange("p k (j m) -> p (k j) m", j=4), 8, P, 0.5, raw[lane],
                                             maxes1, negs1, sums1, scored)
                        yield "dve", exped
                        inv1_ready = E.done("dve", dve.reciprocal(inv1, sums1))
                        yield exped,
                        for r in range(8):
                            mm = pe.transpose(two[:, r // 4, (r % 4) * P:(r % 4 + 1) * P], raw[lane][:, r, :], ident[:, :])
                        turned = E.done("pe", mm)
                        turn1 = turn[lane][:, 0:8 * P].rearrange("p (i c) -> p i c", i=TPS)
                        yield "act", turned
                        half0 = E.done("act", act.activation(turn1[:, 0, :], b0[:, :], ACT.Copy))
                        E.after("dve", turned)
                        half1 = E.done("dve", dve.tensor_copy(turn1[:, 1, :], b1[:, :]))
                        yield half0, half1,
                        for i in range(TPS):
                            for j in range(4):
                                mm = pe.matmul(b0[0:32, i * P:(i + 1) * P], w_wide[:, j, :], turn1[:, i, j * P:(j + 1) * P],
                                               start=(j == 0), stop=(j == 3))
                        produced = E.done("pe", mm)
                        yield "act", produced
                        x_rows = E.done("act", act.activation(rows_, b0[0:32, 0:SEQ], ACT.Copy))
                        yield x_rows,
                        for i in range(TPS):
                            mm = pe.transpose(b1[:, 32 * i:32 * i + 32], rows_[:, i * P:(i + 1) * P], ident[0:32, 0:32])
                        produced = E.done("pe", mm)
                        yield "dve", produced, inv1_ready, v_ready
                        out_view = stream[:, TPS * b:TPS * b + TPS, 32 * g:32 * g + 32].rearrange("p i (j d) -> p i j d", d=HD_A)
                        lane_free[lane] = written[b, g] = E.done("dve", dve.tensor_tensor(
                            out_view, b1[:, 0:64].rearrange("p (i j d) -> p i j d", i=TPS, j=4),
                            bc(inv1.rearrange("p (i j) -> p i j", i=TPS), HD_A), ALU.mult))
                return steps

            written = {}
            E.in_lanes([nystrom_task(b) for b in range(n_seq)])
            block_out = [[written[t // TPS, g] for g in range(QUADS)] for t in range(n_tiles)]
            E.barrier()

        wqkv = [sb(top, f"b_wqkv{n}", [P, 3 * INNER]) for n in range(2)]
        wo = [sb(top, f"b_wo{n}", [P, INNER // P, P]) for n in range(2)]
        rope = [sb(top, f"b_rope{n}", [P, 4, TPS, HD_B]) for n in range(2)]
        band = sb(top, "b_band", [P, KEYS])
        minus_half = sb(top, "minus_half", [P, 2 * HEADS_B])
        f_w1 = [sb(top, f"f_w1{n}", [P, 2 * HID]) for n in range(2)]
        f_w2 = [sb(top, f"f_w2{n}", [P, 3, P]) for n in range(2)]
        f_b1 = [sb(top, f"f_b1{n}", [P, 2, 3]) for n in range(2)]
        f_b2 = [sb(top, f"f_b2{n}", [P, P]) for n in range(2)]
        f_g = [sb(top, f"f_g{n}", [P, 1]) for n in range(2)]
        f_b = [sb(top, f"f_b{n}", [P, 1]) for n in range(2)]
        c_wq, c_wk = sb(top, "c_wq", [P, P]), sb(top, "c_wk", [P, P])
        c_wv = sb(top, "c_wv", [P, P])
        c_bias = sb(top, "c_bias", [P, HEADS_A, KEYS])
        d_wg, d_bg, d_order = (sb(top, f"d_{n}", [P, EXPERTS]) for n in ("wg", "bg", "order"))
        d_w1 = sb(top, "d_w1", [P, EXPERTS * RANK])
        d_w2 = sb(top, "d_w2", [P, EXPERTS * RANK // P, P])
        x_buf = [sb(top, f"x{n}", [P, TPS, P]) for n in range(LANES)]
        feats = [sb(top, f"feat{n}", [P, SEQ]) for n in range(LANES)]
        work = [sb(top, f"work{n}", [P, 3, TPS * INNER]) for n in range(LANES)]
        four = [sb(top, f"four{n}", [P, HEADS_B // 2, SEQ]) for n in range(LANES)]
        eight = [sb(top, f"eight{n}", [P, 2, HEADS_B // 2, SEQ]) for n in range(LANES)]
        small = [sb(top, f"small{n}", [P, 128]) for n in range(LANES)]

        gain = [sb(top, f"b_gain{n}", [P, 4, HD_B]) for n in range(2)]
        slope, rel, causal = sb(top, "c_slope", [P, HEADS_A]), sb(top, "c_rel", [P, KEYS]), sb(top, "c_causal", [P, KEYS])
        loaded = []
        for n in range(2):
            if n == 0:
                band_loaded = E.dma("load_band", band[:, :], io["b_band"])
            for dst, src in ((wqkv[n][:, :], "b_wqkv"), (rope[n][:, :, :, :], None), (gain[n][:, :, :], "b_gain"),
                             (wo[n][:, :, :], "b_wo"), (f_w1[n][:, :], "f_w1"), (f_w2[n][:, :, :], "f_w2"),
                             (f_b1[n][:, :, :], "f_b1"), (f_b2[n][:, :], "f_b2"), (f_g[n][:, :], "f_g"), (f_b[n][:, :], "f_b")):
                layer_loaded = E.dma(f"load_b{n}", dst, io[src][n] if src else io["b_rope"])
            loaded.append([layer_loaded, band_loaded])
        for dst, src in ((slope[:, :], "c_slope"), (rel[:, :], "c_rel"), (causal[:, :], "c_causal"), (c_wq[:, :], "c_wq"),
                         (c_wk[:, :], "c_wk"), (c_wv[:, :], "c_wv"), (d_wg[:, :], "d_wg"), (d_bg[:, :], "d_bg"),
                         (d_order[:, :], "d_order"), (d_w1[:, :], "d_w1"), (d_w2[:, :, :], "d_w2")):
            loaded_cd = E.dma("load_cd", dst, io[src])
        half_set = E.done("dve", dve.memset(minus_half[:, :], -0.5))
        apart = [sb(top, f"apart{n}", [P, TPS, 4, 32]) for n in range(LANES)]
        for n in range(LANES):
            E.done("dve", dve.memset(apart[n][:, :, :, :], 0.0))
            zeros_set = E.done("pool", pool.memset(eight[n][:, :, :, :], 0.0))
        E.after("act", zeros_set)
        E.after("dve", ("dve", E.count["dve"]))
        E.after("pool", half_set)

        def needs(*marks):
            for name in ("pe", "act", "dve", "pool"):
                E.after(name, *marks)

        def rope_table(n):
            E.after("dve", loaded[n])
            return E.done("dve", dve.tensor_tensor(rope[n][:, :, :, :], rope[n][:, :, :, :],
                                                   gain[n][:, :, :].unsqueeze(2).broadcast_to([P, 4, TPS, HD_B]), ALU.mult))

        def bias_table(heads):
            E.after("dve", loaded_cd)
            for h in heads:
                mark = E.done("dve", dve.scalar_tensor_tensor(out=c_bias[:, h, :], in0=rel[:, :], scalar=slope[:, h:h + 1],
                                                              in1=causal[:, :], op0=ALU.mult, op1=ALU.add))
            return mark

        tabled = {}

        def normalized(dst, src, sm, ready):
            stats_, mv, var, rs = (sm[:, 64:76].rearrange("p (i s) -> p i s", i=TPS), sm[:, 76:80].rearrange("p (i s) -> p i s", i=TPS),
                                   sm[:, 80:82], sm[:, 82:84])
            yield "dve", ready
            for i in range(TPS):
                mark = E.done("dve", dve.bn_stats(stats_[:, i, :], src[:, i, :]))
            E.after("dve", mark)
            for i in range(TPS):
                mark = E.done("dve", dve.bn_aggr(mv[:, i, :], stats_[:, i, :]))
            E.after("dve", mark)
            mark = E.done("dve", dve.tensor_scalar(var, mv[:, :, 1], LN_EPS, None, ALU.add))
            E.after("pool", mark)
            mark = E.done("pool", pool.tensor_tensor(rs, var, minus_half[:, 0:TPS], ALU.pow))
            yield "dve", mark
            for i in range(TPS):
                mark = E.done("dve", dve.tensor_scalar(dst[:, i, :], src[:, i, :], mv[:, i, 0:1], rs[:, i:i + 1], ALU.subtract, ALU.mult))
            return mark

        def residual(x, here, sm, ready):
            mark = yield from normalized(here, here, sm, ready)
            E.after("dve", mark)
            return E.done("dve", dve.tensor_tensor(x, x, here, ALU.add))

        def turn_input(lane, src, ready, shift):
            yield ready,
            bank, dst = psum[:, 2 * lane, :], feats[lane]
            for i in range(TPS):
                mm = pe.transpose(bank[:, i * P:(i + 1) * P], src[:, i, :], ident[:, :])
            turned = E.done("pe", mm)
            yield "act", turned
            if shift:
                E.done("act", act.activation(dst[0:64, :], bank[0:64, 0:SEQ], ACT.Copy))
                return E.done("act", act.activation(dst[64:P, 1:SEQ], bank[64:P, 0:SEQ - 1], ACT.Copy))
            return E.done("act", act.activation(dst[:, :], bank[:, 0:SEQ], ACT.Copy))

        def soft_scores(lane, q_of, k_of, bias_of, scale, ex, et, sm, sums, first, weighted):
            two = both(lane)
            for h in range(2):
                pe.matmul(two[:, h, 0:P], q_of(h, 0), k_of(h)[:, 0:P], start=True, stop=True)
                mm = pe.matmul(two[:, h, P + first:KEYS], q_of(h, 1), k_of(h)[:, first:SEQ], start=True, stop=True)
            scored = E.done("pe", mm)
            yield "dve", scored
            maxes, negs, inv = sm[:, 0:4], sm[:, 4:8], sm[:, 8:12]
            spans = [(0, P), (P + first, KEYS)]
            for h in range(2):
                for i, (lo, hi) in enumerate(spans):
                    r = TPS * h + i
                    mark = E.done("dve", dve.tensor_tensor_reduce(
                        out=ex[:, h, lo:hi], in0=two[:, h, lo:hi], in1=bias_of(h)[:, lo:hi], scale=1.0, scalar=LOWEST,
                        op0=ALU.add, op1=ALU.max, accum_out=maxes[:, r:r + 1]))
            E.after("dve", mark)
            negated = E.done("dve", dve.tensor_scalar(negs, maxes, -scale, None, ALU.mult))
            yield "act", negated
            ready = []
            for h in range(2):
                for i, (lo, hi) in enumerate(spans):
                    r = TPS * h + i
                    exped = E.done("act", act.activation(ex[:, h, lo:hi], ex[:, h, lo:hi], ACT.Exp, bias=negs[:, r:r + 1],
                                                         scale=scale, accum_out=sums[:, i, h:h + 1]))
                if weighted:
                    yield "dve", exped
                    invs = E.done("dve", dve.reciprocal(inv[:, TPS * h:TPS * h + TPS], sums[:, :, h]))
                    name = ("pool", "dve")[h]
                    E.after(name, invs)
                    for i, (lo, hi) in enumerate(spans):
                        exped = E.done(name, E.queues[name].tensor_scalar(ex[:, h, lo:hi], ex[:, h, lo:hi],
                                                                          inv[:, TPS * h + i:TPS * h + i + 1], None, ALU.mult))
                ready.append(exped)
            yield ready
            for h in range(2):
                for c in range(3):
                    mm = pe.transpose(two[:, h, c * P:(c + 1) * P], ex[:, h, c * P:(c + 1) * P], ident[:, :])
            turned = E.done("pe", mm)
            yield "act", turned
            half0 = E.done("act", act.activation(et[:, 0, :], two[:, 0, 0:KEYS], ACT.Copy))
            E.after("dve", turned)
            half1 = E.done("dve", dve.tensor_copy(et[:, 1, :], two[:, 1, 0:KEYS]))
            return [half0, half1]

        def local_attention(lane, layer, here, ready):
            b0, two, sm, hT = psum[:, 2 * lane, :], both(lane), small[lane], feats[lane]
            x_, t1, t2 = (work[lane][:, n, :].rearrange("p (i c) -> p i c", i=TPS) for n in range(3))
            v_sb = t2
            q_t, k_sep = four[lane], eight[lane]
            o_t = q_t
            shifted = yield from turn_input(lane, here, ready, True)
            yield shifted,

            def project(kind):
                for i in range(TPS):
                    mm = pe.matmul(two[:, i, :], hT[:, i * P:(i + 1) * P], wqkv[layer][:, kind * INNER:(kind + 1) * INNER],
                                   start=True, stop=True)
                return E.done("pe", mm)

            for kind in range(2):
                produced = project(kind)
                yield "act", produced
                copied = E.done("act", act.activation(x_, two, ACT.Copy))
                E.after("act", copied)
                squared = E.done("act", act.activation(t1, x_, ACT.Square))
                by_head = lambda t: t.rearrange("p i (h d) -> p i h d", d=HD_B)
                cos = rope[layer][:, 2 * kind, :, :].unsqueeze(2).broadcast_to([P, TPS, HEADS_B, HD_B])
                sin = rope[layer][:, 2 * kind + 1, :, :].unsqueeze(2).broadcast_to([P, TPS, HEADS_B, HD_B])
                hh = HD_B // 2
                E.after("pool", copied)
                pool.tensor_tensor(by_head(t2)[:, :, :, 0:hh], by_head(x_)[:, :, :, hh:], sin[:, :, :, 0:hh], ALU.mult)
                sined = E.done("pool", pool.tensor_tensor(by_head(t2)[:, :, :, hh:], by_head(x_)[:, :, :, 0:hh],
                                                          sin[:, :, :, hh:], ALU.mult))
                ss, rn = sm[:, 16:32], sm[:, 32:48]
                heads = lambda t: t.rearrange("p i (h d) -> p (i h) d", d=HD_B)
                yield "dve", squared
                ssed = E.done("dve", dve.tensor_reduce(out=ss, in_=heads(t1), axis=AX.X, op=ALU.add))
                E.after("dve", ssed)
                clipped = E.done("dve", dve.tensor_scalar(ss, ss, 1e-24, None, ALU.max))
                E.after("pool", clipped)
                inv_norm = E.done("pool", pool.tensor_tensor(rn, ss, minus_half[:, :], ALU.pow))
                cosed = E.done("dve", dve.tensor_tensor(by_head(t1), by_head(x_), cos, ALU.mult))
                yield "dve", cosed, sined
                roped = E.done("dve", dve.tensor_tensor(x_, t1, t2, ALU.add))
                E.after("dve", roped, inv_norm)
                roped = E.done("dve", dve.tensor_tensor(heads(x_), heads(x_), bc(rn, HD_B), ALU.mult))
                yield roped,
                for i in range(TPS):
                    for c in range(4):
                        mm = pe.transpose(two[:, i, c * P:(c + 1) * P], x_[:, i, c * P:(c + 1) * P], ident[:, :])
                turned = E.done("pe", mm)
                yield "act", turned
                by_pair = lambda t: t.rearrange("p c (i t) -> p i c t", i=TPS)
                source = two.rearrange("p i (c t) -> p i c t", c=4)
                if kind == 0:
                    copied = E.done("act", act.activation(by_pair(q_t[:, :, :]), source, ACT.Copy))
                else:
                    for h in range(2):
                        half = slice(64 * h, 64 * h + 64)
                        copied = E.done("act", act.activation(by_pair(k_sep[half, h, :, :]), source[half], ACT.Copy))
                yield copied,
            produced = project(2)
            yield "act", produced, roped
            v_ready = E.done("act", act.activation(v_sb, two, ACT.Copy))
            yield v_ready,
            ex, et = (work[lane][:, n, 0:2 * KEYS].rearrange("p (h k) -> p h k", h=2) for n in range(2))
            sums = sm[:, 12:16].rearrange("p (i h) -> p i h", i=TPS)
            E.after("pool", turned)
            gap_zeroed = E.done("pool", pool.memset(ex[:, :, P:2 * P - WIN], 0.0))
            yield gap_zeroed,
            for c in range(HEADS_B // 2):
                halves = yield from soft_scores(
                    lane, lambda h, i: q_t[:, c, i * P:(i + 1) * P], lambda h: k_sep[:, h, c, :],
                    lambda h: band[:, :], 8.0, ex, et, sm, sums, P - WIN, True)
                yield halves
                for h in range(2):
                    v_of = lambda i: v_sb[:, i, c * P + 64 * h:c * P + 64 * h + 64]
                    pe.matmul(two[0:64, h, 0:SEQ], v_of(0), et[:, h, 0:SEQ], start=True, stop=False)
                    mm = pe.matmul(two[0:64, h, P:SEQ], v_of(1), et[:, h, SEQ:KEYS], start=False, stop=True)
                produced = E.done("pe", mm)
                yield "act", produced
                half0 = E.done("act", act.activation(o_t[0:64, c, :], two[0:64, 0, 0:SEQ], ACT.Copy))
                E.after("dve", produced)
                half1 = E.done("dve", dve.tensor_copy(o_t[64:P, c, :], two[0:64, 1, 0:SEQ]))
                yield half0, half1
            for i in range(TPS):
                for c in range(4):
                    mm = pe.matmul(b0[:, i * P:(i + 1) * P], o_t[:, c, i * P:(i + 1) * P], wo[layer][:, c, :],
                                   start=(c == 0), stop=(c == 3))
            produced = E.done("pe", mm)
            yield "dve", produced
            return E.done("dve", dve.tensor_tensor(here, here, b0[:, 0:SEQ].rearrange("p (i d) -> p i d", i=TPS), ALU.add))

        def feed_forward(lane, layer, here, ready):
            b0, b1, two, sm, hT = psum[:, 2 * lane, :], psum[:, 2 * lane + 1, :], both(lane), small[lane], feats[lane]
            h_tok = work[lane][:, 0, 0:SEQ].rearrange("p (i d) -> p i d", i=TPS)
            gate = work[lane][:, 1, 0:3 * SEQ].rearrange("p (c t) -> p c t", c=3)
            normed_t = work[lane][:, 2, 0:SEQ]
            chunks = [(0, P), (P, P), (2 * P, HID - 2 * P)]
            shifted = yield from turn_input(lane, here, ready, True)
            yield shifted,
            for i in range(TPS):
                mm = pe.transpose(b1[:, i * P:(i + 1) * P], hT[:, i * P:(i + 1) * P], ident[:, :])
            turned = E.done("pe", mm)
            yield "act", turned
            copied = E.done("act", act.activation(h_tok, b1[:, 0:SEQ].rearrange("p (i d) -> p i d", i=TPS), ACT.Copy))
            E.after("pool", turned)
            biased = E.done("pool", pool.tensor_tensor(here, here, f_b2[layer][:, :].unsqueeze(1).broadcast_to([P, TPS, P]), ALU.add))
            mark = yield from normalized(h_tok, h_tok, sm, copied)
            yield mark,
            for i in range(TPS):
                mm = pe.transpose(b0[:, i * P:(i + 1) * P], h_tok[:, i, :], ident[:, :])
            turned = E.done("pe", mm)
            yield "dve", turned
            scaled = E.done("dve", dve.tensor_scalar(normed_t, b0[:, 0:SEQ], f_g[layer][:, 0:1], f_b[layer][:, 0:1], ALU.mult, ALU.add))
            yield scaled,

            def chunk(c, part):
                lo, n = chunks[c]
                out = two[0:n, c // 2, (c % 2) * SEQ:(c % 2) * SEQ + SEQ]
                lo += part * HID
                return out, pe.matmul(out, f_w1[layer][:, lo:lo + n], normed_t, start=True, stop=True)

            outs = [chunk(c, 1) for c in range(3)]
            produced = E.done("pe", outs[-1][1])
            yield "act", produced
            for c, (lo, n) in enumerate(chunks):
                gated = E.done("act", act.activation(gate[0:n, c, :], outs[c][0], ACT.Gelu, bias=f_b1[layer][0:n, 1, c:c + 1]))
            yield gated,
            outs = [chunk(c, 0) for c in range(3)]
            produced = E.done("pe", outs[-1][1])
            yield "dve", produced, gated
            for c, (lo, n) in enumerate(chunks):
                used = E.done("dve", dve.scalar_tensor_tensor(out=gate[0:n, c, :], in0=outs[c][0], scalar=f_b1[layer][0:n, 0, c:c + 1],
                                                              in1=gate[0:n, c, :], op0=ALU.add, op1=ALU.mult))
            yield used,
            for i in range(TPS):
                for c, (lo, n) in enumerate(chunks):
                    mm = pe.matmul(b1[:, i * P:(i + 1) * P], gate[0:n, c, i * P:(i + 1) * P], f_w2[layer][0:n, c, :],
                                   start=(c == 0), stop=(c == 2))
            produced = E.done("pe", mm)
            yield "dve", produced, biased
            return E.done("dve", dve.tensor_tensor(here, here, b1[:, 0:SEQ].rearrange("p (i d) -> p i d", i=TPS), ALU.add))

        def causal_attention(lane, here, ready):
            b0, b1, two, sm, hT = psum[:, 2 * lane, :], psum[:, 2 * lane + 1, :], both(lane), small[lane], feats[lane]
            k_sep, v_wide = four[lane][:, :, :], apart[lane][:, :, :, :]
            q_t, k_t, rows_sb = (work[lane][0:n, i, 2 * KEYS:2 * KEYS + SEQ] for i, n in enumerate((P, P, 32)))
            ex = work[lane][:, 0, 0:2 * KEYS].rearrange("p (h k) -> p h k", h=2)
            exp_t = work[lane][:, 1:3, 0:2 * KEYS].rearrange("p n (h k) -> p n h k", h=2)
            turned = yield from turn_input(lane, here, ready, False)
            yield turned,
            for i in range(TPS):
                mm = pe.matmul(b0[:, P * i:P * (i + 1)], hT[:, i * P:(i + 1) * P], c_wv[:, :], start=True, stop=True)
            produced = E.done("pe", mm)
            yield "dve", produced
            v_all = E.done("dve", dve.tensor_copy(here, b0[:, 0:SEQ].rearrange("p (i c) -> p i c", i=TPS)))
            yield v_all,
            pe.matmul(b0[:, 0:SEQ], c_wq[:, :], hT[:, :], start=True, stop=True)
            projected = E.done("pe", pe.matmul(b0[:, SEQ:2 * SEQ], c_wk[:, :], hT[:, :], start=True, stop=True))
            yield "act", projected
            q_ready = E.done("act", act.activation(q_t, b0[:, 0:SEQ], ACT.Copy, scale=1.0 / math.sqrt(P)))
            k_ready = E.done("act", act.activation(k_t, b0[:, SEQ:2 * SEQ], ACT.Copy))
            written = None
            for g in range(QUADS):
                sep_ready = separate(g, k_sep, k_t, [k_ready, written])
                E.after("dve", v_all, written)
                for i in range(TPS):
                    v_ready = E.done("dve", dve.tensor_copy(
                        diagonal(v_wide[:, i, :, :]), here[:, i, 32 * g:32 * g + 32].rearrange("p (j d) -> p j d", j=4)))
                yield sep_ready,
                sums, inv = sm[:, 12:20].rearrange("p (i j) -> p i j", i=TPS), sm[:, 20:28]
                for c in range(2):
                    halves = yield from soft_scores(
                        lane, lambda h, i: q_t[:, i * P:(i + 1) * P], lambda h: k_sep[:, 2 * c + h, :],
                        lambda h: c_bias[:, 4 * g + 2 * c + h, :], 1.0, ex, exp_t[:, c, :, :], sm, sums[:, :, 2 * c:2 * c + 2], 0, False)
                    yield halves + [v_ready]
                for j in range(4):
                    e = exp_t[:, j // 2, j % 2, :]
                    pe.matmul(b0[0:32, 0:SEQ], v_wide[:, 0, j, :], e[:, 0:SEQ], start=(j == 0), stop=False)
                    mm = pe.matmul(b0[0:32, P:SEQ], v_wide[:, 1, j, :], e[:, SEQ:KEYS], start=False, stop=(j == 3))
                produced = E.done("pe", mm)
                yield "act", produced
                x_rows = E.done("act", act.activation(rows_sb, b0[0:32, 0:SEQ], ACT.Copy))
                E.after("dve", produced)
                inv_ready = E.done("dve", dve.reciprocal(inv, sm[:, 12:20]))
                yield x_rows,
                for i in range(TPS):
                    mm = pe.transpose(b1[:, 32 * i:32 * i + 32], rows_sb[:, i * P:(i + 1) * P], ident[0:32, 0:32])
                produced = E.done("pe", mm)
                yield "dve", produced, inv_ready
                out_view = here[:, :, 32 * g:32 * g + 32].rearrange("p i (j d) -> p i j d", d=HD_A)
                written = E.done("dve", dve.tensor_tensor(
                    out_view, b1[:, 0:64].rearrange("p (i j d) -> p i j d", i=TPS, j=4),
                    bc(inv.rearrange("p (i j) -> p i j", i=TPS), HD_A), ALU.mult))
                if g < QUADS - 1:
                    yield written,
            return written

        def experts(lane, here, ready):
            b0, b1, two, sm, hT = psum[:, 2 * lane, :], psum[:, 2 * lane + 1, :], both(lane), small[lane], feats[lane]
            hid, hid_t = (work[lane][:, n, :].rearrange("p (i c) -> p i c", i=TPS) for n in range(2))
            by_tile = lambda n: work[lane][:, 2, 16 * n:16 * n + 16].rearrange("p (i e) -> p i e", i=TPS)
            logits, gates, hot1, hot2, rest = (by_tile(n) for n in range(5))
            v1, v2, m_, gap, e_ = (work[lane][:, 2, 128 + TPS * n:128 + TPS * (n + 1)] for n in range(5))
            turned = yield from turn_input(lane, here, ready, False)
            yield turned,
            for i in range(TPS):
                mm = pe.matmul(b0[:, EXPERTS * i:EXPERTS * (i + 1)], hT[:, i * P:(i + 1) * P], d_wg[:, :], start=True, stop=True)
            produced = E.done("pe", mm)
            yield "dve", produced
            all_tiles = lambda t: t[:, :].unsqueeze(1).broadcast_to([P, TPS, EXPERTS])

            def step(instruction):
                mark = E.done("dve", instruction)
                E.after("dve", mark)
                return mark

            def one_hot(dst, values, v):
                step(dve.tensor_tensor(dst, values, bc(v, EXPERTS), ALU.is_equal))
                step(dve.tensor_tensor(dst, dst, all_tiles(d_order), ALU.mult))
                step(dve.tensor_reduce(out=m_, in_=dst, axis=AX.X, op=ALU.max))
                step(dve.tensor_tensor(dst, dst, bc(m_, EXPERTS), ALU.is_equal))

            read = step(dve.tensor_tensor(logits, b0[:, 0:TPS * EXPERTS].rearrange("p (i e) -> p i e", i=TPS), all_tiles(d_bg), ALU.add))
            step(dve.tensor_reduce(out=v1, in_=logits, axis=AX.X, op=ALU.max))
            one_hot(hot1, logits, v1)
            step(dve.scalar_tensor_tensor(out=rest, in0=hot1, scalar=LOWEST, in1=logits, op0=ALU.mult, op1=ALU.add))
            step(dve.tensor_reduce(out=v2, in_=rest, axis=AX.X, op=ALU.max))
            one_hot(hot2, rest, v2)
            gap_ready = step(dve.tensor_tensor(gap, v2, v1, ALU.subtract))
            E.after("act", gap_ready)
            e_ready = E.done("act", act.activation(e_, gap, ACT.Exp))
            E.after("dve", e_ready)
            step(dve.tensor_scalar(m_, e_, 1.0, None, ALU.add))
            step(dve.reciprocal(v1, m_))
            step(dve.tensor_tensor(v2, e_, v1, ALU.mult))
            step(dve.tensor_tensor(hot1, hot1, bc(v1, EXPERTS), ALU.mult))
            step(dve.tensor_tensor(hot2, hot2, bc(v2, EXPERTS), ALU.mult))
            step(dve.tensor_tensor(gates, hot1, hot2, ALU.add))
            yield read,
            for i in range(TPS):
                mm = pe.matmul(two[:, i, :], hT[:, i * P:(i + 1) * P], d_w1[:, :], start=True, stop=True)
            produced = E.done("pe", mm)
            yield "act", produced
            gelued = E.done("act", act.activation(hid, two, ACT.Gelu))
            E.after("dve", gelued)
            by_e = hid.rearrange("p i (e r) -> p i e r", r=RANK)
            weighted = E.done("dve", dve.tensor_tensor(by_e, by_e, bc(gates, RANK), ALU.mult))
            yield weighted,
            for i in range(TPS):
                for c in range(4):
                    mm = pe.transpose(two[:, i, c * P:(c + 1) * P], hid[:, i, c * P:(c + 1) * P], ident[:, :])
            turned = E.done("pe", mm)
            yield "dve", turned
            half1 = E.done("dve", dve.tensor_copy(hid_t[:, 1, :], two[:, 1, :]))
            E.after("act", turned)
            half0 = E.done("act", act.activation(hid_t[:, 0, :], two[:, 0, :], ACT.Copy))
            yield half0, half1
            for i in range(TPS):
                for c in range(4):
                    mm = pe.matmul(b0[:, i * P:(i + 1) * P], hid_t[:, i, c * P:(c + 1) * P], d_w2[:, c, :],
                                   start=(c == 0), stop=(c == 3))
            produced = E.done("pe", mm)
            yield "dve", produced
            return E.done("dve", dve.tensor_scalar(here, b0[:, 0:SEQ].rearrange("p (i d) -> p i d", i=TPS), 2.0, None, ALU.mult))

        stored = [None] * LANES

        def sequence_task(b):
            def steps(lane):
                x, here, sm = x_buf[lane][:, :, :], stream[:, TPS * b:TPS * b + TPS, :], small[lane]
                tiles = slice(TPS * b, TPS * b + TPS)
                E.after("sp", stored[lane])
                x_loaded = E.dma(f"load_x_lane{lane}", x, x_dram[:, tiles, :])

                added = yield from residual(x, here, sm, [block_out[TPS * b], x_loaded, lane_free[lane]])
                zeroed = E.done("dve", dve.memset(feats[lane][64:P, 0:1], 0.0))
                mark = yield from normalized(here, x, sm, added)
                for layer in range(2):
                    if layer not in tabled:
                        tabled[layer] = rope_table(layer)
                    needs(loaded[layer], tabled[layer])
                    mark = yield from local_attention(lane, layer, here, [mark, zeroed])
                    mark = yield from feed_forward(lane, layer, here, mark)
                    if b < LANES and layer == 0:
                        tabled["bias", lane] = bias_table(range(lane, HEADS_A, min(LANES, n_seq)))
                mark = yield from residual(x, here, sm, mark)
                mark = yield from normalized(here, x, sm, mark)
                needs(loaded_cd, [tabled["bias", n] for n in range(min(LANES, n_seq))])
                mark = yield from causal_attention(lane, here, mark)
                mark = yield from residual(x, here, sm, mark)
                mark = yield from normalized(here, x, sm, mark)
                mark = yield from experts(lane, here, mark)
                lane_free[lane] = yield from residual(x, here, sm, mark)
                E.after("sp", lane_free[lane])
                stored[lane] = E.dma(f"store_lane{lane}", out_dram[:, tiles, :], x)
            return steps

        E.in_lanes([sequence_task(b) for b in range(n_seq)])
        E.after("sp", [m for m in stored if m])


def layouts(inputs):
    a = {k: np.asarray(v) for k, v in inputs.items()}
    f = np.float32

    def rows(v):
        return np.ascontiguousarray(np.broadcast_to(v, (P, *v.shape)))

    t = {"x": a["L0_attn_x"], "ident": np.eye(P, dtype=f)}
    t["a_wq"], t["a_wk"], t["a_wv"] = a["L0_attn_Wq"].T, a["L0_attn_Wk"].T, a["L0_attn_Wv"].T
    t["a_bq"], t["a_bk"] = a["L0_attn_bq"][:, None], a["L0_attn_bk"][:, None]
    t["a_bv"] = rows(a["L0_attn_bv"])
    t["head_mask"] = np.repeat(np.eye(HEADS_A, dtype=f), HD_A, axis=0)
    t["b_wqkv"] = a["L0_ffn_wqkv"]
    t["b_wo"] = a["L0_ffn_wo"].reshape(2, INNER // P, P, P).transpose(0, 2, 1, 3)
    half = np.arange(0, HD_B, 2, dtype=f)
    inv_freq = (1.0 / f(10000.0) ** (half / f(HD_B))).astype(f)
    pos = np.arange(SEQ, dtype=f)
    freqs = pos[:, None] * inv_freq[None, :]
    freqs = np.concatenate([freqs, freqs], -1)
    base = (half + f(0.4 * HD_B)) / f(1.4 * HD_B)
    power = (pos - SEQ // 2) / f(WIN // 2)
    scale = base[None, :] ** power[:, None]
    scale = np.concatenate([scale, scale], -1).astype(f)
    sign = np.concatenate([-np.ones(HD_B // 2), np.ones(HD_B // 2)]).astype(f)
    cos, sin = np.cos(freqs), np.sin(freqs) * sign
    rope = np.stack([cos * scale, sin * scale, cos / scale, sin / scale])
    t["b_rope"] = rope.reshape(4, TPS, P, HD_B).transpose(2, 0, 1, 3).astype(f)

    def rotated(v):
        return np.concatenate([v[..., HD_B // 2:], v[..., :HD_B // 2]], -1)

    qs, ks = a["L0_ffn_q_scale"], a["L0_ffn_k_scale"]
    gain = np.stack([qs, rotated(qs), ks, rotated(ks)], 1)
    t["b_gain"] = np.broadcast_to(gain[:, None], (2, P, 4, HD_B))
    q = np.arange(P)[:, None]
    delta = np.concatenate([q - np.arange(P)[None], q + P - np.arange(SEQ)[None]], 1)
    t["b_band"] = np.where((delta < 0) | (delta > WIN), MASKED, 0.0).astype(f)
    t["f_w1"] = a["L0_ffn_w1"]
    w2 = np.zeros((2, 3 * P, P), f)
    w2[:, :HID] = a["L0_ffn_w2"]
    t["f_w2"] = w2.reshape(2, 3, P, P).transpose(0, 2, 1, 3)
    b1 = np.zeros((2, 2, 3 * P), f)
    b1[:, :, :HID] = a["L0_ffn_b1"].reshape(2, 2, HID)
    t["f_b1"] = b1.reshape(2, 2, 3, P).transpose(0, 3, 1, 2)
    t["f_b2"] = np.broadcast_to(a["L0_ffn_b2"][:, None], (2, P, P))
    t["f_g"], t["f_b"] = a["L0_ffn_ln_g"][:, :, None], a["L0_ffn_ln_b"][:, :, None]
    w = a["L1_attn_W_kqv"]
    t["c_wk"], t["c_wq"], t["c_wv"] = w[:, 0:P], w[:, P:2 * P], w[:, 2 * P:]
    t["c_slope"] = rows(a["L1_attn_m"].reshape(HEADS_A))
    t["c_rel"] = (-delta).astype(f)
    t["c_causal"] = np.where(delta < 0, MASKED, 0.0).astype(f)
    t["d_wg"], t["d_bg"] = a["L1_ffn_Wg"].T, rows(a["L1_ffn_bg"])
    t["d_w1"] = a["L1_ffn_W1"].reshape(EXPERTS * RANK, P).T
    t["d_w2"] = a["L1_ffn_W2"].transpose(0, 2, 1).reshape(4, P, P).transpose(1, 0, 2)
    t["d_order"] = rows(np.arange(EXPERTS, 0, -1).astype(f))
    return {k: np.ascontiguousarray(v) for k, v in t.items()}


def kernel(**inputs):
    import concourse.bacc as bacc
    from concourse.bass_utils import run_bass_kernel_spmd

    arrays = layouts(inputs)
    nc = bacc.Bacc("TRN2", target_bir_lowering=False, num_devices=1)
    io = {n: nc.dram_tensor(f"in_{n}", v.shape, mybir.dt.from_np(v.dtype), kind="ExternalInput").ap() for n, v in arrays.items()}
    io["out"] = nc.dram_tensor("out", arrays["x"].shape, F32, kind="ExternalOutput").ap()
    bass_four_blocks(nc, io)
    run = run_bass_kernel_spmd(nc, [{f"in_{n}": v for n, v in arrays.items()}], core_ids=[0])
    return run.results[0]["out"]
```
